# Optimizing a Trainium2 kernel written in Bass

```python
import numpy as np
import jax
import jax.numpy as jnp

def _softmax(x, axis=-1):
    return jax.nn.softmax(x, axis=axis)

def _gelu(x):
    return jax.nn.gelu(x, approximate=True)

def _silu(x):
    return jax.nn.silu(x)

def _sigmoid(x):
    return jax.nn.sigmoid(x)

def _layernorm(x, axis=-1, eps=1e-05):
    m = jnp.mean(x, axis=axis, keepdims=True)
    v = jnp.var(x, axis=axis, keepdims=True)
    return (x - m) / jnp.sqrt(v + eps)

def _scatter_add(tgt, idx, src, axis=0):
    return tgt.at[idx].add(src)

def _segment_sum(src, seg, n):
    return jax.ops.segment_sum(src, seg, n)
kernel_name = 'mk_seq_preln_d2_jaxref_r8_fea513'

def setup_inputs(seed: int=0):
    np.random.seed(seed)
    _w = jnp.asarray

    def _L0_attn_setup():
        import jax, jax.numpy as jnp
        import numpy as np
        from jax import lax
        B, T, C, H = (4, 256, 128, 16)
        K = C // H
        E_MIX, E_DEC = (32, 64)
        EPS = 1e-05 * 8 ** 2

        def _rwkv6_tmix(x, time_maa_x, time_maa_w, time_maa_k, time_maa_v, time_maa_r, time_maa_g, maa_w1, maa_w2, time_decay, td_w1, td_w2, u, Wr, Wk, Wv, Wg, Wo, ln_g, ln_b):
            b, t, c = x.shape
            x_prev = jnp.pad(x, ((0, 0), (1, 0), (0, 0)))[:, :t]
            xx = x_prev - x
            mix = jnp.tanh((x + xx * time_maa_x) @ maa_w1).reshape(b, t, 5, E_MIX)
            mix = jnp.einsum('btfe,fec->fbtc', mix, maa_w2)
            mw, mk, mv, mr, mg = mix
            xw = x + xx * (time_maa_w + mw)
            xk = x + xx * (time_maa_k + mk)
            xv = x + xx * (time_maa_v + mv)
            xr = x + xx * (time_maa_r + mr)
            xg = x + xx * (time_maa_g + mg)
            r = xr @ Wr.T
            k = xk @ Wk.T
            v = xv @ Wv.T
            g = jax.nn.silu(xg @ Wg.T)
            w = time_decay + jnp.tanh(xw @ td_w1) @ td_w2
            decay = jnp.exp(-jnp.exp(w))
            to_tbhk = lambda a: a.reshape(b, t, H, K).transpose(1, 0, 2, 3)
            rs, ks_, vs, ds = map(to_tbhk, (r, k, v, decay))

            def step(S, inp):
                r_t, k_t, v_t, d_t = inp
                kv = k_t[..., :, None] * v_t[..., None, :]
                y = jnp.einsum('bhk,bhkj->bhj', r_t, S + u[None, :, :, None] * kv)
                S = d_t[..., None] * S + kv
                return (S, y)
            S0 = jnp.zeros((b, H, K, K), x.dtype)
            _, y = lax.scan(step, S0, (rs, ks_, vs, ds))
            y = y.transpose(1, 0, 2, 3)
            mu = y.mean(-1, keepdims=True)
            var = y.var(-1, keepdims=True)
            y = ((y - mu) / jnp.sqrt(var + EPS)).reshape(b, t, c) * ln_g + ln_b
            return y * g @ Wo.T
        key = jax.random.key(seed)
        ks = jax.random.split(key, 24)
        u01 = lambda k, s: jax.random.uniform(k, s, jnp.float32, -0.01, 0.01)
        nrm = lambda k, s, sc: jax.random.normal(k, s, jnp.float32) * sc
        return {'x': jax.random.normal(ks[0], (B, T, C), jnp.float32), 'time_maa_x': jax.random.uniform(ks[1], (1, 1, C)), 'time_maa_w': jax.random.uniform(ks[2], (1, 1, C)), 'time_maa_k': jax.random.uniform(ks[3], (1, 1, C)), 'time_maa_v': jax.random.uniform(ks[4], (1, 1, C)), 'time_maa_r': jax.random.uniform(ks[5], (1, 1, C)), 'time_maa_g': jax.random.uniform(ks[6], (1, 1, C)), 'maa_w1': u01(ks[7], (C, 5 * E_MIX)), 'maa_w2': u01(ks[8], (5, E_MIX, C)), 'time_decay': jax.random.uniform(ks[9], (1, 1, C), jnp.float32, -6.0, -1.0), 'td_w1': u01(ks[10], (C, E_DEC)), 'td_w2': u01(ks[11], (E_DEC, C)), 'u': nrm(ks[12], (H, K), 0.1), 'Wr': nrm(ks[13], (C, C), 0.02), 'Wk': nrm(ks[14], (C, C), 0.02), 'Wv': nrm(ks[15], (C, C), 0.02), 'Wg': nrm(ks[16], (C, C), 0.02), 'Wo': nrm(ks[17], (C, C), 0.02), 'ln_g': jnp.ones((C,), jnp.float32), 'ln_b': jnp.zeros((C,), jnp.float32)}
    _L0_attn_in = _L0_attn_setup()

    def _L0_ffn_setup():
        import jax, jax.numpy as jnp
        import numpy as np
        D_MODEL, D_FF, N_EXP = (128, 512, 8)
        key = jax.random.key(seed)
        ks = jax.random.split(key, 8)
        s = lambda fan_in: 1.0 / np.sqrt(fan_in)
        x = jax.random.normal(ks[0], (4, 256, D_MODEL), dtype=jnp.float32)
        Wr = jax.random.uniform(ks[1], (N_EXP, D_MODEL), jnp.float32, -s(D_MODEL), s(D_MODEL))
        br = jax.random.uniform(ks[2], (N_EXP,), jnp.float32, -s(D_MODEL), s(D_MODEL))
        W1 = jax.random.uniform(ks[3], (N_EXP, D_FF, D_MODEL), jnp.float32, -s(D_MODEL), s(D_MODEL))
        b1 = jax.random.uniform(ks[4], (N_EXP, D_FF), jnp.float32, -s(D_MODEL), s(D_MODEL))
        W2 = jax.random.uniform(ks[5], (N_EXP, D_MODEL, D_FF), jnp.float32, -s(D_FF), s(D_FF))
        b2 = jax.random.uniform(ks[6], (N_EXP, D_MODEL), jnp.float32, -s(D_FF), s(D_FF))
        return {'x': x, 'Wr': Wr, 'br': br, 'W1': W1, 'b1': b1, 'W2': W2, 'b2': b2}
    _L0_ffn_in = _L0_ffn_setup()

    def _L1_attn_setup():
        import jax, jax.numpy as jnp
        import numpy as np
        DIM = 128
        N_QUAT = DIM // 4
        LN_EPS = 1e-05
        NORM_EPS = 1e-12

        def quat_mul(q1, q2):
            r1, i1, j1, k1 = (q1[..., 0], q1[..., 1], q1[..., 2], q1[..., 3])
            r2, i2, j2, k2 = (q2[..., 0], q2[..., 1], q2[..., 2], q2[..., 3])
            r = r1 * r2 - i1 * i2 - j1 * j2 - k1 * k2
            i = r1 * i2 + i1 * r2 + j1 * k2 - k1 * j2
            j = r1 * j2 - i1 * k2 + j1 * r2 + k1 * i2
            k = r1 * k2 + i1 * j2 - j1 * i2 + k1 * r2
            return jnp.stack([r, i, j, k], axis=-1)

        def quat_conj(q):
            return q * jnp.array([1.0, -1.0, -1.0, -1.0], dtype=q.dtype)
        key = jax.random.key(seed)
        ks = jax.random.split(key, 7)
        B, L, D = (4, 512, DIM)
        s = 1.0 / np.sqrt(D)
        return {'x': jax.random.normal(ks[0], (B, L, D), dtype=jnp.float32), 'Wk': jax.random.normal(ks[1], (D, D), dtype=jnp.float32) * s, 'bk': jnp.zeros((D,), dtype=jnp.float32), 'Wv': jax.random.normal(ks[2], (D, D), dtype=jnp.float32) * s, 'bv': jnp.zeros((D,), dtype=jnp.float32), 'ln_g': jnp.ones((D,), dtype=jnp.float32), 'ln_b': jnp.zeros((D,), dtype=jnp.float32), 'Wo': jax.random.normal(ks[3], (D, D), dtype=jnp.float32) * s, 'bo': jnp.zeros((D,), dtype=jnp.float32)}
    _L1_attn_in = _L1_attn_setup()

    def _L1_ffn_setup():
        import jax, jax.numpy as jnp
        import numpy as np
        TOP_K = 4
        CAP_FACTOR = 4

        def swiglu(x, w1, w2, w3):
            return jax.nn.silu(x @ w1) * (x @ w3) @ w2
        key = jax.random.key(seed)
        ks = jax.random.split(key, 8)
        B, S, D, H, E = (2, 256, 128, 64, 32)
        Hs = 2 * H
        sd = lambda *sh: 1.0 / np.sqrt(sh[-2])
        x = jax.random.normal(ks[0], (B, S, D), dtype=jnp.float32)
        Wg = jax.random.normal(ks[1], (D, E), dtype=jnp.float32) * (1.0 / np.sqrt(D))
        W1 = jax.random.normal(ks[2], (E, D, H), dtype=jnp.float32) * (1.0 / np.sqrt(D))
        W3 = jax.random.normal(ks[3], (E, D, H), dtype=jnp.float32) * (1.0 / np.sqrt(D))
        W2 = jax.random.normal(ks[4], (E, H, D), dtype=jnp.float32) * (1.0 / np.sqrt(H))
        Ws1 = jax.random.normal(ks[5], (D, Hs), dtype=jnp.float32) * (1.0 / np.sqrt(D))
        Ws3 = jax.random.normal(ks[6], (D, Hs), dtype=jnp.float32) * (1.0 / np.sqrt(D))
        Ws2 = jax.random.normal(ks[7], (Hs, D), dtype=jnp.float32) * (1.0 / np.sqrt(Hs))
        return {'x': x, 'Wg': Wg, 'W1': W1, 'W2': W2, 'W3': W3, 'Ws1': Ws1, 'Ws2': Ws2, 'Ws3': Ws3}
    _L1_ffn_in = _L1_ffn_setup()
    _d = {'L0_attn_x': _L0_attn_in['x'], 'L0_attn_time_maa_x': _L0_attn_in['time_maa_x'], 'L0_attn_time_maa_w': _L0_attn_in['time_maa_w'], 'L0_attn_time_maa_k': _L0_attn_in['time_maa_k'], 'L0_attn_time_maa_v': _L0_attn_in['time_maa_v'], 'L0_attn_time_maa_r': _L0_attn_in['time_maa_r'], 'L0_attn_time_maa_g': _L0_attn_in['time_maa_g'], 'L0_attn_maa_w1': _L0_attn_in['maa_w1'], 'L0_attn_maa_w2': _L0_attn_in['maa_w2'], 'L0_attn_time_decay': _L0_attn_in['time_decay'], 'L0_attn_td_w1': _L0_attn_in['td_w1'], 'L0_attn_td_w2': _L0_attn_in['td_w2'], 'L0_attn_u': _L0_attn_in['u'], 'L0_attn_Wr': _L0_attn_in['Wr'], 'L0_attn_Wk': _L0_attn_in['Wk'], 'L0_attn_Wv': _L0_attn_in['Wv'], 'L0_attn_Wg': _L0_attn_in['Wg'], 'L0_attn_Wo': _L0_attn_in['Wo'], 'L0_attn_ln_g': _L0_attn_in['ln_g'], 'L0_attn_ln_b': _L0_attn_in['ln_b'], 'L0_ffn_Wr': _L0_ffn_in['Wr'], 'L0_ffn_br': _L0_ffn_in['br'], 'L0_ffn_W1': _L0_ffn_in['W1'], 'L0_ffn_b1': _L0_ffn_in['b1'], 'L0_ffn_W2': _L0_ffn_in['W2'], 'L0_ffn_b2': _L0_ffn_in['b2'], 'L1_attn_Wk': _L1_attn_in['Wk'], 'L1_attn_bk': _L1_attn_in['bk'], 'L1_attn_Wv': _L1_attn_in['Wv'], 'L1_attn_bv': _L1_attn_in['bv'], 'L1_attn_ln_g': _L1_attn_in['ln_g'], 'L1_attn_ln_b': _L1_attn_in['ln_b'], 'L1_attn_Wo': _L1_attn_in['Wo'], 'L1_attn_bo': _L1_attn_in['bo'], 'L1_ffn_Wg': _L1_ffn_in['Wg'], 'L1_ffn_W1': _L1_ffn_in['W1'], 'L1_ffn_W2': _L1_ffn_in['W2'], 'L1_ffn_W3': _L1_ffn_in['W3'], 'L1_ffn_Ws1': _L1_ffn_in['Ws1'], 'L1_ffn_Ws2': _L1_ffn_in['Ws2'], 'L1_ffn_Ws3': _L1_ffn_in['Ws3']}
    _x0 = _d['L0_attn_x']
    _d['L0_attn_x'] = jax.random.normal(jax.random.fold_in(jax.random.key(seed), 1), (4, 1024, 128), dtype=_x0.dtype)
    del _x0
    return _d

def reference(L0_attn_x, L0_attn_time_maa_x, L0_attn_time_maa_w, L0_attn_time_maa_k, L0_attn_time_maa_v, L0_attn_time_maa_r, L0_attn_time_maa_g, L0_attn_maa_w1, L0_attn_maa_w2, L0_attn_time_decay, L0_attn_td_w1, L0_attn_td_w2, L0_attn_u, L0_attn_Wr, L0_attn_Wk, L0_attn_Wv, L0_attn_Wg, L0_attn_Wo, L0_attn_ln_g, L0_attn_ln_b, L0_ffn_Wr, L0_ffn_br, L0_ffn_W1, L0_ffn_b1, L0_ffn_W2, L0_ffn_b2, L1_attn_Wk, L1_attn_bk, L1_attn_Wv, L1_attn_bv, L1_attn_ln_g, L1_attn_ln_b, L1_attn_Wo, L1_attn_bo, L1_ffn_Wg, L1_ffn_W1, L1_ffn_W2, L1_ffn_W3, L1_ffn_Ws1, L1_ffn_Ws2, L1_ffn_Ws3):

    def _L0_attn_ref(x, time_maa_x, time_maa_w, time_maa_k, time_maa_v, time_maa_r, time_maa_g, maa_w1, maa_w2, time_decay, td_w1, td_w2, u, Wr, Wk, Wv, Wg, Wo, ln_g, ln_b):
        import jax, jax.numpy as jnp
        import numpy as np
        from jax import lax
        B, T, C, H = (4, 256, 128, 16)
        K = C // H
        E_MIX, E_DEC = (32, 64)
        EPS = 1e-05 * 8 ** 2

        def _rwkv6_tmix(x, time_maa_x, time_maa_w, time_maa_k, time_maa_v, time_maa_r, time_maa_g, maa_w1, maa_w2, time_decay, td_w1, td_w2, u, Wr, Wk, Wv, Wg, Wo, ln_g, ln_b):
            b, t, c = x.shape
            x_prev = jnp.pad(x, ((0, 0), (1, 0), (0, 0)))[:, :t]
            xx = x_prev - x
            mix = jnp.tanh((x + xx * time_maa_x) @ maa_w1).reshape(b, t, 5, E_MIX)
            mix = jnp.einsum('btfe,fec->fbtc', mix, maa_w2)
            mw, mk, mv, mr, mg = mix
            xw = x + xx * (time_maa_w + mw)
            xk = x + xx * (time_maa_k + mk)
            xv = x + xx * (time_maa_v + mv)
            xr = x + xx * (time_maa_r + mr)
            xg = x + xx * (time_maa_g + mg)
            r = xr @ Wr.T
            k = xk @ Wk.T
            v = xv @ Wv.T
            g = jax.nn.silu(xg @ Wg.T)
            w = time_decay + jnp.tanh(xw @ td_w1) @ td_w2
            decay = jnp.exp(-jnp.exp(w))
            to_tbhk = lambda a: a.reshape(b, t, H, K).transpose(1, 0, 2, 3)
            rs, ks_, vs, ds = map(to_tbhk, (r, k, v, decay))

            def step(S, inp):
                r_t, k_t, v_t, d_t = inp
                kv = k_t[..., :, None] * v_t[..., None, :]
                y = jnp.einsum('bhk,bhkj->bhj', r_t, S + u[None, :, :, None] * kv)
                S = d_t[..., None] * S + kv
                return (S, y)
            S0 = jnp.zeros((b, H, K, K), x.dtype)
            _, y = lax.scan(step, S0, (rs, ks_, vs, ds))
            y = y.transpose(1, 0, 2, 3)
            mu = y.mean(-1, keepdims=True)
            var = y.var(-1, keepdims=True)
            y = ((y - mu) / jnp.sqrt(var + EPS)).reshape(b, t, c) * ln_g + ln_b
            return y * g @ Wo.T
        return _rwkv6_tmix(x, time_maa_x, time_maa_w, time_maa_k, time_maa_v, time_maa_r, time_maa_g, maa_w1, maa_w2, time_decay, td_w1, td_w2, u, Wr, Wk, Wv, Wg, Wo, ln_g, ln_b)

    def _L0_ffn_ref(x, Wr, br, W1, b1, W2, b2):
        import jax, jax.numpy as jnp
        import numpy as np
        D_MODEL, D_FF, N_EXP = (128, 512, 8)
        B, S, D = x.shape
        xf = x.reshape(-1, D)
        logits = xf @ Wr.T + br
        expert_idx = jnp.argmax(logits, axis=-1)
        h = jax.nn.relu(jnp.einsum('td,efd->etf', xf, W1) + b1[:, None, :])
        y = jnp.einsum('etf,edf->etd', h, W2) + b2[:, None, :]
        out = y[expert_idx, jnp.arange(xf.shape[0])]
        return out.reshape(B, S, D)

    def _L1_attn_ref(x, Wk, bk, Wv, bv, ln_g, ln_b, Wo, bo):
        import jax, jax.numpy as jnp
        import numpy as np
        DIM = 128
        N_QUAT = DIM // 4
        LN_EPS = 1e-05
        NORM_EPS = 1e-12

        def quat_mul(q1, q2):
            r1, i1, j1, k1 = (q1[..., 0], q1[..., 1], q1[..., 2], q1[..., 3])
            r2, i2, j2, k2 = (q2[..., 0], q2[..., 1], q2[..., 2], q2[..., 3])
            r = r1 * r2 - i1 * i2 - j1 * j2 - k1 * k2
            i = r1 * i2 + i1 * r2 + j1 * k2 - k1 * j2
            j = r1 * j2 - i1 * k2 + j1 * r2 + k1 * i2
            k = r1 * k2 + i1 * j2 - j1 * i2 + k1 * r2
            return jnp.stack([r, i, j, k], axis=-1)

        def quat_conj(q):
            return q * jnp.array([1.0, -1.0, -1.0, -1.0], dtype=q.dtype)
        B, L, D = x.shape
        keys = (x @ Wk.T + bk).reshape(B, L, N_QUAT, 4)
        knorm = jnp.linalg.norm(keys, axis=-1, keepdims=True)
        keys = keys / jnp.maximum(knorm, NORM_EPS)
        values = (x @ Wv.T + bv).reshape(B, L, N_QUAT, 4)
        bound = quat_mul(values, keys)
        memory = jnp.cumsum(bound, axis=1)
        retrieved = quat_mul(memory, quat_conj(keys)).reshape(B, L, D)
        positions = jnp.arange(1, L + 1, dtype=x.dtype)
        retrieved = retrieved / jnp.sqrt(positions)[None, :, None]
        mu = jnp.mean(retrieved, axis=-1, keepdims=True)
        var = jnp.var(retrieved, axis=-1, keepdims=True)
        normed = (retrieved - mu) / jnp.sqrt(var + LN_EPS) * ln_g + ln_b
        return x + (normed @ Wo.T + bo)

    def _L1_ffn_ref(x, Wg, W1, W2, W3, Ws1, Ws2, Ws3):
        import jax, jax.numpy as jnp
        import numpy as np
        TOP_K = 4
        CAP_FACTOR = 4

        def swiglu(x, w1, w2, w3):
            return jax.nn.silu(x @ w1) * (x @ w3) @ w2
        B, S, D = x.shape
        E = Wg.shape[1]
        T = B * S
        xf = x.reshape(T, D)
        scores = jax.nn.softmax(xf @ Wg, axis=-1)
        weights, indices = jax.lax.top_k(scores, TOP_K)
        P = T * TOP_K
        pair_expert = indices.reshape(-1)
        pair_token = jnp.repeat(jnp.arange(T), TOP_K)
        pair_weight = weights.reshape(-1).astype(xf.dtype)
        C = CAP_FACTOR * P // E
        y = jnp.zeros_like(xf)
        for e in range(E):
            pos = jnp.nonzero(pair_expert == e, size=C, fill_value=P)[0]
            valid = pos < P
            safe = jnp.minimum(pos, P - 1)
            tok = jnp.where(valid, pair_token[safe], 0)
            w = jnp.where(valid, pair_weight[safe], 0.0)
            xg = xf[tok]
            out = swiglu(xg, W1[e], W2[e], W3[e]) * w[:, None]
            y = y.at[tok].add(out)
        z = swiglu(xf, Ws1, Ws2, Ws3)
        return (y + z).reshape(B, S, D)
    x = L0_attn_x
    x = x + _L0_attn_ref(_layernorm(x, axis=-1), L0_attn_time_maa_x, L0_attn_time_maa_w, L0_attn_time_maa_k, L0_attn_time_maa_v, L0_attn_time_maa_r, L0_attn_time_maa_g, L0_attn_maa_w1, L0_attn_maa_w2, L0_attn_time_decay, L0_attn_td_w1, L0_attn_td_w2, L0_attn_u, L0_attn_Wr, L0_attn_Wk, L0_attn_Wv, L0_attn_Wg, L0_attn_Wo, L0_attn_ln_g, L0_attn_ln_b)
    x = x + _L0_ffn_ref(_layernorm(x, axis=-1), L0_ffn_Wr, L0_ffn_br, L0_ffn_W1, L0_ffn_b1, L0_ffn_W2, L0_ffn_b2)
    x = x + _L1_attn_ref(_layernorm(x, axis=-1), L1_attn_Wk, L1_attn_bk, L1_attn_Wv, L1_attn_bv, L1_attn_ln_g, L1_attn_ln_b, L1_attn_Wo, L1_attn_bo)
    x = x + _L1_ffn_ref(_layernorm(x, axis=-1), L1_ffn_Wg, L1_ffn_W1, L1_ffn_W2, L1_ffn_W3, L1_ffn_Ws1, L1_ffn_Ws2, L1_ffn_Ws3)
    return x

_drawn_inputs = setup_inputs


def setup_inputs(seed=0):
    import zlib

    import numpy as np

    out = dict(_drawn_inputs(seed))
    spreads = {'L0_attn_ln_g': (1.0, 0.6),
     'L0_attn_ln_b': (0.0, 0.361),
     'L1_attn_bk': (0.0, 0.1),
     'L1_attn_bv': (0.0, 0.1),
     'L1_attn_ln_g': (1.0, 0.2),
     'L1_attn_ln_b': (0.0, 0.1),
     'L1_attn_bo': (0.0, 0.1)}
    factors = {'L0_attn_time_maa_x': 8.0,
     'L0_attn_time_maa_w': 64.0,
     'L0_attn_maa_w1': 8.0,
     'L0_attn_maa_w2': 8.0,
     'L0_attn_td_w1': 64.0,
     'L0_attn_td_w2': 64.0,
     'L0_attn_u': 25.047}
    for name, (base, spread) in spreads.items():
        noise = np.random.default_rng([zlib.crc32(name.encode()), seed]).standard_normal(out[name].shape)
        drawn = base * np.exp(spread * noise) if base else spread * noise
        out[name] = jnp.asarray(drawn.astype(out[name].dtype))
    for name, factor in factors.items():
        out[name] = (out[name] * factor).astype(out[name].dtype)
    return out
```

```python
from contextlib import ExitStack

import numpy as np

import concourse.bass as bass
from concourse import mybir

ALU = mybir.AluOpType
ACT = mybir.ActivationFunctionType
AXIS = mybir.AxisListType
F32 = mybir.dt.float32
F32R = mybir.dt.float32r
BF16 = mybir.dt.bfloat16
I32 = mybir.dt.int32
U32 = mybir.dt.uint32

P = 128
BATCH, SEQ = 4, 1024
TOKENS = BATCH * SEQ
SUB = 4
TILE = SUB * P
TILES = TOKENS // TILE
GROUPS = TOKENS // P
PER_SEQ = SEQ // TILE
LN_EPS = 1e-5

HEADS, HK = 16, 8
MIXES, E_MIX = 5, 32
GN_EPS = 1e-5 * 8 ** 2

A_PARTS = [("mix1", 2 * P), ("mix2", MIXES * P), ("td1", P), ("td2", P), ("wr", P), ("wk", P),
           ("wv", P), ("wg", P), ("wo", P), ("maa", 6), ("decay", 1), ("u", 1), ("gain", 1), ("shift", 1)]
C_PARTS = [("ident", P), ("spread", HK * P), ("gather", 2 * 32), ("heads", P), ("centre", P), ("mean", HEADS)]


def offsets(parts):
    at, n = {}, 0
    for name, width in parts:
        at[name] = (n, n + width)
        n += width
    return at, n


A_AT, A_WIDTH = offsets(A_PARTS)
C_AT, C_WIDTH = offsets(C_PARTS)

Y_ORDER = [HK * (p % HEADS) + 4 * (p // HEADS % 2) + p // 32 for p in range(P)]


def shape_constants():
    c = np.zeros((P, C_WIDTH), np.float32)
    part = {name: c[:, a:b] for name, (a, b) in C_AT.items()}
    part["ident"][:] = np.eye(P)
    for p, channel in enumerate(Y_ORDER):
        head, j = divmod(channel, HK)
        part["spread"][p, j * P + head * HK:j * P + (head + 1) * HK] = 1
    for k in range(P):
        for a in range(2):
            part["gather"][k, a * 32 + a * HEADS + k // HK] = 1
        part["heads"][k, k // HK::HEADS] = 1
    same = np.equal.outer(np.arange(P) % HEADS, np.arange(P) % HEADS)
    part["centre"][:] = np.eye(P) - same / HK
    part["mean"][:] = np.equal.outer(np.arange(P) % HEADS, np.arange(HEADS)) / HK
    return c


def need(engine, semaphore, value):
    if not isinstance(value, int) or value > 0:
        engine.wait_ge(semaphore, value)


def time_mixing(nc, x_tok, consts, x_in, w_in, c_in):
    with ExitStack() as ctx:
        def sb(name, shape, dt=F32):
            return ctx.enter_context(nc.sbuf_tensor("a_" + name, shape, dt))

        def bank(name):
            return ctx.enter_context(nc.psum_tensor("a_" + name, [P, TILE], F32))

        def sem(name):
            return nc.alloc_semaphore("a_" + name)

        weights = sb("weights", [P, A_WIDTH])
        spread = sb("spread", [P, HK * P], F32R)
        half = sb("minus_half", [P, SUB])
        eps = sb("eps", [P, SUB])
        eps_gn = sb("eps_gn", [P, 1])

        def w(name):
            return weights[:, A_AT[name][0]:A_AT[name][1]]

        def const(name):
            return consts[:, C_AT[name][0]:C_AT[name][1]]

        ident = const("ident")
        maa = w("maa")
        mean = const("mean")

        stats = sb("stats", [P, SUB, 6])
        moments = sb("moments", [P, SUB, 2])
        var_eps = sb("var_eps", [P, SUB])
        rstd = sb("rstd", [P, SUB])
        shift = sb("shift", [P, SUB])
        xn = sb("xn", [P, SUB, P])
        xt = [sb(f"xt{h}", [P, TILE + 1]) for h in range(2)]
        dx = sb("dx", [P, TILE])
        xa = sb("xa", [P, TILE])
        m1 = sb("m1", [P, 2, TILE])
        lerp = sb("lerp", [P, 2, TILE])
        xf = sb("xf", [P, MIXES, TILE])
        td_hidden = sb("td_hidden", [P, TILE])
        rate = sb("rate", [P, TILE])
        decay = sb("decay", [P, 2, TILE])
        kk = sb("k", [P, 2, TILE])
        rr = sb("r", [P, 2, TILE])
        vv = sb("v", [P, TILE])
        v_hi = sb("v_hi", [P, 2, TILE], F32R)
        v_lo = sb("v_lo", [P, 2, TILE], F32R)
        g_tanh = sb("g_tanh", [P, TILE])
        gate = sb("gate", [P, 2, TILE])
        rku = sb("rku", [P, TILE])
        bonus_v = sb("bonus_v", [P, 2, TILE])
        kv = sb("kv", [P, 2, TILE])
        state = sb("state", [P, HK, SEQ + 1])
        rs = sb("rs", [P, HK, TILE])
        y_sum = sb("y_sum", [P, TILE])
        yc = sb("yc", [P, TILE])
        yc2 = sb("yc2", [P, TILE])
        spread_y = sb("std_y", [P, SUB, HEADS])
        rstd_y = sb("rstd_y", [P, SUB, HEADS])
        rstd_wide = sb("rstd_wide", [P, TILE])
        yn = sb("yn", [P, TILE])
        yl = sb("yl", [P, TILE])
        z = sb("z", [P, TILE])

        front = [bank(f"front{n}") for n in range(3)]
        vb = [bank(f"vb{n}") for n in range(2)]
        y_bank = bank("y")
        tail0, tail1 = bank("tail0"), bank("tail1")

        XT, M1A, M1B, MIX, TD1, K, TD2, V, R, G, BONUS = 0, 1, 2, 3, 8, 9, 10, 11, 12, 13, 14
        USES = 15

        x_first, x_rest, w_loaded = sem("x_first"), sem("x_rest"), sem("w_loaded")
        zeroed, eps_set = sem("zeroed"), sem("eps_set")
        spread_ready = sem("spread_ready")
        go = sem("go")
        stats_ready, moments_ready, var_ready = sem("stats_ready"), sem("moments_ready"), sem("var_ready")
        rstd_ready, shift_ready, xn_ready = sem("rstd_ready"), sem("shift_ready"), sem("xn_ready")
        front_out = sem("front_out")
        xt_ready, dx_ready, xa_ready = sem("xt_ready"), sem("dx_ready"), sem("xa_ready")
        m1_ready = sem("m1_ready")
        lerp_ready, xf_ready = sem("lerp_ready"), sem("xf_ready")
        td_ready, k_ready, rate_ready, decay_ready = sem("td_ready"), sem("k_ready"), sem("rate_ready"), sem("decay_ready")
        v_ready, vhi_ready, vlo_ready, r_ready = sem("v_ready"), sem("vhi_ready"), sem("vlo_ready"), sem("r_ready")
        gtanh_ready, gate_ready, rku_ready, bonus_ready = sem("gtanh_ready"), sem("gate_ready"), sem("rku_ready"), sem("bonus_ready")
        vb_out, kv_ready, scan_ready, rs_ready = sem("vb_out"), sem("kv_ready"), sem("scan_ready"), sem("rs_ready")
        y_out = sem("y_out")
        ysum_ready, centred, yc_ready, yc2_ready = sem("ysum_ready"), sem("centred"), sem("yc_ready"), sem("yc2_ready")
        wide_ready = sem("wide_ready")
        var_out, std_ready, rstdy_ready, rstdy_out = sem("var_out"), sem("std_ready"), sem("rstdy_ready"), sem("rstdy_out")
        yn_ready, yl_ready, z_ready, wo_out, x_ready = sem("yn_ready"), sem("yl_ready"), sem("z_ready"), sem("wo_out"), sem("x_ready")

        def groups(i):
            return slice(SUB * i, SUB * i + SUB) if isinstance(i, int) else bass.ds(SUB * i, SUB)

        def seq_cols(h, first):
            return slice(TILE * h + first, TILE * h + first + TILE)

        def pipeline(engine, scan, ahead, tail):
            for step in range(8):
                ahead(0, 0, step)
            for i in range(3):
                for step in range(8):
                    scan(i, i % 2, step)
                    if i:
                        tail(i - 1, 1 - i % 2, step)
                    ahead(i + 1, 1 - i % 2, step)
            with engine.Fori(1, TILES // 2 - 1) as b:
                for h in (1, 0):
                    i = 2 * b + (1 if h else 2)
                    for step in range(8):
                        scan(i, h, step)
                        tail(i - 1, 1 - h, step)
                        ahead(i + 1, 1 - h, step)
            for step in range(8):
                scan(TILES - 1, 1, step)
                tail(TILES - 2, 0, step)
            for step in range(8):
                tail(TILES - 1, 1, step)

        with nc.Block() as block:
            @block.sync
            def _(sp):
                sp.dma_start(x_tok[:, 0:SUB, :], x_in[:, 0:SUB, :]).then_inc(x_first, 16)
                sp.dma_start(weights[:, :], w_in).then_inc(w_loaded, 16)
                sp.dma_start(consts[:, :], c_in).then_inc(w_loaded, 16)
                sp.dma_start(x_tok[:, SUB:, :], x_in[:, SUB:, :]).then_inc(x_rest, 16)

            @block.tensor
            def _(pe):
                def use(i, n):
                    return i * USES + n + 1

                def project(i, n, name, operand):
                    pe.matmul(front[n % 3][:, :], w(name), operand, start=True, stop=True).then_inc(front_out, 1)

                def ahead(i, h, step):
                    if step == 1:
                        pe.wait_ge(xn_ready, i + 1)
                        need(pe, r_ready, i)
                        for s in range(SUB):
                            mm = pe.transpose(front[0][:, s * P:(s + 1) * P], xn[:, s, :], ident)
                        mm.then_inc(front_out, 1)
                    if step == 2:
                        pe.wait_ge(xa_ready, i + 1)
                        need(pe, gate_ready, i)
                        pe.matmul(front[1][:, :], w("mix1")[:, 0:P], xa[:, :], start=True, stop=True).then_inc(front_out, 1)
                        need(pe, bonus_ready, i)
                        pe.matmul(front[2][:, :], w("mix1")[:, P:2 * P], xa[:, :], start=True, stop=True).then_inc(front_out, 1)
                    if step in (3, 4, 5):
                        for f in range(2 * (step - 3), min(2 * (step - 3) + 2, MIXES)):
                            n = MIX + f
                            if f == 0:
                                pe.wait_ge(m1_ready, 2 * i + 1)
                            elif f < 3:
                                pe.wait_ge(m1_ready, 2 * i + f)
                            else:
                                pe.wait_ge(lerp_ready, MIXES * i + f - 2)
                            if f == 4:
                                pe.wait_ge(m1_ready, 2 * i + 2)
                            operand = m1[:, 0, :] if f < 4 else m1[:, 1, :]
                            pe.matmul(front[n % 3][:, :], w("mix2")[:, f * P:(f + 1) * P], operand,
                                      start=True, stop=True).then_inc(front_out, 1)
                    if step == 5:
                        pe.wait_ge(xf_ready, MIXES * i + 1)
                        pe.wait_ge(lerp_ready, MIXES * i + 3)
                        project(i, TD1, "td1", xf[:, 0, :])
                        pe.wait_ge(xf_ready, MIXES * i + 2)
                        pe.wait_ge(lerp_ready, MIXES * i + 4)
                        project(i, K, "wk", xf[:, 1, :])
                    if step == 6:
                        pe.wait_ge(td_ready, i + 1)
                        pe.wait_ge(lerp_ready, MIXES * i + 5)
                        project(i, TD2, "td2", td_hidden[:, :])
                        pe.wait_ge(xf_ready, MIXES * i + 3)
                        project(i, V, "wv", xf[:, 2, :])
                    if step == 7:
                        pe.wait_ge(xf_ready, MIXES * i + 4)
                        pe.wait_ge(k_ready, i + 1)
                        project(i, R, "wr", xf[:, 3, :])
                        pe.wait_ge(xf_ready, MIXES * i + 5)
                        pe.wait_ge(rate_ready, i + 1)
                        project(i, G, "wg", xf[:, 4, :])
                        pe.wait_ge(rku_ready, i + 1)
                        pe.wait_ge(vhi_ready, i + 1)
                        pe.matmul(front[2][:, :], const("heads"), rku[:, :], start=True, stop=True).then_inc(front_out, 1)

                def spread_v(i, h, j):
                    if j == 0:
                        pe.wait_ge(vhi_ready, i + 1)
                        pe.wait_ge(vlo_ready, i + 1)
                    need(pe, kv_ready, HK * i + j - 1)
                    row = spread[:, j * P:(j + 1) * P]
                    pe.matmul(vb[j % 2][:, :], row, v_hi[:, h, :], start=True, stop=False)
                    pe.matmul(vb[j % 2][:, :], row, v_lo[:, h, :], start=False, stop=True).then_inc(vb_out, 1)

                def sum_k(i, a):
                    pe.wait_ge(rs_ready, HK * i + 4 * a + 4)
                    if a == 0:
                        need(pe, ysum_ready, i)
                    for g in range(4):
                        mm = pe.matmul(y_bank[32 * g:32 * g + 32, :], const("gather")[:, 32 * a:32 * a + 32],
                                       rs[:, 4 * a + g, :], start=(a == 0), stop=(a == 1), tile_position=(0, 32 * g))
                    mm.then_inc(y_out, 1)

                def scan(i, h, step):
                    if step == 0:
                        spread_v(i, h, 0)
                    if step < 7:
                        spread_v(i, h, step + 1)
                    if step == 6:
                        sum_k(i, 0)

                def tail(i, h, step):
                    if step == 1:
                        sum_k(i, 1)
                    if step == 2:
                        pe.wait_ge(ysum_ready, i + 1)
                        pe.matmul(tail0[:, :], const("centre"), y_sum[:, :], start=True, stop=True).then_inc(centred, 1)
                    if step == 3:
                        pe.wait_ge(yc2_ready, i + 1)
                        need(pe, x_ready, i)
                        for s in range(SUB):
                            mm = pe.matmul(tail1[:, s * HEADS:(s + 1) * HEADS], yc2[:, s * P:(s + 1) * P], mean,
                                           start=True, stop=True)
                        mm.then_inc(var_out, 1)
                    if step == 4:
                        pe.wait_ge(wide_ready, i + 1)
                        for s in range(SUB):
                            mm = pe.transpose(tail0[:, s * P:(s + 1) * P], rstd_wide[:, s * P:(s + 1) * P], ident)
                        mm.then_inc(rstdy_out, 1)
                    if step == 6:
                        pe.wait_ge(z_ready, i + 1)
                        for s in range(SUB):
                            mm = pe.matmul(tail1[:, s * P:(s + 1) * P], z[:, s * P:(s + 1) * P], w("wo"),
                                           start=True, stop=True)
                        mm.then_inc(wo_out, 1)

                pe.wait_ge(w_loaded, 32)
                pe.wait_ge(spread_ready, 1)
                pipeline(pe, scan, ahead, tail)

            @block.vector
            def _(dve):
                def ahead(i, h, step):
                    here = xt[h]
                    if step == 0:
                        need(dve, rstd_ready, i)
                        for s in range(SUB):
                            group = x_tok[:, SUB * i + s, :]
                            st = dve.bn_stats(stats[:, s, :], group)
                        st.then_inc(stats_ready, 1)
                        dve.wait_ge(stats_ready, i + 1)
                        need(dve, shift_ready, i)
                        dve.sem_inc(go, 1)
                        for s in range(SUB):
                            ag = dve.bn_aggr(moments[:, s, :], stats[:, s, :])
                        ag.then_inc(moments_ready, 1)
                    if step == 1:
                        dve.wait_ge(rstd_ready, i + 1)
                        need(dve, xn_ready, i)
                        dve.scalar_tensor_tensor(shift[:, :], moments[:, :, 0], -1.0, rstd[:, :],
                                                 ALU.mult, ALU.mult).then_inc(shift_ready, 1)
                    if step == 2:
                        dve.wait_ge(xt_ready, i + 1)
                        need(dve, lerp_ready, MIXES * i)
                        dve.tensor_tensor(dx[:, :], here[:, 0:TILE], here[:, 1:TILE + 1], ALU.subtract).then_inc(dx_ready, 1)
                        dve.wait_ge(dx_ready, i + 1)
                        need(dve, m1_ready, 2 * i)
                        dve.scalar_tensor_tensor(xa[:, :], dx[:, :], maa[:, 0:1], here[:, 1:TILE + 1],
                                                 ALU.mult, ALU.add).then_inc(xa_ready, 1)
                    if step in (3, 4, 5):
                        for f in range(2 * (step - 3), min(2 * (step - 3) + 2, MIXES)):
                            dve.wait_ge(front_out, USES * i + MIX + f + 1)
                            need(dve, xf_ready, MIXES * i + f - 1)
                            dve.scalar_tensor_tensor(lerp[:, (f + h) % 2, :], front[(MIX + f) % 3][:, :], maa[:, f + 1:f + 2],
                                                     dx[:, :], ALU.add, ALU.mult).then_inc(lerp_ready, 1)
                    if step == 7:
                        dve.wait_ge(vhi_ready, i + 1)
                        if h == 0:
                            need(dve, vb_out, HK * (i - 1))
                        else:
                            need(dve, vb_out, HK * (i - 1))
                        dve.tensor_tensor(v_lo[:, h, :], vv[:, :], v_hi[:, h, :].bitcast(F32), ALU.subtract).then_inc(vlo_ready, 1)
                        dve.wait_ge(r_ready, i + 1)
                        need(dve, front_out, USES * i)
                        dve.scalar_tensor_tensor(rku[:, :], rr[:, h, :], w("u"), kk[:, h, :],
                                                 ALU.mult, ALU.mult).then_inc(rku_ready, 1)
                        dve.wait_ge(gtanh_ready, i + 1)
                        need(dve, z_ready, i - 1)
                        dve.scalar_tensor_tensor(gate[:, h, :], g_tanh[:, :], 1.0, front[G % 3][:, :],
                                                 ALU.add, ALU.mult).then_inc(gate_ready, 1)
                        dve.wait_ge(front_out, USES * i + BONUS + 1)
                        dve.tensor_tensor(bonus_v[:, h, :], vv[:, :], front[BONUS % 3][:, :], ALU.mult).then_inc(bonus_ready, 1)

                def outer(i, h, j):
                    if j == 0:
                        dve.wait_ge(k_ready, i + 1)
                    dve.wait_ge(vb_out, HK * i + j + 1)
                    need(dve, scan_ready, HK * i + j - 1)
                    dve.tensor_tensor(kv[:, j % 2, :], kk[:, h, :], vb[j % 2][:, :], ALU.mult).then_inc(kv_ready, 1)

                def scan(i, h, step):
                    if step == 0:
                        dve.wait_ge(decay_ready, i + 1)
                        outer(i, h, 0)
                    if step < 7:
                        outer(i, h, step + 1)
                    j = step
                    dve.wait_ge(kv_ready, HK * i + j + 1)
                    need(dve, rs_ready, HK * (i - 1) + j)
                    first = state[:, j, TILE * h:TILE * h + 1]
                    if h:
                        dve.wait_ge(scan_ready, HK * (i - 1) + j + 1)
                    dve.tensor_tensor_scan(state[:, j, seq_cols(h, 1)], decay[:, h, :], kv[:, j % 2, :], first,
                                           ALU.mult, ALU.add).then_inc(scan_ready, 1)

                def tail(i, h, step):
                    if step == 2:
                        dve.wait_ge(y_out, 2 * i + 2)
                        dve.wait_ge(bonus_ready, i + 1)
                        need(dve, centred, i)
                        dve.tensor_tensor(y_sum[:, :], bonus_v[:, h, :], y_bank[:, :], ALU.add).then_inc(ysum_ready, 1)
                    if step == 3:
                        dve.wait_ge(std_ready, i + 1)
                        need(dve, wide_ready, i)
                        dve.reciprocal(rstd_y[:, :, :], spread_y[:, :, :]).then_inc(rstdy_ready, 1)
                    if step == 4:
                        dve.wait_ge(rstdy_out, i + 1)
                        dve.wait_ge(yc_ready, i + 1)
                        need(dve, yl_ready, i)
                        dve.tensor_tensor(yn[:, :], yc[:, :], tail0[:, :], ALU.mult).then_inc(yn_ready, 1)
                    if step == 5:
                        dve.wait_ge(yl_ready, i + 1)
                        dve.wait_ge(gate_ready, i + 1)
                        need(dve, wo_out, i)
                        dve.scalar_tensor_tensor(z[:, :], yl[:, :], 0.5, gate[:, h, :], ALU.mult, ALU.mult).then_inc(z_ready, 1)
                    if step == 6:
                        dve.wait_ge(wo_out, i + 1)
                        x = x_tok[:, groups(i), :]
                        dve.tensor_tensor(x, x, tail1[:, :].rearrange("p (s c) -> p s c", s=SUB), ALU.add).then_inc(x_ready, 1)

                dve.memset(xt[0][:, 0:1], 0.0)
                dve.memset(state[:, :, 0:1], 0.0)
                dve.memset(eps[:, :], LN_EPS)
                dve.memset(half[:, :], -0.5).then_inc(zeroed, 1)
                dve.wait_ge(zeroed, 1)
                dve.wait_ge(w_loaded, 32)
                dve.tensor_copy(spread[:, :], const("spread")).then_inc(spread_ready, 1)
                dve.wait_ge(x_first, 16)
                dve.wait_ge(x_rest, 16)
                pipeline(dve, scan, ahead, tail)

            @block.scalar
            def _(act):
                def ahead(i, h, step):
                    if step == 1:
                        act.wait_ge(shift_ready, i + 1)
                        need(act, xt_ready, i)
                        for s in range(SUB):
                            a = act.activation(xn[:, s, :], x_tok[:, SUB * i + s, :], ACT.Identity,
                                               bias=shift[:, s:s + 1], scale=rstd[:, s:s + 1])
                        a.then_inc(xn_ready, 1)
                        act.wait_ge(front_out, USES * i + XT + 1)
                        need(act, xf_ready, MIXES * (i - 1))
                        if h:
                            act.activation(xt[1][:, 0:1], xt[0][:, TILE:TILE + 1], ACT.Copy)
                        act.activation(xt[h][:, 1:TILE + 1], front[0][:, :], ACT.Copy).then_inc(xt_ready, 1)
                    if step == 2:
                        act.wait_ge(front_out, USES * i + M1A + 1)
                        need(act, lerp_ready, MIXES * i)
                        act.activation(m1[:, 0, :], front[M1A][:, :], ACT.Tanh).then_inc(m1_ready, 1)
                        act.wait_ge(front_out, USES * i + M1B + 1)
                        act.activation(m1[:, 1, :], front[M1B][:, :], ACT.Tanh).then_inc(m1_ready, 1)
                    if step == 5:
                        act.wait_ge(front_out, USES * i + TD1 + 1)
                        act.activation(td_hidden[:, :], front[TD1 % 3][:, :], ACT.Tanh).then_inc(td_ready, 1)
                        act.wait_ge(front_out, USES * i + K + 1)
                        need(act, kv_ready, HK * (i - 1))
                        need(act, rku_ready, i - 1)
                        act.activation(kk[:, h, :], front[K % 3][:, :], ACT.Copy).then_inc(k_ready, 1)
                    if step == 6:
                        act.wait_ge(front_out, USES * i + TD2 + 1)
                        act.activation(rate[:, :], front[TD2 % 3][:, :], ACT.Exp, bias=w("decay")).then_inc(rate_ready, 1)
                        act.wait_ge(rate_ready, i + 1)
                        need(act, scan_ready, HK * (i - 1))
                        act.activation(decay[:, h, :], rate[:, :], ACT.Exp, scale=-1.0).then_inc(decay_ready, 1)
                        act.wait_ge(front_out, USES * i + V + 1)
                        need(act, bonus_ready, i)
                        act.activation(vv[:, :], front[V % 3][:, :], ACT.Copy).then_inc(v_ready, 1)
                        need(act, vb_out, HK * (i - 1))
                        act.activation(v_hi[:, h, :], front[V % 3][:, :], ACT.Copy).then_inc(vhi_ready, 1)
                    if step == 7:
                        act.wait_ge(front_out, USES * i + R + 1)
                        need(act, rs_ready, HK * (i - 1))
                        act.activation(rr[:, h, :], front[R % 3][:, :], ACT.Copy).then_inc(r_ready, 1)
                        act.wait_ge(front_out, USES * i + G + 1)
                        need(act, gate_ready, i)
                        act.activation(g_tanh[:, :], front[G % 3][:, :], ACT.Tanh, scale=0.5).then_inc(gtanh_ready, 1)

                def scan(i, h, step):
                    pass

                def tail(i, h, step):
                    if step == 2:
                        act.wait_ge(centred, i + 1)
                        need(act, yn_ready, i)
                        act.activation(yc[:, :], tail0[:, :], ACT.Copy).then_inc(yc_ready, 1)
                        act.activation(yc2[:, :], tail0[:, :], ACT.Square).then_inc(yc2_ready, 1)
                    if step == 3:
                        act.wait_ge(var_out, i + 1)
                        need(act, rstdy_ready, i)
                        act.activation(spread_y[:, :, :], tail1[:, 0:SUB * HEADS].rearrange("p (s c) -> p s c", s=SUB),
                                       ACT.Sqrt, bias=eps_gn[:, 0:1]).then_inc(std_ready, 1)
                    if step == 4:
                        act.wait_ge(rstdy_ready, i + 1)
                        need(act, rstdy_out, i)
                        act.activation(rstd_wide[:, :].rearrange("p (s j c) -> p s j c", s=SUB, j=HK),
                                       rstd_y[:, :, :].unsqueeze(2).broadcast_to([P, SUB, HK, HEADS]),
                                       ACT.Copy).then_inc(wide_ready, 1)
                    if step == 5:
                        act.wait_ge(yn_ready, i + 1)
                        need(act, z_ready, i)
                        act.activation(yl[:, :], yn[:, :], ACT.Identity, bias=w("shift"), scale=w("gain")).then_inc(yl_ready, 1)

                act.wait_ge(w_loaded, 32)
                act.wait_ge(eps_set, 1)
                pipeline(act, scan, ahead, tail)

            @block.gpsimd
            def _(pool):
                def ahead(i, h, step):
                    if step == 0:
                        pool.wait_ge(moments_ready, i + 1)
                        pool.tensor_tensor(var_eps[:, :], moments[:, :, 1], eps[:, :], ALU.add).then_inc(var_ready, 1)
                        pool.wait_ge(var_ready, i + 1)
                        need(pool, xn_ready, i)
                        pool.tensor_tensor(rstd[:, :], var_eps[:, :], half[:, :], ALU.pow).then_inc(rstd_ready, 1)
                    if step in (3, 4, 5):
                        for f in range(2 * (step - 3), min(2 * (step - 3) + 2, MIXES)):
                            pool.wait_ge(lerp_ready, MIXES * i + f + 1)
                            need(pool, front_out, USES * (i - 1) + (TD1, K, V, R, G)[f] + 1)
                            pool.tensor_tensor(xf[:, f, :], lerp[:, (f + h) % 2, :], xt[h][:, 1:TILE + 1], ALU.add).then_inc(xf_ready, 1)

                def scan(i, h, step):
                    j = step
                    if j == 0:
                        pool.wait_ge(r_ready, i + 1)
                    pool.wait_ge(scan_ready, HK * i + j + 1)
                    need(pool, y_out, 2 * (i - 1) + j // 4 + 1)
                    pool.tensor_tensor(rs[:, j, :], rr[:, h, :], state[:, j, seq_cols(h, 0)], ALU.mult).then_inc(rs_ready, 1)

                def tail(i, h, step):
                    pass

                pool.memset(eps_gn[:, :], GN_EPS).then_inc(eps_set, 1)
                pool.wait_ge(zeroed, 1)
                pipeline(pool, scan, ahead, tail)

EXPERTS, D_FF = 8, 512
FF_CHUNKS = D_FF // P
ROW_TILES = (TOKENS + EXPERTS * (P - 1)) // P
ROWS = ROW_TILES * P

B_PARTS = [("strict", P), ("ones", P), ("rank", EXPERTS), ("tile_no", ROW_TILES), ("bias_r", EXPERTS), ("wr", EXPERTS)]
B_AT, B_WIDTH = offsets(B_PARTS)


def shape_constants_b():
    c = np.zeros((P, B_WIDTH), np.float32)
    part = {name: c[:, a:b] for name, (a, b) in B_AT.items()}
    part["strict"][:] = np.triu(np.ones((P, P)), 1)
    part["ones"][:] = 1
    part["rank"][:] = np.arange(EXPERTS, 0, -1)
    part["tile_no"][:] = np.arange(ROW_TILES)
    return c, part


def top1_experts(nc, x_tok, consts, c_in, w1_in, w2_in, b1_in, b2_in):
    rows_in = nc.dram_tensor("rows_in", [ROWS, P], F32, kind="Internal").ap()
    rows_out = nc.dram_tensor("rows_out", [ROWS, P], F32, kind="Internal").ap()
    with ExitStack() as ctx:
        def sb(name, shape, dt=F32):
            return ctx.enter_context(nc.sbuf_tensor("b_" + name, shape, dt))

        def bank(name):
            return ctx.enter_context(nc.psum_tensor("b_" + name, [P, TILE], F32))

        def sem(name):
            return nc.alloc_semaphore("b_" + name)

        cb = sb("consts", [P, B_WIDTH])

        def const(name):
            return cb[:, B_AT[name][0]:B_AT[name][1]]

        ident = consts[:, C_AT["ident"][0]:C_AT["ident"][1]]
        w1 = sb("w1", [P, EXPERTS * D_FF])
        w2 = sb("w2", [P, EXPERTS * D_FF])
        b1 = sb("b1", [P, EXPERTS * D_FF])
        b2 = sb("b2", [P, EXPERTS * P])
        half = sb("minus_half", [P, SUB])
        eps = sb("eps", [P, SUB])
        ones = sb("ones_row", [P, GROUPS])
        zero_rows = sb("zero_rows", [P, ROW_TILES // 3, P])

        stats = sb("stats", [P, SUB, 6])
        moments = sb("moments", [P, SUB, 2])
        var_eps = sb("var_eps", [P, SUB])
        rstd = sb("rstd", [P, SUB])
        shift = sb("shift", [P, SUB])
        xn = sb("xn", [P, GROUPS, P])
        xn_tile = sb("xn_tile", [P, 2, SUB, P])
        xt = sb("xt", [P, 2, TILE])
        logits = sb("logits", [P, SUB, EXPERTS])
        best = sb("best", [P, SUB])
        is_best = sb("is_best", [P, SUB, EXPERTS])
        ranked = sb("ranked", [P, SUB, EXPERTS])
        top_rank = sb("top_rank", [P, SUB])
        chosen = sb("chosen", [P, GROUPS, EXPERTS])

        counts = sb("counts", [P, GROUPS, EXPERTS])
        upto = sb("upto", [P, EXPERTS, GROUPS])
        before = sb("before", [P, EXPERTS, GROUPS])
        rounded = sb("rounded", [P, EXPERTS], I32)
        n_tiles_i = sb("n_tiles_i", [P, EXPERTS], I32)
        n_tiles = sb("n_tiles", [P, EXPERTS])
        end_tile = sb("end_tile", [P, EXPERTS])
        base = sb("base", [P, EXPERTS])
        based = sb("based", [P, EXPERTS, GROUPS])
        place = sb("place", [P, GROUPS, EXPERTS])
        own_place = sb("own_place", [P, GROUPS, EXPERTS])
        position = sb("position", [P, GROUPS])
        index = sb("index", [P, GROUPS], U32)
        ended = sb("ended", [P, ROW_TILES, EXPERTS])
        expert_f = sb("expert_f", [P, ROW_TILES])
        expert = sb("expert", [P, ROW_TILES], I32)

        xin = sb("xin", [P, 2, P])
        xin_t = sb("xin_t", [P, 2, P])
        hidden = sb("hidden", [P, 2, D_FF])
        hidden_t = sb("hidden_t", [P, 2, D_FF])
        y_row = sb("y_row", [P, 2, P])

        bank_x = [bank(f"x{n}") for n in range(2)]
        bank_l = [bank(f"l{n}") for n in range(2)]
        bank_h = [bank(f"h{n}") for n in range(2)]
        bank_y = [bank(f"y{n}") for n in range(2)]

        c_loaded, w_loaded, zero_set, zeroed = sem("c_loaded"), sem("w_loaded"), sem("zero_set"), sem("zeroed")
        go = sem("go")
        stats_ready, moments_ready, var_ready = sem("stats_ready"), sem("moments_ready"), sem("var_ready")
        rstd_ready, shift_ready, xn_ready = sem("rstd_ready"), sem("shift_ready"), sem("xn_ready")
        xt_out, xt_ready, logits_out, choice = sem("xt_out"), sem("xt_ready"), sem("logits_out"), sem("choice")
        chosen_ready, counts_out, placing, index_ready = sem("chosen_ready"), sem("counts_out"), sem("placing"), sem("index_ready")
        scattered, gathered = sem("scattered"), [sem(f"gathered{n}") for n in range(4)]
        row_loaded = [sem(f"row_loaded{n}") for n in range(2)]
        row_stored = [sem(f"row_stored{n}") for n in range(2)]
        row_t_out, row_t_ready, h_out, h_ready = sem("row_t_out"), sem("row_t_ready"), sem("h_out"), sem("h_ready")
        ht_out, ht_ready, y_out, y_ready = sem("ht_out"), sem("ht_ready"), sem("y_out"), sem("y_ready")

        xn_kept = sem("xn_kept")
        CHOICE = 5

        def route(engine, ahead, choose):
            ahead(0, 0)
            for i in range(2):
                ahead(i + 1, 1 - i)
                choose(i, i)
            with engine.Fori(1, TILES // 2 - 1) as b:
                ahead(2 * b + 1, 1)
                choose(2 * b, 0)
                ahead(2 * b + 2, 0)
                choose(2 * b + 1, 1)
            ahead(TILES - 1, 1)
            choose(TILES - 2, 0)
            choose(TILES - 1, 1)

        def over_rows(engine, tile, first=None):
            for k in range(3):
                tile(k, k % 2)
            with engine.Fori(1, (ROW_TILES - 3) // 2) as b:
                tile(2 * b + 1, 1)
                tile(2 * b + 2, 0)
            tile(ROW_TILES - 2, 1)
            tile(ROW_TILES - 1, 0)

        with nc.Block() as block:
            @block.sync
            def _(sp):
                sp.dma_start(cb[:, :], c_in).then_inc(c_loaded, 16)
                sp.wait_ge(zero_set, 1)
                for n in range(3):
                    third = rows_in.rearrange("(n p t) c -> n p t c", n=3, p=P)[n]
                    sp.dma_start(third, zero_rows[:, :, :]).then_inc(zeroed, 16)
                sp.dma_start(w1[:, :], w1_in).then_inc(w_loaded, 16)
                sp.dma_start(w2[:, :], w2_in).then_inc(w_loaded, 16)
                sp.dma_start(b1[:, :], b1_in.broadcast_to([P, EXPERTS * D_FF])).then_inc(w_loaded, 16)
                sp.dma_start(b2[:, :], b2_in.broadcast_to([P, EXPERTS * P])).then_inc(w_loaded, 16)
                sp.wait_ge(scattered, 16 * GROUPS)

                def load(k, h):
                    need(sp, row_t_out, k - 1)
                    sp.dma_start(xin[:, h, :], rows_in[bass.ds(k * P, P), :]).then_inc(row_loaded[h], 16)

                def store(k, h):
                    sp.wait_ge(y_ready, k + 1)
                    sp.dma_start(rows_out[bass.ds(k * P, P), :], y_row[:, h, :]).then_inc(row_stored[h], 16)

                def tile(k, h):
                    if not (isinstance(k, int) and k >= ROW_TILES - 2):
                        load(k + 2, h)
                    if not (isinstance(k, int) and k == 0):
                        store(k - 1, 1 - h)

                load(0, 0)
                load(1, 1)
                over_rows(sp, tile)
                store(ROW_TILES - 1, 0)

            @block.tensor
            def _(pe):
                def ahead(i, h):
                    pe.wait_ge(xn_ready, i + 1)
                    need(pe, xt_ready, i - 1)
                    for s in range(SUB):
                        mm = pe.transpose(bank_x[h][:, s * P:(s + 1) * P], xn_tile[:, h, s, :], ident)
                    mm.then_inc(xt_out, 1)

                def choose(i, h):
                    pe.wait_ge(xt_ready, i + 1)
                    need(pe, choice, CHOICE * (i - 2) + 1)
                    for s in range(SUB):
                        mm = pe.matmul(bank_l[h][:, s * EXPERTS:(s + 1) * EXPERTS], xt[:, h, s * P:(s + 1) * P],
                                       const("wr"), start=True, stop=True)
                    mm.then_inc(logits_out, 1)

                pe.wait_ge(c_loaded, 16)
                route(pe, ahead, choose)
                pe.wait_ge(chosen_ready, TILES)
                flat = chosen[:, :, :].rearrange("p g e -> p (g e)")
                pe.matmul(bank_h[0][:, 0:GROUPS * EXPERTS], const("ones"), flat, start=True, stop=True).then_inc(counts_out, 1)
                pe.matmul(bank_h[1][:, 0:GROUPS * EXPERTS], const("strict"), flat, start=True, stop=True).then_inc(counts_out, 1)

                def turn_rows(k, h):
                    pe.wait_ge(row_loaded[h], 16 * (k // 2 + 1) if isinstance(k, int) else 8 * k + (16 - 8 * h))
                    if isinstance(k, int) and k < 2:
                        pe.wait_ge(xt_ready, TILES)
                    else:
                        pe.wait_ge(row_t_ready, k - 1)
                    pe.transpose(bank_x[h][:, 0:P], xin[:, h, :], ident).then_inc(row_t_out, 1)

                def expand(k, h, e):
                    pe.wait_ge(row_t_ready, k + 1)
                    need(pe, h_ready, k - 1)
                    pe.matmul(bank_h[h][:, :], xin_t[:, h, :], w1[:, bass.ds(e * D_FF, D_FF)],
                              start=True, stop=True).then_inc(h_out, 1)

                def turn_hidden(k, h):
                    pe.wait_ge(h_ready, k + 1)
                    need(pe, ht_ready, k - 1)
                    for f in range(FF_CHUNKS):
                        mm = pe.transpose(bank_l[h][:, f * P:(f + 1) * P], hidden[:, h, f * P:(f + 1) * P], ident)
                    mm.then_inc(ht_out, 1)

                def contract(k, h, e):
                    pe.wait_ge(ht_ready, k + 1)
                    need(pe, y_ready, k - 1)
                    for f in range(FF_CHUNKS):
                        mm = pe.matmul(bank_y[h][:, 0:P], hidden_t[:, h, f * P:(f + 1) * P],
                                       w2[:, bass.ds(e * D_FF + f * P, P)], start=(f == 0), stop=(f == FF_CHUNKS - 1))
                    mm.then_inc(y_out, 1)

                def tile(k, h):
                    def expert_of(n):
                        return pe.value_load(expert[0:1, bass.ds(n, 1)], min_val=0, max_val=EXPERTS - 1)
                    first = isinstance(k, int) and k == 0
                    if first:
                        turn_rows(0, 0)
                    else:
                        turn_hidden(k - 1, 1 - h)
                    expand(k, h, expert_of(k))
                    if not first:
                        contract(k - 1, 1 - h, expert_of(k - 1))
                    if not (isinstance(k, int) and k == ROW_TILES - 1):
                        turn_rows(k + 1, 1 - h)
                    else:
                        turn_hidden(k, h)
                        contract(k, h, expert_of(k))

                pe.wait_ge(index_ready, 2)
                pe.wait_ge(w_loaded, 64)
                over_rows(pe, tile)

            @block.vector
            def _(dve):
                def ahead(i, h):
                    need(dve, var_ready, i)
                    for s in range(SUB):
                        st = dve.bn_stats(stats[:, s, :], x_tok[:, SUB * i + s, :])
                    st.then_inc(stats_ready, 1)
                    dve.wait_ge(stats_ready, i + 1)
                    need(dve, shift_ready, i)
                    dve.sem_inc(go, 1)
                    for s in range(SUB):
                        ag = dve.bn_aggr(moments[:, s, :], stats[:, s, :])
                    ag.then_inc(moments_ready, 1)

                def choose(i, h):
                    def step(n):
                        dve.wait_ge(choice, CHOICE * i + n)
                    dve.wait_ge(logits_out, i + 1)
                    dve.tensor_tensor(logits[:, :, :], bank_l[h][:, 0:SUB * EXPERTS].rearrange("p (s e) -> p s e", s=SUB),
                                      const("bias_r").unsqueeze(1).broadcast_to([P, SUB, EXPERTS]), ALU.add).then_inc(choice, 1)
                    step(1)
                    dve.tensor_reduce(best[:, :], logits[:, :, :], AXIS.X, ALU.max).then_inc(choice, 1)
                    step(2)
                    dve.tensor_tensor(is_best[:, :, :], logits[:, :, :],
                                      best[:, :].unsqueeze(2).broadcast_to([P, SUB, EXPERTS]), ALU.is_equal).then_inc(choice, 1)
                    step(3)
                    dve.tensor_tensor(ranked[:, :, :], is_best[:, :, :],
                                      const("rank").unsqueeze(1).broadcast_to([P, SUB, EXPERTS]), ALU.mult).then_inc(choice, 1)
                    step(4)
                    dve.tensor_reduce(top_rank[:, :], ranked[:, :, :], AXIS.X, ALU.max).then_inc(choice, 1)
                    step(5)
                    out = chosen[:, bass.ds(SUB * i, SUB), :]
                    dve.tensor_tensor(out, ranked[:, :, :], top_rank[:, :].unsqueeze(2).broadcast_to([P, SUB, EXPERTS]),
                                      ALU.is_equal).then_inc(chosen_ready, 1)

                def pre(i, h):
                    ahead(i, h)
                    dve.wait_ge(rstd_ready, i + 1)
                    need(dve, xn_ready, i)
                    dve.scalar_tensor_tensor(shift[:, :], moments[:, :, 0], -1.0, rstd[:, :],
                                             ALU.mult, ALU.mult).then_inc(shift_ready, 1)

                dve.memset(eps[:, :], LN_EPS)
                dve.memset(half[:, :], -0.5)
                dve.memset(ones[:, :], 1.0)
                dve.memset(zero_rows[:, :, :], 0.0).then_inc(zero_set, 1)
                dve.wait_ge(zero_set, 1)
                dve.wait_ge(c_loaded, 16)
                route(dve, pre, choose)

                done = 0

                def put(instruction):
                    nonlocal done
                    done += 1
                    instruction.then_inc(placing, 1)

                def all_put():
                    dve.wait_ge(placing, done)

                by_expert = counts[:, :, :].rearrange("p g e -> p e g")
                grid = [P, EXPERTS, GROUPS]
                dve.wait_ge(counts_out, 2)
                put(dve.tensor_copy(counts[:, :, :].rearrange("p g e -> p (g e)"), bank_h[0][:, 0:GROUPS * EXPERTS]))
                all_put()
                for e in range(EXPERTS):
                    put(dve.tensor_tensor_scan(upto[:, e, :], ones[:, :], counts[:, :, e], 0.0, ALU.mult, ALU.add))
                all_put()
                put(dve.tensor_scalar(rounded[:, :], upto[:, :, GROUPS - 1], float(P - 1), None, ALU.add))
                put(dve.tensor_tensor(before[:, :, :], upto[:, :, :], by_expert, ALU.subtract))
                all_put()
                put(dve.tensor_scalar(n_tiles_i[:, :], rounded[:, :], P.bit_length() - 1, None, ALU.arith_shift_right))
                all_put()
                put(dve.tensor_copy(n_tiles[:, :], n_tiles_i[:, :]))
                all_put()
                put(dve.tensor_tensor_scan(end_tile[:, :], ones[:, 0:EXPERTS], n_tiles[:, :], 0.0, ALU.mult, ALU.add))
                all_put()
                put(dve.tensor_tensor(base[:, :], end_tile[:, :], n_tiles[:, :], ALU.subtract))
                put(dve.tensor_tensor(ended[:, :, :], end_tile[:, :].unsqueeze(1).broadcast_to([P, ROW_TILES, EXPERTS]),
                                      const("tile_no").unsqueeze(2).broadcast_to([P, ROW_TILES, EXPERTS]), ALU.is_le))
                all_put()
                put(dve.scalar_tensor_tensor(based[:, :, :], base[:, :].unsqueeze(2).broadcast_to(grid), float(P),
                                             before[:, :, :], ALU.mult, ALU.add))
                put(dve.tensor_reduce(expert_f[:, :], ended[:, :, :], AXIS.X, ALU.add))
                all_put()
                put(dve.tensor_tensor(place[:, :, :], based[:, :, :].rearrange("p e g -> p g e"),
                                      bank_h[1][:, 0:GROUPS * EXPERTS].rearrange("p (g e) -> p g e", g=GROUPS), ALU.add))
                dve.tensor_scalar(expert[:, :], expert_f[:, :], float(EXPERTS - 1), None, ALU.min).then_inc(index_ready, 1)
                all_put()
                put(dve.tensor_tensor(own_place[:, :, :], place[:, :, :], chosen[:, :, :], ALU.mult))
                all_put()
                put(dve.tensor_reduce(position[:, :], own_place[:, :, :], AXIS.X, ALU.add))
                all_put()
                dve.tensor_copy(index[:, :], position[:, :]).then_inc(index_ready, 1)

                def bias_hidden(k, h, e):
                    dve.wait_ge(h_out, k + 1)
                    need(dve, ht_out, k - 1)
                    dve.tensor_tensor(hidden[:, h, :], bank_h[h][:, :], b1[:, bass.ds(e * D_FF, D_FF)], ALU.add).then_inc(h_ready, 1)

                def bias_out(k, h, e):
                    dve.wait_ge(y_out, k + 1)
                    if not isinstance(k, int) or k >= 2:
                        dve.wait_ge(row_stored[h], 16 * (k // 2) if isinstance(k, int) else 8 * k - 8 * h)
                    dve.tensor_tensor(y_row[:, h, :], bank_y[h][:, 0:P], b2[:, bass.ds(e * P, P)], ALU.add).then_inc(y_ready, 1)

                def tile(k, h):
                    def expert_of(n):
                        return dve.value_load(expert[0:1, bass.ds(n, 1)], min_val=0, max_val=EXPERTS - 1)
                    bias_hidden(k, h, expert_of(k))
                    if not (isinstance(k, int) and k == 0):
                        bias_out(k - 1, 1 - h, expert_of(k - 1))
                    if isinstance(k, int) and k == ROW_TILES - 1:
                        bias_out(k, h, expert_of(k))

                dve.wait_ge(index_ready, 2)
                dve.wait_ge(w_loaded, 64)
                over_rows(dve, tile)
                for n in range(4):
                    dve.wait_ge(gathered[n], 16 * GROUPS // 4)
                    part = slice(n * GROUPS // 4, (n + 1) * GROUPS // 4)
                    dve.tensor_tensor(x_tok[:, part, :], x_tok[:, part, :], xn[:, part, :], ALU.add)

            @block.scalar
            def _(act):
                def ahead(i, h):
                    act.wait_ge(shift_ready, i + 1)
                    need(act, xt_out, i - 1)
                    need(act, xn_kept, i - 1)
                    for s in range(SUB):
                        a = act.activation(xn_tile[:, h, s, :], x_tok[:, SUB * i + s, :], ACT.Identity,
                                           bias=shift[:, s:s + 1], scale=rstd[:, s:s + 1])
                    a.then_inc(xn_ready, 1)
                    act.wait_ge(xt_out, i + 1)
                    need(act, logits_out, i - 1)
                    act.activation(xt[:, h, :], bank_x[h][:, :], ACT.Copy).then_inc(xt_ready, 1)

                def choose(i, h):
                    act.activation(xn[:, bass.ds(SUB * i, SUB), :], xn_tile[:, h, :, :], ACT.Copy).then_inc(xn_kept, 1)

                route(act, ahead, choose)

                def tile(k, h):
                    first = isinstance(k, int) and k == 0
                    if not first:
                        act.wait_ge(ht_out, k)
                        need(act, y_out, k - 2)
                        act.activation(hidden_t[:, 1 - h, :], bank_l[1 - h][:, :], ACT.Relu).then_inc(ht_ready, 1)
                    if first:
                        act.wait_ge(row_t_out, 1)
                        act.activation(xin_t[:, 0, :], bank_x[0][:, 0:P], ACT.Copy).then_inc(row_t_ready, 1)
                    if not (isinstance(k, int) and k == ROW_TILES - 1):
                        act.wait_ge(row_t_out, k + 2)
                        need(act, h_out, k)
                        act.activation(xin_t[:, 1 - h, :], bank_x[1 - h][:, 0:P], ACT.Copy).then_inc(row_t_ready, 1)
                    else:
                        act.wait_ge(ht_out, k + 1)
                        act.activation(hidden_t[:, h, :], bank_l[h][:, :], ACT.Relu).then_inc(ht_ready, 1)

                over_rows(act, tile)

            @block.gpsimd
            def _(pool):
                def ahead(i, h):
                    pool.wait_ge(moments_ready, i + 1)
                    need(pool, rstd_ready, i)
                    pool.tensor_tensor(var_eps[:, :], moments[:, :, 1], eps[:, :], ALU.add).then_inc(var_ready, 1)
                    pool.wait_ge(var_ready, i + 1)
                    need(pool, xn_ready, i)
                    pool.tensor_tensor(rstd[:, :], var_eps[:, :], half[:, :], ALU.pow).then_inc(rstd_ready, 1)

                def choose(i, h):
                    pass

                pool.wait_ge(zero_set, 1)
                route(pool, ahead, choose)
                pool.wait_ge(index_ready, 2)
                pool.wait_ge(xn_kept, TILES)
                pool.wait_ge(zeroed, 48)
                for g in range(GROUPS):
                    pool.indirect_dma_start(rows_in, bass.IndirectOffsetOnAxis(ap=index[:, g:g + 1], axis=0),
                                            xn[:, g, :], None).then_inc(scattered, 16)
                pool.wait_ge(scattered, 16 * GROUPS)
                pool.wait_ge(row_stored[0], 16 * ((ROW_TILES + 1) // 2))
                pool.wait_ge(row_stored[1], 16 * (ROW_TILES // 2))
                for g in range(GROUPS):
                    pool.indirect_dma_start(xn[:, g, :], None, rows_out,
                                            bass.IndirectOffsetOnAxis(ap=index[:, g:g + 1], axis=0)).then_inc(gathered[g // (GROUPS // 4)], 16)

QUATS, QC = P // 4, 4
NORM_EPS = 1e-12
C_W = [("wk", QC * P), ("wv", P), ("bk", QC * P), ("bv", P), ("wo", P), ("bo", P), ("gain", 1), ("shift", 1),
       ("eps_pos", PER_SEQ * SUB), ("upto", P), ("last", P)]
CW_AT, CW_WIDTH = offsets(C_W)
MINUS = [(1, 0), (1, 2), (2, 0), (2, 3), (3, 0), (3, 1)]


def shape_constants_c():
    c = np.zeros((P, CW_WIDTH), np.float32)
    part = {name: c[:, a:b] for name, (a, b) in CW_AT.items()}
    part["eps_pos"][:] = LN_EPS * (np.arange(PER_SEQ * SUB)[None] * P + np.arange(P)[:, None] + 1)
    part["upto"][:] = np.triu(np.ones((P, P)))
    part["last"][P - 1] = 1
    return c, part


def in_steps(engine, ahead, main, tail):
    for step in range(8):
        ahead(0, 0, step)
    for i in range(3):
        for step in range(8):
            if i:
                tail(i - 1, 1 - i % 2, step)
            main(i, i % 2, step)
            ahead(i + 1, 1 - i % 2, step)
    with engine.Fori(1, TILES // 2 - 1) as b:
        for h in (1, 0):
            i = 2 * b + (1 if h else 2)
            for step in range(8):
                tail(i - 1, 1 - h, step)
                main(i, h, step)
                ahead(i + 1, 1 - h, step)
    for step in range(8):
        tail(TILES - 2, 0, step)
        main(TILES - 1, 1, step)
    for step in range(8):
        tail(TILES - 1, 1, step)


def quaternion_memory(nc, x_tok, consts, w_in):
    with ExitStack() as ctx:
        def sb(name, shape, dt=F32):
            return ctx.enter_context(nc.sbuf_tensor("c_" + name, shape, dt))

        def bank(name):
            return ctx.enter_context(nc.psum_tensor("c_" + name, [P, TILE], F32))

        def sem(name):
            return nc.alloc_semaphore("c_" + name)

        weights = sb("weights", [P, CW_WIDTH])

        def w(name):
            return weights[:, CW_AT[name][0]:CW_AT[name][1]]

        ident = consts[:, C_AT["ident"][0]:C_AT["ident"][1]]
        half = sb("minus_half", [P, SUB])
        eps = sb("eps", [P, SUB])
        stats = sb("stats", [P, SUB, 6])
        moments = sb("moments", [P, SUB, 2])
        var_eps = sb("var_eps", [P, SUB])
        rstd = sb("rstd", [P, SUB])
        shift = sb("shift", [P, SUB])
        xn = sb("xn", [P, SUB, P])
        xt = sb("xt", [P, TILE])
        key = sb("key", [P, 2, SUB, QC, P])
        value = sb("value", [P, SUB, P])
        square = sb("square", [P, SUB, P])
        norm2 = sb("norm2", [P, P])
        norm = sb("norm", [P, P])
        norm_max = sb("norm_max", [P, P])
        rnorm = sb("rnorm", [P, 2, P])
        value_n = sb("value_n", [P, SUB, P])
        bound = sb("bound", [P, SUB, QC, P])
        memory = sb("memory", [P, 2, SUB, P])
        memory_n = sb("memory_n", [P, SUB, P])
        read = sb("read", [P, SUB, QC, P])
        real = sb("real", [P, SUB, P])
        got = sb("got", [P, SUB, P])
        stats2 = sb("stats2", [P, SUB, 6])
        moments2 = sb("moments2", [P, SUB, 2])
        var_eps2 = sb("var_eps2", [P, SUB])
        rstd2 = sb("rstd2", [P, SUB])
        shift2 = sb("shift2", [P, SUB])
        normed = sb("normed", [P, SUB, P])
        normed_t = sb("normed_t", [P, TILE])
        kept0 = sb("kept0", [P, SUB, P])
        kept = sb("kept", [P, 2, SUB, P])

        bank_x, bank_v, bank_r, bank_o = bank("x"), bank("v"), bank("r"), bank("o")
        bank_k = [bank(f"k{n}") for n in range(2)]
        bank_m = [bank(f"m{n}") for n in range(2)]

        w_loaded, half_set, signed = sem("w_loaded"), sem("half_set"), sem("signed")
        go = sem("go")
        stats_ready, moments_ready, var_ready = sem("stats_ready"), sem("moments_ready"), sem("var_ready")
        rstd_ready, shift_ready, xn_ready = sem("rstd_ready"), sem("shift_ready"), sem("xn_ready")
        xt_out, xt_ready = sem("xt_out"), sem("xt_ready")
        k_out, v_out, key_ready, value_ready = sem("k_out"), sem("v_out"), sem("key_ready"), sem("value_ready")
        square_ready, norm2_ready, norm_ready, max_ready = sem("square_ready"), sem("norm2_ready"), sem("norm_ready"), sem("max_ready")
        rnorm_ready, valuen_ready = sem("rnorm_ready"), sem("valuen_ready")
        bound_dve, bound_pool = sem("bound_dve"), sem("bound_pool")
        memory_out, memory_ready, memoryn_ready = sem("memory_out"), sem("memory_ready"), sem("memoryn_ready")
        read_dve, read_pool = sem("read_dve"), sem("read_pool")
        read_out, real_ready, got_ready = sem("read_out"), sem("real_ready"), sem("got_ready")
        stats2_ready, moments2_ready, var2_ready = sem("stats2_ready"), sem("moments2_ready"), sem("var2_ready")
        rstd2_ready, shift2_ready, normed_ready = sem("rstd2_ready"), sem("shift2_ready"), sem("normed_ready")
        normedt_out, normedt_ready, wo_out, x_ready = sem("normedt_out"), sem("normedt_ready"), sem("wo_out"), sem("x_ready")
        kept0_ready, kept_ready = sem("kept0_ready"), sem("kept_ready")

        def by_quat(ap):
            return ap.rearrange("p s (q c) -> p (s q) c", c=QC)

        def per_quat(ap):
            return ap.unsqueeze(2).broadcast_to([P, P, QC])

        def spread_component(ap):
            return ap.rearrange("p (q m) -> p m q", m=QC).unsqueeze(3).broadcast_to([P, QC, QUATS, QC])

        def in_quats(ap):
            return ap.rearrange("p m (q c) -> p m q c", c=QC)

        with nc.Block() as block:
            @block.sync
            def _(sp):
                sp.dma_start(weights[:, :], w_in).then_inc(w_loaded, 16)

            @block.tensor
            def _(pe):
                def ahead(i, h, step):
                    if step == 1:
                        pe.wait_ge(xn_ready, i + 1)
                        need(pe, normedt_ready, i - 2)
                        for s in range(SUB):
                            mm = pe.transpose(bank_x[:, s * P:(s + 1) * P], xn[:, s, :], ident)
                        mm.then_inc(xt_out, 1)
                    if step in (2, 3):
                        if step == 2:
                            pe.wait_ge(xt_ready, i + 1)
                            need(pe, value_ready, i)
                        for s in (0, 1) if step == 2 else (2, 3):
                            need(pe, key_ready, SUB * i + s - 1)
                            tokens = xt[:, s * P:(s + 1) * P]
                            pe.matmul(bank_k[s % 2][:, :], tokens, w("wk"), start=True, stop=True).then_inc(k_out, 1)
                            mm = pe.matmul(bank_v[:, s * P:(s + 1) * P], tokens, w("wv"), start=True, stop=True)
                        if step == 3:
                            mm.then_inc(v_out, 1)

                def main(i, h, step):
                    if step in (1, 2, 3, 4):
                        s = step - 1
                        if s < 2:
                            pe.wait_ge(bound_dve, 2 * i + s + 1)
                        else:
                            pe.wait_ge(bound_pool, 2 * i + s - 1)
                        need(pe, memory_ready, SUB * i + s - 1)
                        carried = h or s
                        for m in range(QC):
                            mm = pe.matmul(bank_m[s % 2][:, 0:P], w("upto"), bound[:, s, m, :],
                                           start=(m == 0), stop=(m == QC - 1 and not carried))
                        if carried:
                            pe.wait_ge(memory_ready, SUB * i + s)
                            before = memory[:, h, s - 1, :] if s else memory[:, 1 - h, SUB - 1, :]
                            mm = pe.matmul(bank_m[s % 2][:, 0:P], w("last"), before, start=False, stop=True)
                        mm.then_inc(memory_out, 1)
                    if step == 7:
                        need(pe, got_ready, i)
                        for s in range(SUB):
                            if s < 2:
                                pe.wait_ge(read_dve, 2 * i + s + 1)
                            else:
                                pe.wait_ge(read_pool, 2 * i + s - 1)
                            for m in range(QC):
                                mm = pe.matmul(bank_r[:, s * P:(s + 1) * P], ident, read[:, s, m, :],
                                               start=(m == 0), stop=(m == QC - 1))
                        mm.then_inc(read_out, 1)

                def tail(i, h, step):
                    if step == 3:
                        pe.wait_ge(normed_ready, i + 1)
                        pe.wait_ge(xt_ready, min(i + 3, TILES) if isinstance(i, int) else i + 3)
                        for s in range(SUB):
                            mm = pe.transpose(bank_x[:, s * P:(s + 1) * P], normed[:, s, :], ident)
                        mm.then_inc(normedt_out, 1)
                    if step == 5:
                        pe.wait_ge(normedt_ready, i + 1)
                        need(pe, x_ready, i)
                        for s in range(SUB):
                            mm = pe.matmul(bank_o[:, s * P:(s + 1) * P], normed_t[:, s * P:(s + 1) * P], w("wo"),
                                           start=True, stop=True)
                        mm.then_inc(wo_out, 1)

                pe.wait_ge(w_loaded, 16)
                pe.wait_ge(signed, 2 * len(MINUS))
                in_steps(pe, ahead, main, tail)

            @block.vector
            def _(dve):
                def ahead(i, h, step):
                    if step == 0:
                        need(dve, var_ready, i)
                        for s in range(SUB):
                            st = dve.bn_stats(stats[:, s, :], x_tok[:, SUB * i + s, :])
                        st.then_inc(stats_ready, 1)
                        dve.wait_ge(stats_ready, i + 1)
                        need(dve, shift_ready, i)
                        dve.sem_inc(go, 1)
                        for s in range(SUB):
                            ag = dve.bn_aggr(moments[:, s, :], stats[:, s, :])
                        ag.then_inc(moments_ready, 1)
                    if step == 1:
                        dve.wait_ge(rstd_ready, i + 1)
                        need(dve, xn_ready, i)
                        dve.scalar_tensor_tensor(shift[:, :], moments[:, :, 0], -1.0, rstd[:, :],
                                                 ALU.mult, ALU.mult).then_inc(shift_ready, 1)
                    if step in (3, 4):
                        for s in (0, 1) if step == 3 else (2, 3):
                            dve.wait_ge(k_out, SUB * i + s + 1)
                            need(dve, real_ready, i - 1)
                            need(dve, read_pool, 2 * (i - 1))
                            dve.tensor_tensor(key[:, h, s, :, :].rearrange("p m c -> p (m c)"), bank_k[s % 2][:, :], w("bk"),
                                              ALU.add).then_inc(key_ready, 1)
                    if step == 5:
                        dve.wait_ge(v_out, i + 1)
                        need(dve, valuen_ready, i)
                        dve.tensor_tensor(value[:, :, :], bank_v[:, :].rearrange("p (s c) -> p s c", s=SUB),
                                          w("bv").unsqueeze(1).broadcast_to([P, SUB, P]), ALU.add).then_inc(value_ready, 1)
                        dve.wait_ge(square_ready, i + 1)
                        need(dve, norm_ready, i)
                        dve.tensor_reduce(norm2[:, :], by_quat(square[:, :, :]), AXIS.X, ALU.add).then_inc(norm2_ready, 1)
                    if step == 6:
                        dve.wait_ge(norm_ready, i + 1)
                        dve.tensor_scalar(norm_max[:, :], norm[:, :], NORM_EPS, None, ALU.max).then_inc(max_ready, 1)
                        dve.wait_ge(max_ready, i + 1)
                        dve.reciprocal(rnorm[:, h, :], norm_max[:, :]).then_inc(rnorm_ready, 1)
                    if step == 7:
                        dve.wait_ge(value_ready, i + 1)
                        dve.wait_ge(rnorm_ready, i + 1)
                        need(dve, bound_dve, 2 * i)
                        need(dve, bound_pool, 2 * i)
                        dve.tensor_tensor(by_quat(value_n[:, :, :]), by_quat(value[:, :, :]), per_quat(rnorm[:, h, :]),
                                          ALU.mult).then_inc(valuen_ready, 1)

                def main(i, h, step):
                    if step == 0:
                        dve.wait_ge(valuen_ready, i + 1)
                        need(dve, memory_out, SUB * i)
                        for s in (0, 1):
                            dve.tensor_tensor(in_quats(bound[:, s, :, :]), in_quats(key[:, h, s, :, :]),
                                              spread_component(value_n[:, s, :]), ALU.mult).then_inc(bound_dve, 1)
                    if step == 5:
                        dve.wait_ge(memory_ready, SUB * (i + 1))
                        need(dve, real_ready, i)
                        need(dve, read_pool, 2 * i)
                        dve.tensor_tensor(by_quat(memory_n[:, :, :]), by_quat(memory[:, h, :, :]), per_quat(rnorm[:, h, :]),
                                          ALU.mult).then_inc(memoryn_ready, 1)
                    if step == 6:
                        dve.wait_ge(memoryn_ready, i + 1)
                        need(dve, read_out, i)
                        for s in (0, 1):
                            dve.tensor_tensor(in_quats(read[:, s, :, :]), in_quats(key[:, h, s, :, :]),
                                              spread_component(memory_n[:, s, :]), ALU.mult).then_inc(read_dve, 1)
                    if step == 7:
                        need(dve, got_ready, i)
                        k0 = key[:, h, :, 0, 0:P:QC]
                        dve.tensor_tensor(real[:, :, :].rearrange("p s (q c) -> p s q c", c=QC),
                                          memory_n[:, :, :].rearrange("p s (q c) -> p s q c", c=QC),
                                          k0.unsqueeze(3).broadcast_to([P, SUB, QUATS, QC]), ALU.mult).then_inc(real_ready, 1)

                def tail(i, h, step):
                    if step == 0:
                        dve.wait_ge(real_ready, i + 1)
                        dve.wait_ge(read_out, i + 1)
                        need(dve, normed_ready, i)
                        dve.scalar_tensor_tensor(got[:, :, :].rearrange("p s c -> p (s c)"), real[:, :, :].rearrange("p s c -> p (s c)"),
                                                 2.0, bank_r[:, :], ALU.mult, ALU.subtract).then_inc(got_ready, 1)
                        dve.wait_ge(got_ready, i + 1)
                        for s in range(SUB):
                            st = dve.bn_stats(stats2[:, s, :], got[:, s, :])
                        st.then_inc(stats2_ready, 1)
                        dve.wait_ge(stats2_ready, i + 1)
                        dve.sem_inc(go, 1)
                        for s in range(SUB):
                            ag = dve.bn_aggr(moments2[:, s, :], stats2[:, s, :])
                        ag.then_inc(moments2_ready, 1)
                    if step == 2:
                        dve.wait_ge(rstd2_ready, i + 1)
                        dve.scalar_tensor_tensor(shift2[:, :], moments2[:, :, 0], -1.0, rstd2[:, :],
                                                 ALU.mult, ALU.mult).then_inc(shift2_ready, 1)
                    if step == 5:
                        dve.wait_ge(wo_out, i + 1)
                        dve.wait_ge(kept_ready, i + 1)
                        dve.tensor_tensor(x_tok[:, bass.ds(SUB * i, SUB), :], bank_o[:, :].rearrange("p (s c) -> p s c", s=SUB),
                                          kept[:, h, :, :], ALU.add).then_inc(x_ready, 1)

                dve.memset(eps[:, :], LN_EPS)
                dve.memset(half[:, :], -0.5).then_inc(half_set, 1)
                dve.wait_ge(w_loaded, 16)
                for name in ("wk", "bk"):
                    for m, c in MINUS:
                        place = w(name)[:, m * P + c:(m + 1) * P:QC]
                        dve.tensor_scalar(place, place, -1.0, None, ALU.mult).then_inc(signed, 1)
                dve.wait_ge(signed, 2 * len(MINUS))
                in_steps(dve, ahead, main, tail)

            @block.scalar
            def _(act):
                def ahead(i, h, step):
                    if step == 1:
                        act.wait_ge(shift_ready, i + 1)
                        need(act, xt_out, i)
                        need(act, kept0_ready, i)
                        for s in range(SUB):
                            a = act.activation(xn[:, s, :], x_tok[:, SUB * i + s, :], ACT.Identity,
                                               bias=shift[:, s:s + 1], scale=rstd[:, s:s + 1])
                        a.then_inc(xn_ready, 1)
                        act.wait_ge(xt_out, i + 1)
                        need(act, v_out, i)
                        act.activation(xt[:, :], bank_x[:, :], ACT.Copy).then_inc(xt_ready, 1)
                    if step == 4:
                        act.wait_ge(key_ready, SUB * (i + 1))
                        need(act, norm2_ready, i)
                        act.activation(square[:, :, :], key[:, h, :, 0, :], ACT.Square).then_inc(square_ready, 1)
                    if step == 5:
                        act.wait_ge(norm2_ready, i + 1)
                        need(act, max_ready, i)
                        act.activation(norm[:, :], norm2[:, :], ACT.Sqrt).then_inc(norm_ready, 1)

                def main(i, h, step):
                    if step in (1, 2, 3, 4):
                        s = step - 1
                        act.wait_ge(memory_out, SUB * i + s + 1)
                        need(act, memoryn_ready, i - 1)
                        act.activation(memory[:, h, s, :], bank_m[s % 2][:, 0:P], ACT.Copy).then_inc(memory_ready, 1)

                def tail(i, h, step):
                    if step == 2:
                        act.wait_ge(shift2_ready, i + 1)
                        need(act, normedt_out, i)
                        for s in range(SUB):
                            a = act.activation(normed[:, s, :], got[:, s, :], ACT.Identity,
                                               bias=shift2[:, s:s + 1], scale=rstd2[:, s:s + 1])
                        a.then_inc(normed_ready, 1)
                    if step == 3:
                        act.wait_ge(normedt_out, i + 1)
                        need(act, wo_out, i)
                        act.activation(normed_t[:, :], bank_x[:, :], ACT.Identity, bias=w("shift"), scale=w("gain")).then_inc(normedt_ready, 1)

                act.wait_ge(w_loaded, 16)
                in_steps(act, ahead, main, tail)

            @block.gpsimd
            def _(pool):
                def ahead(i, h, step):
                    if step == 0:
                        pool.wait_ge(moments_ready, i + 1)
                        pool.tensor_tensor(var_eps[:, :], moments[:, :, 1], eps[:, :], ALU.add).then_inc(var_ready, 1)
                        pool.wait_ge(var_ready, i + 1)
                        need(pool, xn_ready, i)
                        pool.tensor_tensor(rstd[:, :], var_eps[:, :], half[:, :], ALU.pow).then_inc(rstd_ready, 1)
                    if step == 6:
                        pool.wait_ge(xn_ready, i + 1)
                        pool.tensor_tensor(kept0[:, :, :], xn[:, :, :], w("bo").unsqueeze(1).broadcast_to([P, SUB, P]),
                                           ALU.add).then_inc(kept0_ready, 1)
                        pool.wait_ge(kept0_ready, i + 1)
                        need(pool, x_ready, i - 1)
                        pool.tensor_tensor(kept[:, h, :, :], kept0[:, :, :], x_tok[:, bass.ds(SUB * i, SUB), :],
                                           ALU.add).then_inc(kept_ready, 1)

                def main(i, h, step):
                    if step == 0:
                        pool.wait_ge(valuen_ready, i + 1)
                        need(pool, memory_out, SUB * i)
                        for s in (2, 3):
                            pool.tensor_tensor(in_quats(bound[:, s, :, :]), in_quats(key[:, h, s, :, :]),
                                               spread_component(value_n[:, s, :]), ALU.mult).then_inc(bound_pool, 1)
                    if step == 6:
                        pool.wait_ge(memoryn_ready, i + 1)
                        need(pool, read_out, i)
                        for s in (2, 3):
                            pool.tensor_tensor(in_quats(read[:, s, :, :]), in_quats(key[:, h, s, :, :]),
                                               spread_component(memory_n[:, s, :]), ALU.mult).then_inc(read_pool, 1)

                def tail(i, h, step):
                    if step == 1:
                        pool.wait_ge(moments2_ready, i + 1)
                        pool.tensor_tensor(var_eps2[:, :], moments2[:, :, 1], w("eps_pos")[:, h * SUB:(h + 1) * SUB],
                                           ALU.add).then_inc(var2_ready, 1)
                        pool.wait_ge(var2_ready, i + 1)
                        need(pool, normed_ready, i)
                        pool.tensor_tensor(rstd2[:, :], var_eps2[:, :], half[:, :], ALU.pow).then_inc(rstd2_ready, 1)

                pool.wait_ge(half_set, 1)
                pool.wait_ge(w_loaded, 16)
                in_steps(pool, ahead, main, tail)

E2, H2, TOP_K = 32, 64, 4
CAPACITY = 4 * (TOKENS * TOP_K) // E2
PAIRS = E2 // 2
UNITS = PAIRS + 1
D_W = [("wg", E2), ("spread", PAIRS * P), ("segment", SUB * E2), ("strict", P), ("ones", P)]
DW_AT, DW_WIDTH = offsets(D_W)


def shape_constants_d():
    c = np.zeros((P, DW_WIDTH), np.float32)
    part = {name: c[:, a:b] for name, (a, b) in DW_AT.items()}
    for e in range(E2):
        for half in (0, E2):
            part["spread"][half + e, e * H2:(e + 1) * H2] = 1
    part["segment"][:] = np.arange(SUB * E2) % E2 != 0
    part["strict"][:] = np.triu(np.ones((P, P)), 1)
    part["ones"][:] = 1
    return c, part


def top4_experts(nc, x_tok, consts, out_dram, w_in, w1_in, w3_in, w2_in):
    with ExitStack() as ctx:
        def sb(name, shape, dt=F32):
            return ctx.enter_context(nc.sbuf_tensor("d_" + name, shape, dt))

        def bank(name):
            return ctx.enter_context(nc.psum_tensor("d_" + name, [P, TILE], F32))

        def sem(name):
            return nc.alloc_semaphore("d_" + name)

        small = sb("small", [P, DW_WIDTH])

        def w(name):
            return small[:, DW_AT[name][0]:DW_AT[name][1]]

        ident = consts[:, C_AT["ident"][0]:C_AT["ident"][1]]
        raw = [sb(f"raw{n}", [P, UNITS * P]) for n in range(3)]
        hi = [sb(f"hi{n}", [P, UNITS * P], F32R) for n in range(3)]
        lo = [sb(f"lo{n}", [P, UNITS * P], F32R) for n in range(3)]
        spread = sb("spread", [P, PAIRS * P], F32R)
        wg_hi = sb("wg_hi", [P, E2], F32R)
        wg_lo = sb("wg_lo", [P, E2], F32R)
        strict = sb("strict", [P, P], BF16)
        ones = sb("ones", [P, P], BF16)
        half = sb("minus_half", [P, SUB])
        eps = sb("eps", [P, SUB])

        stats = sb("stats", [P, SUB, 6])
        moments = sb("moments", [P, SUB, 2])
        var_eps = sb("var_eps", [P, SUB])
        rstd = sb("rstd", [P, SUB])
        shift = sb("shift", [P, SUB])
        xn = sb("xn", [P, SUB, P])
        x_hi = sb("x_hi", [P, 2, TILE], F32R)
        x_lo = sb("x_lo", [P, 2, TILE], F32R)

        minus_max = sb("minus_max", [P, SUB])
        exps = sb("exps", [P, SUB, E2])
        total = sb("total", [P, SUB])
        inverse = sb("inverse", [P, SUB])
        scores = sb("scores", [P, SUB, E2])
        top = sb("top", [P, SUB, 8])
        above = sb("above", [P, SUB, E2])
        n_above = sb("n_above", [P, SUB])
        room = sb("room", [P, SUB])
        equal = sb("equal", [P, SUB, E2])
        nth_equal = sb("nth_equal", [P, SUB, E2])
        fits = sb("fits", [P, SUB, E2])
        taken = sb("taken", [P, SUB, E2])
        mask = sb("mask", [P, SUB, E2])
        mask_b = sb("mask_b", [P, SUB, E2], BF16)
        used = sb("used", [P, E2])
        rank = sb("rank", [P, SUB, E2])
        masked = sb("masked", [P, SUB, E2])
        weight = sb("weight", [P, SUB, E2])
        parts = sb("parts", [P, SUB, P])
        parts_t = sb("parts_t", [P, 2, TILE], F32R)

        silu = sb("silu", [P, 2, TILE])
        product = sb("product", [P, 2, TILE])
        hidden = sb("hidden", [P, 2, TILE])
        hid_hi = sb("hid_hi", [P, 2, TILE], F32R)
        hid_lo = sb("hid_lo", [P, 2, TILE], F32R)
        y_sb = sb("y_sb", [P, TILE])
        out_sb = [sb(f"out{n}", [P, SUB, P]) for n in range(2)]

        bank_1 = [bank(f"h1_{n}") for n in range(2)]
        bank_3 = [bank(f"h3_{n}") for n in range(2)]
        bank_w = bank("w")
        bank_y = [bank(f"y{n}") for n in range(2)]
        bank_x = bank("x")

        loaded = [sem(f"loaded{n}") for n in range(4)]
        set_up, split_hi, split_lo = sem("set_up"), sem("split_hi"), sem("split_lo")
        go = sem("go")
        stats_ready, moments_ready, var_ready = sem("stats_ready"), sem("moments_ready"), sem("var_ready")
        rstd_ready, shift_ready, xn_ready = sem("rstd_ready"), sem("shift_ready"), sem("xn_ready")
        xt_out, xhi_ready, xlo_ready = sem("xt_out"), sem("xhi_ready"), sem("xlo_ready")
        logits_out, exps_ready, routing, mask_ready = sem("logits_out"), sem("exps_ready"), sem("routing"), sem("mask_ready")
        rank_out, parts_ready, parts_out, partst_ready = sem("rank_out"), sem("parts_ready"), sem("parts_out"), sem("partst_ready")
        h1_out, h3_out, w_out = sem("h1_out"), sem("h3_out"), sem("w_out")
        silu_ready, product_ready, hidden_ready = sem("silu_ready"), sem("product_ready"), sem("hidden_ready")
        hi_ready, lo_ready, unit_out = sem("hi_ready"), sem("lo_ready"), sem("unit_out")
        y_ready, yt_out, out_ready, stored = sem("y_ready"), sem("yt_out"), sem("out_ready"), [sem(f"stored{n}") for n in range(2)]

        ranking = sem("ranking")
        ROUTING = 14

        def schedule(engine, ahead, unit, end):
            for step in range(UNITS):
                ahead(0, 0, step)
            for i in range(3):
                for u in range(UNITS):
                    unit(i, i % 2, u)
                    if i:
                        end(i - 1, 1 - i % 2, u)
                    ahead(i + 1, 1 - i % 2, u)
            with engine.Fori(1, TILES // 2 - 1) as b:
                for h in (1, 0):
                    i = 2 * b + (1 if h else 2)
                    for u in range(UNITS):
                        unit(i, h, u)
                        end(i - 1, 1 - h, u)
                        ahead(i + 1, 1 - h, u)
            for u in range(UNITS):
                unit(TILES - 1, 1, u)
                end(TILES - 2, 0, u)
            for u in range(UNITS):
                end(TILES - 1, 1, u)

        with nc.Block() as block:
            @block.sync
            def _(sp):
                sp.dma_start(small[:, :], w_in).then_inc(loaded[3], 16)
                for n, w_dram in enumerate((w1_in, w3_in, w2_in)):
                    sp.dma_start(raw[n][:, :], w_dram).then_inc(loaded[n], 16)

                def ahead(i, h, u):
                    pass

                def unit(i, h, u):
                    pass

                def end(i, h, u):
                    if u == 6:
                        sp.wait_ge(out_ready, i + 1)
                        sp.dma_start(out_dram[:, bass.ds(SUB * i, SUB), :], out_sb[h][:, :, :]).then_inc(stored[h], 16)

                schedule(sp, ahead, unit, end)
                for n in range(2):
                    sp.wait_ge(stored[n], 16 * TILES // 2)

            @block.tensor
            def _(pe):
                def three(out, weights_hi, weights_lo, moving_hi, moving_lo, start=True, stop=True):
                    pe.matmul(out, weights_hi, moving_hi, start=start, stop=False)
                    pe.matmul(out, weights_hi, moving_lo, start=False, stop=False)
                    return pe.matmul(out, weights_lo, moving_hi, start=False, stop=stop)

                def ahead(i, h, u):
                    if u == 3:
                        pe.wait_ge(xn_ready, i + 1)
                        need(pe, partst_ready, i)
                        for s in range(SUB):
                            mm = pe.transpose(bank_x[:, s * P:(s + 1) * P], xn[:, s, :], ident)
                        mm.then_inc(xt_out, 1)
                    if u == 5:
                        pe.wait_ge(xlo_ready, i + 1)
                        pe.wait_ge(xhi_ready, i + 1)
                        need(pe, out_ready, i - 1)
                        for s in range(SUB):
                            tokens = slice(s * P, (s + 1) * P)
                            mm = three(bank_x[:, s * E2:(s + 1) * E2], x_hi[:, h, tokens], x_lo[:, h, tokens],
                                       wg_hi[:, :], wg_lo[:, :])
                        mm.then_inc(logits_out, 1)
                    if u == 11:
                        pe.wait_ge(mask_ready, i + 1)
                        for s in range(SUB):
                            for t in range(s):
                                pe.matmul(bank_x[:, s * E2:(s + 1) * E2], ones[:, :], mask_b[:, t, :], start=(t == 0), stop=False)
                            pe.matmul(bank_x[:, s * E2:(s + 1) * E2], strict[:, :], mask_b[:, s, :], start=(s == 0), stop=True)
                        for t in range(SUB):
                            mm = pe.matmul(bank_x[:, SUB * E2:(SUB + 1) * E2], ones[:, :], mask_b[:, t, :],
                                           start=(t == 0), stop=(t == SUB - 1))
                        mm.then_inc(rank_out, 1)
                    if u == 14:
                        pe.wait_ge(parts_ready, i + 1)
                        for s in range(SUB):
                            mm = pe.transpose(bank_x[:, s * P:(s + 1) * P], parts[:, s, :], ident)
                        mm.then_inc(parts_out, 1)

                def second(i, h, u):
                    n, r = UNITS * i + u, (h + u) % 2
                    pe.wait_ge(hi_ready, n + 1)
                    pe.wait_ge(lo_ready, n + 1)
                    if u == 0:
                        need(pe, y_ready, i - 1)
                    cols = slice(u * P, (u + 1) * P)
                    three(bank_y[h][:, :], hi[2][:, cols], lo[2][:, cols], hid_hi[:, r, :], hid_lo[:, r, :],
                          start=(u == 0), stop=(u == UNITS - 1)).then_inc(unit_out, 1)

                def unit(i, h, u):
                    n, r = UNITS * i + u, (h + u) % 2
                    if u == 0:
                        pe.wait_ge(xlo_ready, i + 1)
                        pe.wait_ge(xhi_ready, i + 1)
                    cols = slice(u * P, (u + 1) * P)
                    need(pe, silu_ready, n - 1)
                    three(bank_1[r][:, :], hi[0][:, cols], lo[0][:, cols], x_hi[:, h, :], x_lo[:, h, :]).then_inc(h1_out, 1)
                    need(pe, product_ready, n - 1)
                    three(bank_3[r][:, :], hi[1][:, cols], lo[1][:, cols], x_hi[:, h, :], x_lo[:, h, :]).then_inc(h3_out, 1)
                    if u < PAIRS:
                        if u == 0:
                            pe.wait_ge(partst_ready, i + 1)
                        need(pe, hidden_ready, n - 1 if u == 0 else n)
                        pe.matmul(bank_w[:, :], spread[:, cols], parts_t[:, h, :], start=True, stop=True).then_inc(w_out, 1)
                    if u >= 2:
                        second(i, h, u - 2)
                    elif not (isinstance(i, int) and i == 0):
                        second(i - 1, 1 - h, UNITS - 2 + u)

                def end(i, h, u):
                    if isinstance(i, int) and i == TILES - 1 and u < 2:
                        second(i, h, UNITS - 2 + u)
                    if u == 4:
                        pe.wait_ge(y_ready, i + 1)
                        if isinstance(i, int) and i >= TILES - 2:
                            if i == TILES - 2:
                                pe.wait_ge(partst_ready, TILES)
                            else:
                                pe.wait_ge(out_ready, TILES - 1)
                        else:
                            pe.wait_ge(xlo_ready, i + 3)
                        for s in range(SUB):
                            mm = pe.transpose(bank_x[:, s * P:(s + 1) * P], y_sb[:, s * P:(s + 1) * P], ident)
                        mm.then_inc(yt_out, 1)

                pe.wait_ge(set_up, 2)
                pe.wait_ge(split_hi, 4)
                pe.wait_ge(split_lo, 4)
                schedule(pe, ahead, unit, end)

            @block.vector
            def _(dve):
                def ahead(i, h, u):
                    def put(instruction):
                        instruction.then_inc(routing, 1)

                    def after(n):
                        dve.wait_ge(routing, ROUTING * i + n)

                    def each(ap):
                        return ap.unsqueeze(2).broadcast_to([P, SUB, E2])

                    if u == 0:
                        need(dve, var_ready, i)
                        for s in range(SUB):
                            st = dve.bn_stats(stats[:, s, :], x_tok[:, SUB * i + s, :])
                        st.then_inc(stats_ready, 1)
                        dve.wait_ge(stats_ready, i + 1)
                        need(dve, shift_ready, i)
                        dve.sem_inc(go, 1)
                        for s in range(SUB):
                            ag = dve.bn_aggr(moments[:, s, :], stats[:, s, :])
                        ag.then_inc(moments_ready, 1)
                    if u == 1:
                        dve.wait_ge(rstd_ready, i + 1)
                        need(dve, xn_ready, i)
                        dve.scalar_tensor_tensor(shift[:, :], moments[:, :, 0], -1.0, rstd[:, :],
                                                 ALU.mult, ALU.mult).then_inc(shift_ready, 1)
                    if u == 4:
                        dve.wait_ge(xhi_ready, i + 1)
                        need(dve, h3_out, UNITS * (i - 1))
                        dve.tensor_tensor(x_lo[:, h, :], bank_x[:, :], x_hi[:, h, :].bitcast(F32), ALU.subtract).then_inc(xlo_ready, 1)
                    if u == 6:
                        dve.wait_ge(logits_out, i + 1)
                        need(dve, exps_ready, i)
                        dve.tensor_reduce(minus_max[:, :], bank_x[:, 0:SUB * E2].rearrange("p (s e) -> p s e", s=SUB),
                                          AXIS.X, ALU.max, negate=True).then_inc(routing, 1)
                    if u == 7:
                        dve.wait_ge(exps_ready, i + 1)
                        put(dve.tensor_reduce(total[:, :], exps[:, :, :], AXIS.X, ALU.add))
                        after(2)
                        put(dve.reciprocal(inverse[:, :], total[:, :]))
                        after(3)
                        put(dve.tensor_tensor(scores[:, :, :], exps[:, :, :], each(inverse[:, :]), ALU.mult))
                        after(4)
                        dve.sem_inc(go, 1)
                        for s in range(SUB):
                            mx = dve.max(top[:, s, :], scores[:, s, :])
                        put(mx)
                    if u == 8:
                        fourth = each(top[:, :, TOP_K - 1])
                        after(5)
                        put(dve.tensor_tensor(above[:, :, :], scores[:, :, :], fourth, ALU.is_gt))
                        put(dve.tensor_tensor(equal[:, :, :], scores[:, :, :], fourth, ALU.is_equal))
                        after(7)
                        put(dve.tensor_reduce(n_above[:, :], above[:, :, :], AXIS.X, ALU.add))
                        put(dve.tensor_tensor_scan(nth_equal[:, :, :].rearrange("p s e -> p (s e)"), w("segment"),
                                                   equal[:, :, :].rearrange("p s e -> p (s e)"), 0.0, ALU.mult, ALU.add))
                        after(9)
                        put(dve.tensor_scalar(room[:, :], n_above[:, :], -1.0, float(TOP_K), ALU.mult, ALU.add))
                    if u == 9:
                        after(10)
                        put(dve.tensor_tensor(fits[:, :, :], nth_equal[:, :, :], each(room[:, :]), ALU.is_le))
                        after(11)
                        put(dve.tensor_tensor(taken[:, :, :], fits[:, :, :], equal[:, :, :], ALU.mult))
                        after(12)
                        put(dve.tensor_tensor(mask[:, :, :], taken[:, :, :], above[:, :, :], ALU.add))
                        after(13)
                        need(dve, rank_out, i)
                        dve.tensor_copy(mask_b[:, :, :], mask[:, :, :]).then_inc(mask_ready, 1)
                        put(dve.tensor_tensor(masked[:, :, :], mask[:, :, :], scores[:, :, :], ALU.mult))
                    if u == 12:
                        dve.wait_ge(rank_out, i + 1)
                        dve.tensor_tensor(rank[:, :, :], bank_x[:, 0:SUB * E2].rearrange("p (s e) -> p s e", s=SUB),
                                          used[:, :].unsqueeze(1).broadcast_to([P, SUB, E2]), ALU.add).then_inc(ranking, 1)
                        dve.wait_ge(ranking, 4 * i + 1)
                        after(14)
                        dve.tensor_tensor(used[:, :], used[:, :], bank_x[:, SUB * E2:(SUB + 1) * E2], ALU.add).then_inc(ranking, 1)
                        dve.scalar_tensor_tensor(weight[:, :, :], rank[:, :, :], float(CAPACITY), masked[:, :, :],
                                                 ALU.is_lt, ALU.mult).then_inc(ranking, 1)
                    if u == 13:
                        dve.wait_ge(ranking, 4 * i + 3)
                        need(dve, parts_out, i)
                        dve.tensor_copy(parts[:, :, 0:E2].bitcast(F32R), weight[:, :, :]).then_inc(ranking, 1)
                        dve.wait_ge(ranking, 4 * i + 4)
                        dve.tensor_tensor(parts[:, :, E2:2 * E2], weight[:, :, :], parts[:, :, 0:E2],
                                          ALU.subtract).then_inc(parts_ready, 1)

                def unit(i, h, u):
                    n, r = UNITS * i + u, (h + u) % 2
                    dve.wait_ge(silu_ready, n + 1)
                    dve.wait_ge(h3_out, n + 1)
                    if u < PAIRS:
                        need(dve, hidden_ready, n - 1)
                        dve.tensor_tensor(product[:, r, :], silu[:, r, :], bank_3[r][:, :], ALU.mult).then_inc(product_ready, 1)
                        dve.wait_ge(product_ready, n + 1)
                        dve.wait_ge(w_out, PAIRS * i + u + 1)
                        need(dve, hi_ready, n - 1)
                        need(dve, lo_ready, n - 1)
                        dve.tensor_tensor(hidden[:, r, :], product[:, r, :], bank_w[:, :], ALU.mult).then_inc(hidden_ready, 1)
                    else:
                        need(dve, hi_ready, n - 1)
                        need(dve, lo_ready, n - 1)
                        dve.tensor_tensor(hidden[:, r, :], silu[:, r, :], bank_3[r][:, :], ALU.mult).then_inc(product_ready, 1)
                        dve.wait_ge(product_ready, n + 1)
                        dve.sem_inc(hidden_ready, 1)

                def end(i, h, u):
                    if u == 5:
                        dve.wait_ge(yt_out, i + 1)
                        if not isinstance(i, int) or i >= 2:
                            dve.wait_ge(stored[h], 16 * (i // 2) if isinstance(i, int) else 8 * i - 8 * h)
                        dve.tensor_tensor(out_sb[h][:, :, :], x_tok[:, bass.ds(SUB * i, SUB), :],
                                          bank_x[:, :].rearrange("p (s c) -> p s c", s=SUB), ALU.add).then_inc(out_ready, 1)

                dve.memset(eps[:, :], LN_EPS)
                dve.memset(half[:, :], -0.5)
                dve.memset(used[:, :], 0.0)
                dve.memset(parts[:, :, :], 0.0).then_inc(set_up, 1)
                dve.wait_ge(loaded[3], 16)
                dve.tensor_copy(strict[:, :], w("strict"))
                dve.tensor_copy(ones[:, :], w("ones"))
                dve.tensor_copy(spread[:, :], w("spread")).then_inc(set_up, 1)
                dve.wait_ge(split_hi, 1)
                dve.tensor_tensor(wg_lo[:, :], w("wg"), wg_hi[:, :].bitcast(F32), ALU.subtract).then_inc(split_lo, 1)
                for n in range(3):
                    dve.wait_ge(split_hi, n + 2)
                    dve.tensor_tensor(lo[n][:, :], raw[n][:, :], hi[n][:, :].bitcast(F32), ALU.subtract).then_inc(split_lo, 1)
                dve.wait_ge(set_up, 2)
                schedule(dve, ahead, unit, end)

            @block.scalar
            def _(act):
                def ahead(i, h, u):
                    if u == 2:
                        act.wait_ge(shift_ready, i + 1)
                        need(act, xt_out, i)
                        for s in range(SUB):
                            a = act.activation(xn[:, s, :], x_tok[:, SUB * i + s, :], ACT.Identity,
                                               bias=shift[:, s:s + 1], scale=rstd[:, s:s + 1])
                        a.then_inc(xn_ready, 1)
                    if u == 3:
                        act.wait_ge(xt_out, i + 1)
                        need(act, h3_out, UNITS * (i - 1))
                        act.activation(x_hi[:, h, :], bank_x[:, :], ACT.Copy).then_inc(xhi_ready, 1)
                    if u == 6:
                        act.wait_ge(routing, ROUTING * i + 1)
                        need(act, routing, ROUTING * (i - 1) + 4)
                        for s in range(SUB):
                            a = act.activation(exps[:, s, :], bank_x[:, s * E2:(s + 1) * E2], ACT.Exp, bias=minus_max[:, s:s + 1])
                        a.then_inc(exps_ready, 1)
                    if u == 14:
                        act.wait_ge(parts_out, i + 1)
                        need(act, w_out, PAIRS * (i - 1))
                        act.activation(parts_t[:, h, :], bank_x[:, :], ACT.Copy).then_inc(partst_ready, 1)

                def unit(i, h, u):
                    n, r = UNITS * i + u, (h + u) % 2
                    act.wait_ge(h1_out, n + 1)
                    need(act, product_ready, n - 1)
                    act.activation(silu[:, r, :], bank_1[r][:, :], ACT.Silu).then_inc(silu_ready, 1)
                    if u >= 1:
                        split(n - 1, 1 - r)
                    elif not (isinstance(i, int) and i == 0):
                        split(n - 1, 1 - r)

                def split(n, r):
                    act.wait_ge(hidden_ready, n + 1)
                    need(act, unit_out, n - 1)
                    act.activation(hid_hi[:, r, :], hidden[:, r, :], ACT.Copy).then_inc(hi_ready, 1)

                def end(i, h, u):
                    if isinstance(i, int) and i == TILES - 1 and u == 0:
                        split(UNITS * TILES - 1, (1 + UNITS - 1) % 2)
                    if u == 3:
                        act.wait_ge(unit_out, UNITS * (i + 1))
                        need(act, yt_out, i)
                        act.activation(y_sb[:, :], bank_y[h][:, :], ACT.Copy).then_inc(y_ready, 1)

                act.wait_ge(loaded[3], 16)
                act.activation(wg_hi[:, :], w("wg"), ACT.Copy).then_inc(split_hi, 1)
                for n in range(3):
                    act.wait_ge(loaded[n], 16)
                    act.activation(hi[n][:, :], raw[n][:, :], ACT.Copy).then_inc(split_hi, 1)
                schedule(act, ahead, unit, end)

            @block.gpsimd
            def _(pool):
                def ahead(i, h, u):
                    if u == 0:
                        pool.wait_ge(moments_ready, i + 1)
                        pool.tensor_tensor(var_eps[:, :], moments[:, :, 1], eps[:, :], ALU.add).then_inc(var_ready, 1)
                        pool.wait_ge(var_ready, i + 1)
                        need(pool, xn_ready, i)
                        pool.tensor_tensor(rstd[:, :], var_eps[:, :], half[:, :], ALU.pow).then_inc(rstd_ready, 1)

                def unit(i, h, u):
                    n, r = UNITS * i + u, (h + u) % 2
                    pool.wait_ge(hi_ready, n + 1)
                    need(pool, unit_out, n - 1)
                    pool.tensor_tensor(hid_lo[:, r, :], hidden[:, r, :], hid_hi[:, r, :].bitcast(F32), ALU.subtract).then_inc(lo_ready, 1)

                def end(i, h, u):
                    pass

                pool.wait_ge(set_up, 1)
                schedule(pool, ahead, unit, end)


def build(nc, x_in, out, a_in, c_in, b_in, w1_in, w2_in, b1_in, b2_in, q_in, d_in, d1_in, d3_in, d2_in):
    by_group = "b (g p) c -> p (b g) c"
    with ExitStack() as ctx:
        x_tok = ctx.enter_context(nc.sbuf_tensor("x_tok", [P, GROUPS, P], F32))
        consts = ctx.enter_context(nc.sbuf_tensor("shape_consts", [P, C_WIDTH], F32))
        with nc.cleanup_on_exit():
            time_mixing(nc, x_tok, consts, x_in.rearrange(by_group, p=P), a_in, c_in)
        with nc.cleanup_on_exit():
            top1_experts(nc, x_tok, consts, b_in, w1_in, w2_in, b1_in, b2_in)
        with nc.cleanup_on_exit():
            quaternion_memory(nc, x_tok, consts, q_in)
        with nc.cleanup_on_exit():
            top4_experts(nc, x_tok, consts, out.rearrange(by_group, p=P), d_in, d1_in, d3_in, d2_in)



def packed_time_mixing(t):
    w = np.zeros((P, A_WIDTH), np.float32)
    part = {name: w[:, a:b] for name, (a, b) in A_AT.items()}
    part["mix1"][:, 0:MIXES * E_MIX] = t["maa_w1"]
    for f in range(MIXES):
        first = E_MIX * f % P
        part["mix2"][first:first + E_MIX, f * P:(f + 1) * P] = t["maa_w2"][f]
    part["td1"][:, 0:P // 2] = t["td_w1"]
    part["td2"][0:P // 2] = t["td_w2"]
    part["wr"][:] = t["Wr"].T
    part["wk"][:] = t["Wk"].T
    part["wv"][:] = t["Wv"][Y_ORDER].T
    part["wg"][:] = t["Wg"][Y_ORDER].T
    part["wo"][:] = t["Wo"].T[Y_ORDER]
    for n, name in enumerate("xwkvrg"):
        part["maa"][:, n] = t["time_maa_" + name].reshape(P)
    part["decay"][:, 0] = t["time_decay"].reshape(P)
    part["u"][:, 0] = t["u"].reshape(P)
    part["gain"][:, 0] = t["ln_g"][Y_ORDER]
    part["shift"][:, 0] = t["ln_b"][Y_ORDER]
    return w


def packed_router(t):
    w, part = shape_constants_b()
    part["bias_r"][:] = t["br"][None]
    part["wr"][:] = t["Wr"].T
    return w


def packed_quaternions(t):
    w, part = shape_constants_c()
    for m in range(QC):
        other = [c ^ m for c in range(P)]
        part["wk"][:, m * P:(m + 1) * P] = t["Wk"].T[:, other]
        part["bk"][:, m * P:(m + 1) * P] = t["bk"][other][None]
    part["wv"][:] = t["Wv"].T
    part["bv"][:] = t["bv"][None]
    part["wo"][:] = t["Wo"].T
    part["bo"][:] = t["bo"][None]
    part["gain"][:, 0] = t["ln_g"]
    part["shift"][:, 0] = t["ln_b"]
    return w


def packed_gate(t):
    w, part = shape_constants_d()
    part["wg"][:] = t["Wg"]
    return w


def kernel(**inputs):
    import concourse.bacc as bacc
    from concourse.bass_utils import run_bass_kernel_spmd

    given = {name: np.asarray(a) for name, a in inputs.items()}

    def under(prefix):
        return {name[len(prefix):]: a for name, a in given.items() if name.startswith(prefix)}

    mixing, ffn, memory, moe = under("L0_attn_"), under("L0_ffn_"), under("L1_attn_"), under("L1_ffn_")
    arrays = {
        "in_x": mixing["x"],
        "in_mixing": packed_time_mixing(mixing),
        "in_consts": shape_constants(),
        "in_router": packed_router(ffn),
        "in_w1": ffn["W1"].transpose(2, 0, 1).reshape(P, EXPERTS * D_FF),
        "in_w2": ffn["W2"].reshape(EXPERTS, P, FF_CHUNKS, P).transpose(3, 0, 2, 1).reshape(P, EXPERTS * D_FF),
        "in_b1": ffn["b1"].reshape(1, EXPERTS * D_FF),
        "in_b2": ffn["b2"].reshape(1, EXPERTS * P),
        "in_memory": packed_quaternions(memory),
        "in_gate": packed_gate(moe),
        "in_moe1": np.concatenate([moe["W1"].transpose(1, 0, 2).reshape(P, PAIRS * P), moe["Ws1"]], axis=1),
        "in_moe3": np.concatenate([moe["W3"].transpose(1, 0, 2).reshape(P, PAIRS * P), moe["Ws3"]], axis=1),
        "in_moe2": np.concatenate([moe["W2"].reshape(PAIRS, P, P).transpose(1, 0, 2).reshape(P, PAIRS * P), moe["Ws2"]], axis=1),
    }
    arrays = {name: np.ascontiguousarray(a) for name, a in arrays.items()}
    nc = bacc.Bacc("TRN2", target_bir_lowering=False, num_devices=1)
    aps = [nc.dram_tensor(name, a.shape, mybir.dt.from_np(a.dtype), kind="ExternalInput").ap() for name, a in arrays.items()]
    out = nc.dram_tensor("out", [BATCH, SEQ, P], F32, kind="ExternalOutput").ap()
    build(nc, aps[0], out, *aps[1:])
    r = run_bass_kernel_spmd(nc, [arrays], core_ids=[0])
    return r.results[0]["out"]
```

```python
from contextlib import ExitStack

import numpy as np

import concourse.bass as bass
from concourse import mybir

ALU = mybir.AluOpType
ACT = mybir.ActivationFunctionType
AXIS = mybir.AxisListType
F32 = mybir.dt.float32
F32R = mybir.dt.float32r
BF16 = mybir.dt.bfloat16
I32 = mybir.dt.int32
U32 = mybir.dt.uint32

P = 128
BATCH, SEQ = 4, 1024
TOKENS = BATCH * SEQ
SUB = 4
TILE = SUB * P
TILES = TOKENS // TILE
GROUPS = TOKENS // P
PER_SEQ = SEQ // TILE
LN_EPS = 1e-5

HEADS, HK = 16, 8
MIXES, E_MIX = 5, 32
GN_EPS = 1e-5 * 8 ** 2

A_PARTS = [("mix1", 2 * P), ("mix2", MIXES * P), ("td1", P), ("td2", P), ("wr", P), ("wk", P),
           ("wv", P), ("wg", P), ("wo", P), ("maa", 6), ("decay", 1), ("u", 1), ("gain", 1), ("shift", 1)]
C_PARTS = [("ident", P), ("spread", HK * P), ("gather", 2 * 32), ("heads", P), ("centre", P), ("mean", HEADS)]


def offsets(parts):
    at, n = {}, 0
    for name, width in parts:
        at[name] = (n, n + width)
        n += width
    return at, n


A_AT, A_WIDTH = offsets(A_PARTS)
C_AT, C_WIDTH = offsets(C_PARTS)

Y_ORDER = [HK * (p % HEADS) + 4 * (p // HEADS % 2) + p // 32 for p in range(P)]


def shape_constants():
    c = np.zeros((P, C_WIDTH), np.float32)
    part = {name: c[:, a:b] for name, (a, b) in C_AT.items()}
    part["ident"][:] = np.eye(P)
    for p, channel in enumerate(Y_ORDER):
        head, j = divmod(channel, HK)
        part["spread"][p, j * P + head * HK:j * P + (head + 1) * HK] = 1
    for k in range(P):
        for a in range(2):
            part["gather"][k, a * 32 + a * HEADS + k // HK] = 1
        part["heads"][k, k // HK::HEADS] = 1
    same = np.equal.outer(np.arange(P) % HEADS, np.arange(P) % HEADS)
    part["centre"][:] = np.eye(P) - same / HK
    part["mean"][:] = np.equal.outer(np.arange(P) % HEADS, np.arange(HEADS)) / HK
    return c


def need(engine, semaphore, value):
    if not isinstance(value, int) or value > 0:
        engine.wait_ge(semaphore, value)


def time_mixing(nc, x_tok, consts, x_in, w_in, c_in, early):
    with ExitStack() as ctx:
        def sb(name, shape, dt=F32):
            return ctx.enter_context(nc.sbuf_tensor("a_" + name, shape, dt))

        def bank(name):
            return ctx.enter_context(nc.psum_tensor("a_" + name, [P, TILE], F32))

        def sem(name):
            return nc.alloc_semaphore("a_" + name)

        weights = sb("weights", [P, A_WIDTH])
        spread = sb("spread", [P, HK * P], F32R)
        half = sb("minus_half", [P, SUB])
        eps = sb("eps", [P, SUB])
        eps_gn = sb("eps_gn", [P, 1])

        def w(name):
            return weights[:, A_AT[name][0]:A_AT[name][1]]

        def const(name):
            return consts[:, C_AT[name][0]:C_AT[name][1]]

        ident = const("ident")
        maa = w("maa")
        mean = const("mean")

        stats = sb("stats", [P, SUB, 6])
        moments = sb("moments", [P, SUB, 2])
        var_eps = sb("var_eps", [P, SUB])
        rstd = sb("rstd", [P, SUB])
        shift = sb("shift", [P, SUB])
        xn = sb("xn", [P, SUB, P])
        xt = [sb(f"xt{h}", [P, TILE + 1]) for h in range(2)]
        dx = sb("dx", [P, TILE])
        xa = sb("xa", [P, TILE])
        m1 = sb("m1", [P, 2, TILE])
        lerp = sb("lerp", [P, 2, TILE])
        xf = sb("xf", [P, MIXES, TILE])
        td_hidden = sb("td_hidden", [P, TILE])
        rate = sb("rate", [P, TILE])
        decay = sb("decay", [P, 2, TILE])
        kk = sb("k", [P, 2, TILE])
        rr = sb("r", [P, 2, TILE])
        vv = sb("v", [P, TILE])
        v_hi = sb("v_hi", [P, 2, TILE], F32R)
        v_lo = sb("v_lo", [P, 2, TILE], F32R)
        g_tanh = sb("g_tanh", [P, TILE])
        gate = sb("gate", [P, 2, TILE])
        rku = sb("rku", [P, TILE])
        bonus_v = sb("bonus_v", [P, 2, TILE])
        kv = sb("kv", [P, 2, TILE])
        state = sb("state", [P, HK, SEQ + 1])
        rs = sb("rs", [P, HK, TILE])
        y_sum = sb("y_sum", [P, TILE])
        yc = sb("yc", [P, TILE])
        yc2 = sb("yc2", [P, TILE])
        spread_y = sb("std_y", [P, SUB, HEADS])
        rstd_y = sb("rstd_y", [P, SUB, HEADS])
        rstd_wide = sb("rstd_wide", [P, TILE])
        yn = sb("yn", [P, TILE])
        yl = sb("yl", [P, TILE])
        z = sb("z", [P, TILE])

        front = [bank(f"front{n}") for n in range(3)]
        vb = [bank(f"vb{n}") for n in range(2)]
        y_bank = bank("y")
        tail0, tail1 = bank("tail0"), bank("tail1")

        XT, M1A, M1B, MIX, TD1, K, TD2, V, R, G, BONUS = 0, 1, 2, 3, 8, 9, 10, 11, 12, 13, 14
        USES = 14
        STEPS = 2 * HK
        PRODUCT_STEPS = (1, 3, 5, 8, 11, 12, 14, 15)

        x_first, x_rest, w_loaded, c_loaded = sem("x_first"), sem("x_rest"), sem("w_loaded"), sem("c_loaded")
        early_loaded = sem("early_loaded")
        zeroed, eps_set = sem("zeroed"), sem("eps_set")
        spread_ready = sem("spread_ready")
        go = sem("go")
        stats_ready, moments_ready, var_ready = sem("stats_ready"), sem("moments_ready"), sem("var_ready")
        rstd_ready, shift_ready, xn_ready = sem("rstd_ready"), sem("shift_ready"), sem("xn_ready")
        xt_out = sem("xt_out")
        front_out = sem("front_out")
        xt_ready, dx_ready, xa_ready = sem("xt_ready"), sem("dx_ready"), sem("xa_ready")
        m1_ready = sem("m1_ready")
        lerp_ready, xf_ready = sem("lerp_ready"), sem("xf_ready")
        td_ready, k_ready, rate_ready, decay_ready = sem("td_ready"), sem("k_ready"), sem("rate_ready"), sem("decay_ready")
        v_ready, vhi_ready, vlo_ready, r_ready = sem("v_ready"), sem("vhi_ready"), sem("vlo_ready"), sem("r_ready")
        gtanh_ready, gate_ready, rku_ready, bonus_ready = sem("gtanh_ready"), sem("gate_ready"), sem("rku_ready"), sem("bonus_ready")
        vb_out, kv_ready, scan_ready, rs_ready = sem("vb_out"), sem("kv_ready"), sem("scan_ready"), sem("rs_ready")
        y_out = sem("y_out")
        ysum_ready, centred, yc_ready, yc2_ready = sem("ysum_ready"), sem("centred"), sem("yc_ready"), sem("yc2_ready")
        wide_ready = sem("wide_ready")
        var_out, std_ready, rstdy_ready, rstdy_out = sem("var_out"), sem("std_ready"), sem("rstdy_ready"), sem("rstdy_out")
        yn_ready, yl_ready, z_ready, wo_out, x_ready = sem("yn_ready"), sem("yl_ready"), sem("z_ready"), sem("wo_out"), sem("x_ready")

        def groups(i):
            return slice(SUB * i, SUB * i + SUB) if isinstance(i, int) else bass.ds(SUB * i, SUB)

        def seq_cols(h, first):
            return slice(TILE * h + first, TILE * h + first + TILE)

        def pipeline(engine, scan, norm, ahead, tail):
            def steps(i, h):
                for step in range(STEPS):
                    scan(i, h, step)
                    if not isinstance(i, int) or i > 0:
                        tail(i - 1, 1 - h, step)
                    if not isinstance(i, int) or i + 1 < TILES:
                        ahead(i + 1, 1 - h, step)
                    if not isinstance(i, int) or i + 2 < TILES:
                        norm(i + 2, h, step)

            for step in range(STEPS):
                norm(0, 0, step)
            for step in range(STEPS):
                ahead(0, 0, step)
                norm(1, 1, step)
            steps(0, 0)
            steps(1, 1)
            with engine.Fori(1, TILES // 2 - 1) as b:
                steps(2 * b, 0)
                steps(2 * b + 1, 1)
            steps(TILES - 2, 0)
            steps(TILES - 1, 1)
            for step in range(STEPS):
                tail(TILES - 1, 1, step)

        with nc.Block() as block:
            @block.sync
            def _(sp):
                sp.dma_start(x_tok[:, 0:SUB, :], x_in[:, 0:SUB, :]).then_inc(x_first, 16)
                sp.dma_start(consts[:, :], c_in).then_inc(c_loaded, 16)
                sp.dma_start(weights[:, :], w_in).then_inc(w_loaded, 16)
                sp.dma_start(x_tok[:, SUB:, :], x_in[:, SUB:, :]).then_inc(x_rest, 16)
                for tensor, source in early:
                    sp.dma_start(tensor[:, :], source).then_inc(early_loaded, 16)
                sp.wait_ge(early_loaded, 16 * len(early))

            @block.tensor
            def _(pe):
                def project(i, n, name, operand):
                    pe.matmul(front[n % 3][:, :], w(name), operand, start=True, stop=True).then_inc(front_out, 1)

                def norm(i, h, step):
                    if step == 14:
                        pe.wait_ge(xn_ready, i + 1)
                        need(pe, r_ready, i)
                        for s in range(SUB):
                            mm = pe.transpose(front[0][:, s * P:(s + 1) * P], xn[:, s, :], ident)
                        mm.then_inc(xt_out, 1)

                def ahead(i, h, step):
                    if step == 2:
                        pe.wait_ge(xa_ready, i + 1)
                        if isinstance(i, int) and i == 0:
                            pe.wait_ge(w_loaded, 16)
                        need(pe, gate_ready, i)
                        pe.matmul(front[1][:, :], w("mix1")[:, 0:P], xa[:, :], start=True, stop=True).then_inc(front_out, 1)
                    if step == 3:
                        need(pe, bonus_ready, i)
                        pe.matmul(front[2][:, :], w("mix1")[:, P:2 * P], xa[:, :], start=True, stop=True).then_inc(front_out, 1)
                    if 4 <= step < 4 + MIXES:
                        f = step - 4
                        n = MIX + f
                        if f == 0:
                            pe.wait_ge(m1_ready, 2 * i + 1)
                        elif f < 3:
                            pe.wait_ge(m1_ready, 2 * i + f)
                        else:
                            pe.wait_ge(lerp_ready, MIXES * i + f - 2)
                        if f == 4:
                            pe.wait_ge(m1_ready, 2 * i + 2)
                        operand = m1[:, 0, :] if f < 4 else m1[:, 1, :]
                        pe.matmul(front[n % 3][:, :], w("mix2")[:, f * P:(f + 1) * P], operand,
                                  start=True, stop=True).then_inc(front_out, 1)
                    if step == 8:
                        pe.wait_ge(xf_ready, MIXES * i + 1)
                        pe.wait_ge(lerp_ready, MIXES * i + 3)
                        project(i, TD1, "td1", xf[:, 0, :])
                    if step == 9:
                        pe.wait_ge(xf_ready, MIXES * i + 2)
                        pe.wait_ge(lerp_ready, MIXES * i + 4)
                        project(i, K, "wk", xf[:, 1, :])
                    if step == 11:
                        pe.wait_ge(td_ready, i + 1)
                        pe.wait_ge(lerp_ready, MIXES * i + 5)
                        project(i, TD2, "td2", td_hidden[:, :])
                    if step == 11:
                        pe.wait_ge(xf_ready, MIXES * i + 3)
                        project(i, V, "wv", xf[:, 2, :])
                    if step == 12:
                        pe.wait_ge(xf_ready, MIXES * i + 4)
                        pe.wait_ge(k_ready, i + 1)
                        project(i, R, "wr", xf[:, 3, :])
                    if step == 13:
                        pe.wait_ge(xf_ready, MIXES * i + 5)
                        pe.wait_ge(rate_ready, i + 1)
                        project(i, G, "wg", xf[:, 4, :])
                    if step == 15:
                        pe.wait_ge(rku_ready, i + 1)
                        pe.wait_ge(vhi_ready, i + 1)
                        pe.matmul(front[2][:, :], const("heads"), rku[:, :], start=True, stop=True).then_inc(front_out, 1)
                        spread_v(i, h, 0)
                        spread_v(i, h, 1)

                def spread_v(i, h, j):
                    if j == 0:
                        pe.wait_ge(vhi_ready, i + 1)
                        pe.wait_ge(vlo_ready, i + 1)
                        if isinstance(i, int) and i == 0:
                            pe.wait_ge(spread_ready, 1)
                    need(pe, kv_ready, HK * i + j - 1)
                    row = spread[:, j * P:(j + 1) * P]
                    pe.matmul(vb[j % 2][:, :], row, v_hi[:, h, :], start=True, stop=False)
                    pe.matmul(vb[j % 2][:, :], row, v_lo[:, h, :], start=False, stop=True).then_inc(vb_out, 1)

                def sum_k(i, a):
                    pe.wait_ge(rs_ready, HK * i + 4 * a + 4)
                    if a == 0:
                        need(pe, ysum_ready, i)
                    for g in range(4):
                        mm = pe.matmul(y_bank[32 * g:32 * g + 32, :], const("gather")[:, 32 * a:32 * a + 32],
                                       rs[:, 4 * a + g, :], start=(a == 0), stop=(a == 1), tile_position=(0, 32 * g))
                    mm.then_inc(y_out, 1)

                def scan(i, h, step):
                    if step % 2 == 1 and 2 <= step // 2 + 2 < HK:
                        spread_v(i, h, step // 2 + 2)
                    if step == 11:
                        sum_k(i, 0)

                def tail(i, h, step):
                    if step == 2:
                        sum_k(i, 1)
                    if step == 4:
                        pe.wait_ge(ysum_ready, i + 1)
                        pe.matmul(tail0[:, :], const("centre"), y_sum[:, :], start=True, stop=True).then_inc(centred, 1)
                    if step == 6:
                        pe.wait_ge(yc2_ready, i + 1)
                        need(pe, x_ready, i)
                        for s in range(SUB):
                            mm = pe.matmul(tail1[:, s * HEADS:(s + 1) * HEADS], yc2[:, s * P:(s + 1) * P], mean,
                                           start=True, stop=True)
                        mm.then_inc(var_out, 1)
                    if step == 10:
                        pe.wait_ge(wide_ready, i + 1)
                        for s in range(SUB):
                            mm = pe.transpose(tail0[:, s * P:(s + 1) * P], rstd_wide[:, s * P:(s + 1) * P], ident)
                        mm.then_inc(rstdy_out, 1)
                    if step == 14:
                        pe.wait_ge(z_ready, i + 1)
                        for s in range(SUB):
                            mm = pe.matmul(tail1[:, s * P:(s + 1) * P], z[:, s * P:(s + 1) * P], w("wo"),
                                           start=True, stop=True)
                        mm.then_inc(wo_out, 1)

                pe.wait_ge(c_loaded, 16)
                pipeline(pe, scan, norm, ahead, tail)

            @block.vector
            def _(dve):
                def norm(i, h, step):
                    if step == 2:
                        if isinstance(i, int) and i < 2:
                            dve.wait_ge(x_rest if i else x_first, 16)
                        need(dve, rstd_ready, i)
                        for s in range(SUB):
                            group = x_tok[:, SUB * i + s, :]
                            st = dve.bn_stats(stats[:, s, :], group)
                        st.then_inc(stats_ready, 1)
                    if step == 3:
                        dve.wait_ge(stats_ready, i + 1)
                        need(dve, shift_ready, i)
                        dve.sem_inc(go, 1)
                        for s in range(SUB):
                            ag = dve.bn_aggr(moments[:, s, :], stats[:, s, :])
                        ag.then_inc(moments_ready, 1)
                    if step == 6:
                        dve.wait_ge(rstd_ready, i + 1)
                        need(dve, xn_ready, i)
                        dve.scalar_tensor_tensor(shift[:, :], moments[:, :, 0], -1.0, rstd[:, :],
                                                 ALU.mult, ALU.mult).then_inc(shift_ready, 1)

                def ahead(i, h, step):
                    here = xt[h]
                    if step == 0:
                        dve.wait_ge(xt_ready, i + 1)
                        if isinstance(i, int) and i == 0:
                            dve.wait_ge(w_loaded, 16)
                            dve.wait_ge(c_loaded, 16)
                        need(dve, lerp_ready, MIXES * i)
                        dve.tensor_tensor(dx[:, :], here[:, 0:TILE], here[:, 1:TILE + 1], ALU.subtract).then_inc(dx_ready, 1)
                    if step == 1:
                        dve.wait_ge(dx_ready, i + 1)
                        need(dve, m1_ready, 2 * i)
                        dve.scalar_tensor_tensor(xa[:, :], dx[:, :], maa[:, 0:1], here[:, 1:TILE + 1],
                                                 ALU.mult, ALU.add).then_inc(xa_ready, 1)
                    if step == 2 and isinstance(i, int) and i == 0:
                        dve.tensor_copy(spread[:, :], const("spread")).then_inc(spread_ready, 1)
                    if 5 <= step < 5 + MIXES:
                        f = step - 5
                        dve.wait_ge(front_out, USES * i + MIX + f)
                        need(dve, xf_ready, MIXES * i + f - 1)
                        dve.scalar_tensor_tensor(lerp[:, (f + h) % 2, :], front[(MIX + f) % 3][:, :], maa[:, f + 1:f + 2],
                                                 dx[:, :], ALU.add, ALU.mult).then_inc(lerp_ready, 1)
                    if step == 13:
                        dve.wait_ge(vhi_ready, i + 1)
                        need(dve, vb_out, HK * (i - 1))
                        dve.tensor_tensor(v_lo[:, h, :], vv[:, :], v_hi[:, h, :].bitcast(F32), ALU.subtract).then_inc(vlo_ready, 1)
                    if step == 14:
                        dve.wait_ge(r_ready, i + 1)
                        need(dve, front_out, USES * i)
                        dve.scalar_tensor_tensor(rku[:, :], rr[:, h, :], w("u"), kk[:, h, :],
                                                 ALU.mult, ALU.mult).then_inc(rku_ready, 1)
                    if step == 15:
                        dve.wait_ge(gtanh_ready, i + 1)
                        need(dve, z_ready, i - 1)
                        dve.scalar_tensor_tensor(gate[:, h, :], g_tanh[:, :], 1.0, front[G % 3][:, :],
                                                 ALU.add, ALU.mult).then_inc(gate_ready, 1)

                def outer(i, h, j):
                    if j == 0:
                        dve.wait_ge(k_ready, i + 1)
                    dve.wait_ge(vb_out, HK * i + j + 1)
                    need(dve, scan_ready, HK * i + j - 1)
                    dve.tensor_tensor(kv[:, j % 2, :], kk[:, h, :], vb[j % 2][:, :], ALU.mult).then_inc(kv_ready, 1)

                def scan(i, h, step):
                    j = step // 2
                    if step == 0:
                        dve.wait_ge(decay_ready, i + 1)
                        outer(i, h, 0)
                    if step % 2 == 0:
                        if j < HK - 1:
                            outer(i, h, j + 1)
                    else:
                        dve.wait_ge(kv_ready, HK * i + j + 1)
                        need(dve, rs_ready, HK * (i - 1) + j + 1)
                        first = state[:, j, TILE * h:TILE * h + 1]
                        if h:
                            dve.wait_ge(scan_ready, HK * (i - 1) + j + 1)
                        dve.tensor_tensor_scan(state[:, j, seq_cols(h, 1)], decay[:, h, :], kv[:, j % 2, :], first,
                                               ALU.mult, ALU.add).then_inc(scan_ready, 1)
                    if step == 1:
                        dve.wait_ge(front_out, USES * (i + 1))
                        need(dve, ysum_ready, i - 1)
                        dve.tensor_tensor(bonus_v[:, h, :], vv[:, :], front[BONUS % 3][:, :], ALU.mult).then_inc(bonus_ready, 1)

                def tail(i, h, step):
                    if step == 3:
                        dve.wait_ge(y_out, 2 * i + 2)
                        dve.wait_ge(bonus_ready, i + 1)
                        need(dve, centred, i)
                        dve.tensor_tensor(y_sum[:, :], bonus_v[:, h, :], y_bank[:, :], ALU.add).then_inc(ysum_ready, 1)
                    if step == 8:
                        dve.wait_ge(std_ready, i + 1)
                        need(dve, wide_ready, i)
                        dve.reciprocal(rstd_y[:, :, :], spread_y[:, :, :]).then_inc(rstdy_ready, 1)
                    if step == 11:
                        dve.wait_ge(rstdy_out, i + 1)
                        dve.wait_ge(yc_ready, i + 1)
                        need(dve, yl_ready, i)
                        dve.tensor_tensor(yn[:, :], yc[:, :], tail0[:, :], ALU.mult).then_inc(yn_ready, 1)
                    if step == 13:
                        dve.wait_ge(yl_ready, i + 1)
                        dve.wait_ge(gate_ready, i + 1)
                        need(dve, wo_out, i)
                        dve.scalar_tensor_tensor(z[:, :], yl[:, :], 0.5, gate[:, h, :], ALU.mult, ALU.mult).then_inc(z_ready, 1)
                    if step == 15:
                        dve.wait_ge(wo_out, i + 1)
                        x = x_tok[:, groups(i), :]
                        dve.tensor_tensor(x, x, tail1[:, :].rearrange("p (s c) -> p s c", s=SUB), ALU.add).then_inc(x_ready, 1)

                dve.memset(xt[0][:, 0:1], 0.0)
                dve.memset(state[:, :, 0:1], 0.0)
                dve.memset(eps[:, :], LN_EPS)
                dve.memset(half[:, :], -0.5).then_inc(zeroed, 1)
                dve.wait_ge(zeroed, 1)
                pipeline(dve, scan, norm, ahead, tail)

            @block.scalar
            def _(act):
                def norm(i, h, step):
                    if step == 8:
                        act.wait_ge(shift_ready, i + 1)
                        need(act, xt_ready, i)
                        for s in range(SUB):
                            a = act.activation(xn[:, s, :], x_tok[:, SUB * i + s, :], ACT.Identity,
                                               bias=shift[:, s:s + 1], scale=rstd[:, s:s + 1])
                        a.then_inc(xn_ready, 1)
                    if step == 15:
                        act.wait_ge(xt_out, i + 1)
                        need(act, xf_ready, MIXES * (i - 1))
                        if h:
                            act.activation(xt[1][:, 0:1], xt[0][:, TILE:TILE + 1], ACT.Copy)
                        act.activation(xt[h][:, 1:TILE + 1], front[0][:, :], ACT.Copy).then_inc(xt_ready, 1)

                def ahead(i, h, step):
                    if step == 2:
                        act.wait_ge(front_out, USES * i + M1A)
                        need(act, lerp_ready, MIXES * i)
                        act.activation(m1[:, 0, :], front[M1A][:, :], ACT.Tanh).then_inc(m1_ready, 1)
                    if step == 4:
                        act.wait_ge(front_out, USES * i + M1B)
                        act.activation(m1[:, 1, :], front[M1B][:, :], ACT.Tanh).then_inc(m1_ready, 1)
                    if step == 9:
                        act.wait_ge(front_out, USES * i + TD1)
                        act.activation(td_hidden[:, :], front[TD1 % 3][:, :], ACT.Tanh).then_inc(td_ready, 1)
                    if step == 10:
                        act.wait_ge(front_out, USES * i + K)
                        need(act, kv_ready, HK * (i - 1))
                        need(act, rku_ready, i - 1)
                        act.activation(kk[:, h, :], front[K % 3][:, :], ACT.Copy).then_inc(k_ready, 1)
                    if step == 11:
                        act.wait_ge(front_out, USES * i + TD2)
                        if isinstance(i, int) and i == 0:
                            act.wait_ge(w_loaded, 16)
                        act.activation(rate[:, :], front[TD2 % 3][:, :], ACT.Exp, bias=w("decay")).then_inc(rate_ready, 1)
                    if step == 12:
                        act.wait_ge(front_out, USES * i + V)
                        need(act, bonus_ready, i)
                        act.activation(vv[:, :], front[V % 3][:, :], ACT.Copy).then_inc(v_ready, 1)
                        need(act, vb_out, HK * (i - 1))
                        act.activation(v_hi[:, h, :], front[V % 3][:, :], ACT.Copy).then_inc(vhi_ready, 1)
                    if step == 13:
                        act.wait_ge(front_out, USES * i + R)
                        need(act, rs_ready, HK * (i - 1))
                        act.activation(rr[:, h, :], front[R % 3][:, :], ACT.Copy).then_inc(r_ready, 1)
                        act.wait_ge(rate_ready, i + 1)
                        need(act, scan_ready, HK * (i - 1))
                        act.activation(decay[:, h, :], rate[:, :], ACT.Exp, scale=-1.0).then_inc(decay_ready, 1)
                    if step == 14:
                        act.wait_ge(front_out, USES * i + G)
                        need(act, gate_ready, i)
                        act.activation(g_tanh[:, :], front[G % 3][:, :], ACT.Tanh, scale=0.5).then_inc(gtanh_ready, 1)

                def scan(i, h, step):
                    pass

                def tail(i, h, step):
                    if step == 5:
                        act.wait_ge(centred, i + 1)
                        need(act, yn_ready, i)
                        act.activation(yc[:, :], tail0[:, :], ACT.Copy).then_inc(yc_ready, 1)
                        act.activation(yc2[:, :], tail0[:, :], ACT.Square).then_inc(yc2_ready, 1)
                    if step == 7:
                        act.wait_ge(var_out, i + 1)
                        need(act, rstdy_ready, i)
                        act.activation(spread_y[:, :, :], tail1[:, 0:SUB * HEADS].rearrange("p (s c) -> p s c", s=SUB),
                                       ACT.Sqrt, bias=eps_gn[:, 0:1]).then_inc(std_ready, 1)
                    if step == 9:
                        act.wait_ge(rstdy_ready, i + 1)
                        need(act, rstdy_out, i)
                        act.activation(rstd_wide[:, :].rearrange("p (s j c) -> p s j c", s=SUB, j=HK),
                                       rstd_y[:, :, :].unsqueeze(2).broadcast_to([P, SUB, HK, HEADS]),
                                       ACT.Copy).then_inc(wide_ready, 1)
                    if step == 12:
                        act.wait_ge(yn_ready, i + 1)
                        need(act, z_ready, i)
                        act.activation(yl[:, :], yn[:, :], ACT.Identity, bias=w("shift"), scale=w("gain")).then_inc(yl_ready, 1)

                act.wait_ge(eps_set, 1)
                act.activation(g_tanh[:, 0:1], eps_gn[:, :], ACT.Tanh)
                pipeline(act, scan, norm, ahead, tail)

            @block.gpsimd
            def _(pool):
                def norm(i, h, step):
                    if step == 4:
                        pool.wait_ge(moments_ready, i + 1)
                        pool.tensor_tensor(var_eps[:, :], moments[:, :, 1], eps[:, :], ALU.add).then_inc(var_ready, 1)
                        pool.wait_ge(var_ready, i + 1)
                        need(pool, xn_ready, i)
                        pool.tensor_tensor(rstd[:, :], var_eps[:, :], half[:, :], ALU.pow).then_inc(rstd_ready, 1)

                def ahead(i, h, step):
                    if 6 <= step < 6 + MIXES:
                        f = step - 6
                        pool.wait_ge(lerp_ready, MIXES * i + f + 1)
                        need(pool, front_out, USES * (i - 1) + (TD1, K, V, R, G)[f])
                        pool.tensor_tensor(xf[:, f, :], lerp[:, (f + h) % 2, :], xt[h][:, 1:TILE + 1], ALU.add).then_inc(xf_ready, 1)

                def scan(i, h, step):
                    if step not in PRODUCT_STEPS:
                        return
                    j = PRODUCT_STEPS.index(step)
                    if j == 0:
                        pool.wait_ge(r_ready, i + 1)
                    pool.wait_ge(scan_ready, HK * i + j + 1)
                    need(pool, y_out, 2 * (i - 1) + j // 4 + 1)
                    pool.tensor_tensor(rs[:, j, :], rr[:, h, :], state[:, j, seq_cols(h, 0)], ALU.mult).then_inc(rs_ready, 1)

                def tail(i, h, step):
                    pass

                pool.memset(eps_gn[:, :], GN_EPS).then_inc(eps_set, 1)
                pool.wait_ge(zeroed, 1)
                pipeline(pool, scan, norm, ahead, tail)

EXPERTS, D_FF = 8, 512
FF_CHUNKS = D_FF // P
ROW_TILES = (TOKENS + EXPERTS * (P - 1)) // P
FEWEST_TILES = TOKENS // P
SPARE_TILES = ROW_TILES - FEWEST_TILES
REGION = P + TOKENS
SPARE_ROWS = SPARE_TILES * P
ROWS = SPARE_ROWS + EXPERTS * REGION
ROW_WIDTH = P + 1
EMPTY_TILES = SPARE_TILES + EXPERTS

B_PARTS = [("strict", P), ("ones", P), ("rank", EXPERTS), ("region", EXPERTS), ("first_row", EXPERTS),
           ("tile_no", ROW_TILES), ("tile_end", ROW_TILES), ("token", GROUPS), ("empty", EMPTY_TILES),
           ("bias_r", EXPERTS), ("wr", EXPERTS)]
B_AT, B_WIDTH = offsets(B_PARTS)


def shape_constants_b():
    c = np.zeros((P, B_WIDTH), np.float32)
    part = {name: c[:, a:b] for name, (a, b) in B_AT.items()}
    part["strict"][:] = np.triu(np.ones((P, P)), 1)
    part["ones"][:] = 1
    part["rank"][:] = np.arange(EXPERTS, 0, -1)
    first_row = SPARE_ROWS + P + REGION * np.arange(EXPERTS)
    part["first_row"][:] = first_row
    part["region"][0] = first_row
    part["tile_no"][:] = np.arange(ROW_TILES)
    part["tile_end"][:] = P * (np.arange(ROW_TILES) + 1)
    part["token"][:] = np.arange(TOKENS).reshape(P, GROUPS)
    part["empty"][:] = TOKENS + np.arange(EMPTY_TILES * P).reshape(P, EMPTY_TILES)
    return c, part


def top1_experts(nc, x_tok, consts, cb, w1_in, w2_in, b1_in, b2_in, early):
    rows_in = nc.dram_tensor("rows_in", [ROWS, ROW_WIDTH], F32, kind="Internal").ap()
    results = nc.dram_tensor("results", [TOKENS + EMPTY_TILES * P, P], F32, kind="Internal").ap()
    with ExitStack() as ctx:
        def sb(name, shape, dt=F32):
            return ctx.enter_context(nc.sbuf_tensor("b_" + name, shape, dt))

        def bank(name):
            return ctx.enter_context(nc.psum_tensor("b_" + name, [P, TILE], F32))

        def sem(name):
            return nc.alloc_semaphore("b_" + name)

        def const(name):
            return cb[:, B_AT[name][0]:B_AT[name][1]]

        ident = consts[:, C_AT["ident"][0]:C_AT["ident"][1]]
        w1 = sb("w1", [P, EXPERTS * D_FF])
        w2 = sb("w2", [P, EXPERTS * D_FF])
        b1 = sb("b1", [P, EXPERTS * D_FF])
        b2 = sb("b2", [P, EXPERTS * P])
        eps = sb("eps", [P, 1])
        ones = sb("ones_row", [P, EXPERTS])
        empty_rows = sb("empty_rows", [P, EMPTY_TILES, ROW_WIDTH])

        stats = sb("stats", [P, SUB, 6])
        moments = sb("moments", [P, 2, SUB, 2])
        std = sb("std", [P, SUB])
        rstd = sb("rstd", [P, SUB])
        shift = sb("shift", [P, SUB])
        xn = sb("xn", [P, 2, SUB, P])
        rows = sb("rows", [P, GROUPS, ROW_WIDTH])
        xt = sb("xt", [P, 2, TILE])
        logits = sb("logits", [P, SUB, EXPERTS])
        best = sb("best", [P, SUB])
        is_best = sb("is_best", [P, SUB, EXPERTS])
        ranked = sb("ranked", [P, SUB, EXPERTS])
        top_rank = sb("top_rank", [P, SUB])
        chosen = sb("chosen", [P, 2, SUB, EXPERTS])
        here = sb("here", [P, EXPERTS])
        total = sb("total", [P, EXPERTS])
        own_place = sb("own_place", [P, SUB, EXPERTS])
        position = sb("position", [P, SUB])
        index = sb("index", [P, GROUPS], U32)

        count = sb("count", [P, EXPERTS])
        rounded = sb("rounded", [P, EXPERTS], I32)
        n_tiles_i = sb("n_tiles_i", [P, EXPERTS], I32)
        n_tiles = sb("n_tiles", [P, EXPERTS])
        end_tile = sb("end_tile", [P, EXPERTS])
        base = sb("base", [P, EXPERTS])
        top = sb("top", [P, EXPERTS + 1])
        climb = sb("climb", [P, EXPERTS])
        ended = sb("ended", [P, ROW_TILES, EXPERTS])
        climbed = sb("climbed", [P, ROW_TILES, EXPERTS])
        expert_f = sb("expert_f", [P, ROW_TILES])
        expert = sb("expert", [P, ROW_TILES], I32)
        start_f = sb("start_f", [P, ROW_TILES])
        start = sb("start", [P, ROW_TILES], I32)

        xin = sb("xin", [P, 4, ROW_WIDTH])
        result_row = sb("result_row", [P, 4], U32)
        y_row = sb("y_row", [P, 4, P])
        xin_t = sb("xin_t", [P, 2, P])
        hidden = sb("hidden", [P, 2, D_FF])
        hidden_t = sb("hidden_t", [P, 2, D_FF])
        back = sb("back", [P, GROUPS, P])

        bank_x = [bank(f"x{n}") for n in range(2)]
        bank_l = [bank(f"l{n}") for n in range(2)]
        bank_h = [bank(f"h{n}") for n in range(2)]
        bank_y = [bank(f"y{n}") for n in range(2)]

        early_loaded, w_loaded, empty_set, emptied = sem("early_loaded"), sem("w_loaded"), sem("empty_set"), sem("emptied")
        cleared, eps_set = sem("cleared"), sem("eps_set")
        go, send = sem("go"), sem("send")
        stats_ready, moments_ready, std_ready = sem("stats_ready"), sem("moments_ready"), sem("std_ready")
        rstd_ready, shift_ready, xn_ready = sem("rstd_ready"), sem("shift_ready"), sem("xn_ready")
        xt_out, xt_ready, logits_out, choice = sem("xt_out"), sem("xt_ready"), sem("logits_out"), sem("choice")
        chosen_ready, here_ready, total_ready = sem("chosen_ready"), sem("here_ready"), sem("total_ready")
        rank_out, own_ready, position_ready = sem("rank_out"), sem("own_ready"), sem("position_ready")
        index_ready, rows_ready = sem("index_ready"), sem("rows_ready")
        scattered = sem("scattered")
        total_out, planning, plan_ready = sem("total_out"), sem("planning"), sem("plan_ready")
        row_loaded = [sem(f"row_loaded{n}") for n in range(4)]
        row_stored = [sem(f"row_stored{n}") for n in range(4)]
        row_t_out, row_t_ready, h_out, h_ready = sem("row_t_out"), sem("row_t_ready"), sem("h_out"), sem("h_ready")
        result_row_ready = sem("result_row_ready")
        ht_out, ht_ready, y_out, y_ready = sem("ht_out"), sem("ht_ready"), sem("y_out"), sem("y_ready")
        come_back = [sem(f"come_back{n}") for n in range(4)]
        CHOICE = 5

        def route(engine, step):
            for i in range(-3, 1):
                step(i, i % 2)
            with engine.Fori(1, (TILES - 4) // 2 + 1) as b:
                step(2 * b - 1, 1)
                step(2 * b, 0)
            for i in range(TILES - 3, TILES + 1):
                step(i, i % 2)

        def is_tile(i):
            return not isinstance(i, int) or 0 <= i < TILES

        def over_rows(engine, tile):
            for k in range(4):
                tile(k, k, 0, k == 0, k == 3)
            bodies = (ROW_TILES - 4) // 8
            with engine.Fori(0, bodies) as b:
                for n in range(8):
                    tile(8 * b + 4 + n, n % 4, 2 * b + 1 + n // 4, n == 0, n == 7)
            for k in range(4 + 8 * bodies, ROW_TILES):
                tile(k, k % 4, k // 4, k == 4 + 8 * bodies, k == ROW_TILES - 1)

        with nc.Block() as block:
            @block.sync
            def _(sp):
                sp.wait_ge(empty_set, 1)
                sp.dma_start(rows_in[0:SPARE_ROWS, :].rearrange("(t p) c -> p t c", p=P),
                             empty_rows[:, 0:SPARE_TILES, :]).then_inc(emptied, 16)
                sp.dma_start(rows_in[SPARE_ROWS:, :].rearrange("(e r) c -> r e c", e=EXPERTS)[0:P],
                             empty_rows[:, SPARE_TILES:, :]).then_inc(emptied, 16)
                sp.dma_start(w1[:, :], w1_in).then_inc(w_loaded, 16)
                sp.dma_start(w2[:, :], w2_in).then_inc(w_loaded, 16)
                sp.dma_start(b1[:, :], b1_in.broadcast_to([P, EXPERTS * D_FF])).then_inc(w_loaded, 16)
                sp.dma_start(b2[:, :], b2_in.broadcast_to([P, EXPERTS * P])).then_inc(w_loaded, 16)
                for tensor, source in early:
                    sp.dma_start(tensor[:, :], source).then_inc(early_loaded, 16)
                sp.wait_ge(early_loaded, 16 * len(early))
                sp.wait_ge(emptied, 32)
                sp.wait_ge(plan_ready, 1)
                sp.wait_ge(scattered, 16 * GROUPS)

                def load(k, n):
                    first = sp.value_load(start[0:1, bass.ds(k, 1)], min_val=0, max_val=ROWS - P)
                    sp.dma_start(xin[:, n, :], rows_in[bass.ds(first, P), :]).then_inc(row_loaded[n], 16)

                def tile(k, n, turn, first, last):
                    if not (isinstance(k, int) and k + 3 >= ROW_TILES):
                        need(sp, result_row_ready, k)
                        load(k + 3, (n + 3) % 4)

                for k in range(3):
                    load(k, k)
                over_rows(sp, tile)
                for n in range(4):
                    sp.wait_ge(row_stored[n], 16 * len(range(n, ROW_TILES, 4)))
                by_token = results[0:TOKENS, :].rearrange("(p g) c -> p g c", p=P)
                for n in range(4):
                    part = slice(n * GROUPS // 4, (n + 1) * GROUPS // 4)
                    sp.dma_start(back[:, part, :], by_token[:, part, :]).then_inc(come_back[n], 16)

            @block.tensor
            def _(pe):
                def step(i, h):
                    if is_tile(i - 1):
                        place = bank_h[1 - h][:, 0:SUB * EXPERTS]
                        flags = chosen[:, 1 - h, :, :].rearrange("p s e -> p (s e)")
                        pe.wait_ge(chosen_ready, i)
                        pe.wait_ge(total_ready, i)
                        pe.matmul(place, const("strict"), flags, start=True, stop=False)
                        for back_by in range(1, SUB):
                            pe.matmul(place[:, back_by * EXPERTS:], const("ones"), flags[:, 0:(SUB - back_by) * EXPERTS],
                                      start=False, stop=False)
                        pe.matmul(place.rearrange("p (s e) -> p s e", s=SUB), const("ones"),
                                  total[:, :].unsqueeze(1).broadcast_to([P, SUB, EXPERTS]), start=False, stop=True).then_inc(rank_out, 1)
                    if is_tile(i + 1):
                        other = 1 - h
                        pe.wait_ge(xt_ready, i + 2)
                        need(pe, choice, CHOICE * (i - 1) + 1)
                        for s in range(SUB):
                            mm = pe.matmul(bank_l[other][:, s * EXPERTS:(s + 1) * EXPERTS], xt[:, other, s * P:(s + 1) * P],
                                           const("wr"), start=True, stop=True)
                        mm.then_inc(logits_out, 1)
                    if is_tile(i + 2):
                        pe.wait_ge(xn_ready, i + 3)
                        for s in range(SUB):
                            mm = pe.transpose(bank_x[h][:, s * P:(s + 1) * P], xn[:, h, s, :], ident)
                        mm.then_inc(xt_out, 1)

                route(pe, step)
                pe.wait_ge(total_ready, TILES + 1)
                pe.matmul(bank_y[0][:, 0:EXPERTS], const("ones"), total[:, :], start=True, stop=True).then_inc(total_out, 1)

                def turn_rows(k, n, turn):
                    h = n % 2
                    pe.wait_ge(row_loaded[n], 16 * turn + 16)
                    need(pe, row_t_ready, k - 1)
                    pe.transpose(bank_x[h][:, 0:P], xin[:, n, 0:P], ident).then_inc(row_t_out, 1)

                def expand(k, h, e):
                    pe.wait_ge(row_t_ready, k + 1)
                    need(pe, h_ready, k - 1)
                    pe.matmul(bank_h[h][:, :], xin_t[:, h, :], w1[:, bass.ds(e * D_FF, D_FF)],
                              start=True, stop=True).then_inc(h_out, 1)

                def turn_hidden(k, h):
                    pe.wait_ge(h_ready, k + 1)
                    need(pe, ht_ready, k - 1)
                    for f in range(FF_CHUNKS):
                        mm = pe.transpose(bank_l[h][:, f * P:(f + 1) * P], hidden[:, h, f * P:(f + 1) * P], ident)
                    mm.then_inc(ht_out, 1)

                def contract(k, h, e):
                    pe.wait_ge(ht_ready, k + 1)
                    need(pe, y_ready, k - 1)
                    for f in range(FF_CHUNKS):
                        mm = pe.matmul(bank_y[h][:, 0:P], hidden_t[:, h, f * P:(f + 1) * P],
                                       w2[:, bass.ds(e * D_FF + f * P, P)], start=(f == 0), stop=(f == FF_CHUNKS - 1))
                    mm.then_inc(y_out, 1)

                def expert_of(k):
                    return pe.value_load(expert[0:1, bass.ds(k, 1)], min_val=0, max_val=EXPERTS - 1)

                expert_now = []

                def tile(k, n, turn, first, last):
                    h = n % 2
                    if isinstance(k, int) and k == 0:
                        turn_rows(0, 0, 0)
                        expert_now[:] = expert_of(0), expert_of(1)
                        expand(0, 0, expert_now[0])
                        turn_rows(1, 1, 0)
                        return
                    turn_hidden(k - 1, 1 - h)
                    if first:
                        expert_now[:] = expert_of(k), expert_of(k - 1)
                        expert_now.reverse()
                    expand(k, h, expert_now[1])
                    if not last:
                        expert_now.append(expert_of(k + 1))
                    contract(k - 1, 1 - h, expert_now.pop(0))
                    if not (isinstance(k, int) and k == ROW_TILES - 1):
                        turn_rows(k + 1, (n + 1) % 4, turn if n < 3 else turn + 1)
                    else:
                        turn_hidden(k, h)
                        contract(k, h, expert_now[0])

                pe.wait_ge(plan_ready, 1)
                pe.wait_ge(w_loaded, 64)
                over_rows(pe, tile)

            @block.vector
            def _(dve):
                def step(i, h):
                    other = 1 - h
                    by_expert = [P, SUB, EXPERTS]

                    def chose(n):
                        dve.wait_ge(choice, CHOICE * i + n)
                    if is_tile(i):
                        dve.wait_ge(logits_out, i + 1)
                        dve.tensor_tensor(logits[:, :, :], bank_l[h][:, 0:SUB * EXPERTS].rearrange("p (s e) -> p s e", s=SUB),
                                          const("bias_r").unsqueeze(1).broadcast_to(by_expert), ALU.add).then_inc(choice, 1)
                    if is_tile(i + 2):
                        dve.wait_ge(std_ready, i + 3)
                        dve.reciprocal(rstd[:, :], std[:, :]).then_inc(rstd_ready, 1)
                    if is_tile(i):
                        chose(1)
                        dve.tensor_reduce(best[:, :], logits[:, :, :], AXIS.X, ALU.max).then_inc(choice, 1)
                    if is_tile(i + 2):
                        dve.wait_ge(rstd_ready, i + 3)
                        dve.scalar_tensor_tensor(shift[:, :], moments[:, h, :, 0], -1.0, rstd[:, :],
                                                 ALU.mult, ALU.mult).then_inc(shift_ready, 1)
                    if is_tile(i):
                        chose(2)
                        dve.tensor_tensor(is_best[:, :, :], logits[:, :, :],
                                          best[:, :].unsqueeze(2).broadcast_to(by_expert), ALU.is_equal).then_inc(choice, 1)
                    if is_tile(i + 3):
                        need(dve, moments_ready, i + 3)
                        for s in range(SUB):
                            st = dve.bn_stats(stats[:, s, :], x_tok[:, SUB * i + 3 * SUB + s, :])
                        st.then_inc(stats_ready, 1)
                    if is_tile(i):
                        chose(3)
                        dve.tensor_tensor(ranked[:, :, :], is_best[:, :, :],
                                          const("rank").unsqueeze(1).broadcast_to(by_expert), ALU.mult).then_inc(choice, 1)
                    if is_tile(i + 2):
                        dve.wait_ge(shift_ready, i + 3)
                        need(dve, xt_out, i + 1)
                        need(dve, rows_ready, i + 1)
                        dve.sem_inc(go, 1)
                        for s in range(SUB):
                            xs = dve.tensor_scalar(xn[:, h, s, :], x_tok[:, SUB * i + 2 * SUB + s, :], rstd[:, s:s + 1],
                                                   shift[:, s:s + 1], ALU.mult, ALU.add)
                        xs.then_inc(xn_ready, 1)
                    if is_tile(i):
                        chose(4)
                        dve.tensor_reduce(top_rank[:, :], ranked[:, :, :], AXIS.X, ALU.max).then_inc(choice, 1)
                    if is_tile(i - 1):
                        dve.wait_ge(rank_out, i)
                        dve.tensor_tensor(own_place[:, :, :], chosen[:, other, :, :],
                                          bank_h[other][:, 0:SUB * EXPERTS].rearrange("p (s e) -> p s e", s=SUB),
                                          ALU.mult).then_inc(own_ready, 1)
                        dve.wait_ge(here_ready, i)
                        dve.tensor_tensor(total[:, :], total[:, :], here[:, :], ALU.add).then_inc(total_ready, 1)
                    if is_tile(i):
                        chose(5)
                        dve.tensor_tensor(chosen[:, h, :, :], ranked[:, :, :], top_rank[:, :].unsqueeze(2).broadcast_to(by_expert),
                                          ALU.is_equal).then_inc(chosen_ready, 1)
                    if is_tile(i - 1):
                        dve.wait_ge(own_ready, i)
                        dve.tensor_reduce(position[:, :], own_place[:, :, :], AXIS.X, ALU.add).then_inc(position_ready, 1)
                    if is_tile(i + 3):
                        dve.wait_ge(stats_ready, i + 4)
                        need(dve, shift_ready, i + 2)
                        dve.sem_inc(go, 1)
                        for s in range(SUB):
                            ag = dve.bn_aggr(moments[:, other, s, :], stats[:, s, :])
                        ag.then_inc(moments_ready, 1)
                    if is_tile(i - 1):
                        dve.wait_ge(position_ready, i)
                        dve.tensor_copy(index[:, bass.ds(SUB * i - SUB, SUB)], position[:, :]).then_inc(index_ready, 1)
                    if is_tile(i):
                        dve.wait_ge(chosen_ready, i + 1)
                        need(dve, total_ready, i + 1)
                        dve.tensor_reduce(here[:, :], chosen[:, h, :, :].rearrange("p s e -> p e s"), AXIS.X,
                                          ALU.add).then_inc(here_ready, 1)

                dve.memset(eps[:, :], LN_EPS).then_inc(eps_set, 1)
                dve.memset(ones[:, :], 1.0)
                dve.memset(top[:, EXPERTS:], float(P * ROW_TILES))
                dve.tensor_copy(total[:, :], const("region")).then_inc(total_ready, 1)
                route(dve, step)

                done = 0

                def put(instruction):
                    nonlocal done
                    done += 1
                    instruction.then_inc(planning, 1)

                def all_put():
                    dve.wait_ge(planning, done)

                grid = [P, ROW_TILES, EXPERTS]
                last_row = bank_y[0][:, 0:EXPERTS]
                dve.wait_ge(total_out, 1)
                put(dve.tensor_tensor(count[:, :], last_row, const("first_row"), ALU.subtract))
                all_put()
                put(dve.tensor_scalar(rounded[:, :], count[:, :], float(P - 1), None, ALU.add))
                all_put()
                put(dve.tensor_scalar(n_tiles_i[:, :], rounded[:, :], P.bit_length() - 1, None, ALU.arith_shift_right))
                all_put()
                put(dve.tensor_copy(n_tiles[:, :], n_tiles_i[:, :]))
                all_put()
                put(dve.tensor_tensor_scan(end_tile[:, :], ones[:, :], n_tiles[:, :], 0.0, ALU.mult, ALU.add))
                all_put()
                put(dve.tensor_tensor(base[:, :], end_tile[:, :], n_tiles[:, :], ALU.subtract))
                put(dve.tensor_tensor(ended[:, :, :], end_tile[:, :].unsqueeze(1).broadcast_to(grid),
                                      const("tile_no").unsqueeze(2).broadcast_to(grid), ALU.is_le))
                all_put()
                put(dve.scalar_tensor_tensor(top[:, 0:EXPERTS], base[:, :], float(P), last_row, ALU.mult, ALU.add))
                put(dve.tensor_reduce(expert_f[:, :], ended[:, :, :], AXIS.X, ALU.add))
                all_put()
                put(dve.tensor_tensor(climb[:, :], top[:, 1:], top[:, 0:EXPERTS], ALU.subtract))
                put(dve.tensor_scalar(expert[:, :], expert_f[:, :], float(EXPERTS - 1), None, ALU.min))
                all_put()
                put(dve.tensor_tensor(climbed[:, :, :], ended[:, :, :], climb[:, :].unsqueeze(1).broadcast_to(grid), ALU.mult))
                all_put()
                put(dve.tensor_reduce(start_f[:, :], climbed[:, :, :], AXIS.X, ALU.add))
                all_put()
                dve.scalar_tensor_tensor(start[:, :], start_f[:, :], top[:, 0:1], const("tile_end"),
                                         ALU.add, ALU.subtract).then_inc(plan_ready, 1)

                def bias_hidden(k, n, turn, e):
                    h = n % 2
                    dve.wait_ge(h_out, k + 1)
                    need(dve, ht_out, k - 1)
                    dve.tensor_tensor(hidden[:, h, :], bank_h[h][:, :], b1[:, bass.ds(e * D_FF, D_FF)], ALU.add).then_inc(h_ready, 1)
                    need(dve, row_stored[n], 16 * turn)
                    dve.tensor_copy(result_row[:, n:n + 1], xin[:, n, P:]).then_inc(result_row_ready, 1)

                def bias_out(k, n, e):
                    dve.wait_ge(y_out, k + 1)
                    dve.tensor_tensor(y_row[:, n, :], bank_y[n % 2][:, 0:P], b2[:, bass.ds(e * P, P)], ALU.add).then_inc(y_ready, 1)

                def expert_of(k):
                    return dve.value_load(expert[0:1, bass.ds(k, 1)], min_val=0, max_val=EXPERTS - 1)

                def tile(k, n, turn, first, last):
                    bias_hidden(k, n, turn, expert_of(k))
                    if not (isinstance(k, int) and k == 0):
                        bias_out(k - 1, (n + 3) % 4, expert_of(k - 1))
                    if isinstance(k, int) and k == ROW_TILES - 1:
                        bias_out(k, n, expert_of(k))

                dve.wait_ge(plan_ready, 1)
                dve.wait_ge(w_loaded, 64)
                over_rows(dve, tile)
                for n in range(4):
                    dve.wait_ge(come_back[n], 16)
                    part = slice(n * GROUPS // 4, (n + 1) * GROUPS // 4)
                    dve.tensor_tensor(x_tok[:, part, :], x_tok[:, part, :], back[:, part, :], ALU.add)

            @block.scalar
            def _(act):
                def step(i, h):
                    other = 1 - h
                    if is_tile(i):
                        act.activation(rows[:, bass.ds(SUB * i, SUB), P:], const("token")[:, bass.ds(SUB * i, SUB)].unsqueeze(2), ACT.Copy)
                        act.activation(rows[:, bass.ds(SUB * i, SUB), 0:P], xn[:, h, :, :], ACT.Copy).then_inc(rows_ready, 1)
                    if is_tile(i + 2):
                        act.wait_ge(xt_out, i + 3)
                        need(act, logits_out, i + 1)
                        act.activation(xt[:, h, :], bank_x[h][:, :], ACT.Copy).then_inc(xt_ready, 1)
                    if is_tile(i + 3):
                        act.wait_ge(moments_ready, i + 4)
                        need(act, rstd_ready, i + 3)
                        act.activation(std[:, :], moments[:, other, :, 1], ACT.Sqrt, bias=eps[:, 0:1]).then_inc(std_ready, 1)

                act.wait_ge(eps_set, 1)
                route(act, step)

                def tile(k, n, turn, first, last):
                    h = n % 2
                    if isinstance(k, int) and k == 0:
                        act.wait_ge(row_t_out, 1)
                        act.activation(xin_t[:, 0, :], bank_x[0][:, 0:P], ACT.Copy).then_inc(row_t_ready, 1)
                    else:
                        act.wait_ge(ht_out, k)
                        need(act, y_out, k - 2)
                        act.activation(hidden_t[:, 1 - h, :], bank_l[1 - h][:, :], ACT.Relu).then_inc(ht_ready, 1)
                    if not (isinstance(k, int) and k == ROW_TILES - 1):
                        act.wait_ge(row_t_out, k + 2)
                        need(act, h_out, k)
                        act.activation(xin_t[:, 1 - h, :], bank_x[1 - h][:, 0:P], ACT.Copy).then_inc(row_t_ready, 1)
                    else:
                        act.wait_ge(ht_out, k + 1)
                        act.activation(hidden_t[:, h, :], bank_l[h][:, :], ACT.Relu).then_inc(ht_ready, 1)

                over_rows(act, tile)

            @block.gpsimd
            def _(pool):
                pool.memset(empty_rows[:, :, :], 0.0).then_inc(cleared, 1)
                pool.wait_ge(cleared, 1)
                pool.tensor_copy(empty_rows[:, :, P:], const("empty").unsqueeze(2)).then_inc(empty_set, 1)
                for i in range(TILES):
                    pool.wait_ge(index_ready, i + 1)
                    pool.wait_ge(rows_ready, i + 1)
                    for g in range(SUB * i, SUB * i + SUB):
                        pool.indirect_dma_start(rows_in, bass.IndirectOffsetOnAxis(ap=index[:, g:g + 1], axis=0),
                                                rows[:, g, :], None).then_inc(scattered, 16)

                def tile(k, n, turn, first, last):
                    pool.wait_ge(y_ready, k + 1)
                    pool.sem_inc(send, 1)
                    pool.indirect_dma_start(results, bass.IndirectOffsetOnAxis(ap=result_row[:, n:n + 1], axis=0),
                                            y_row[:, n, :], None).then_inc(row_stored[n], 16)

                over_rows(pool, tile)

QUATS, QC = P // 4, 4
NORM_EPS = 1e-12
C_W = [("wk", QC * P), ("wv", P), ("bk", QC * P), ("bv", P), ("wo", P), ("bo", P), ("gain", 1), ("shift", 1),
       ("eps_pos", PER_SEQ * SUB), ("upto", P), ("last", P)]
CW_AT, CW_WIDTH = offsets(C_W)
MINUS = [(1, 0), (1, 2), (2, 0), (2, 3), (3, 0), (3, 1)]


def shape_constants_c():
    c = np.zeros((P, CW_WIDTH), np.float32)
    part = {name: c[:, a:b] for name, (a, b) in CW_AT.items()}
    part["eps_pos"][:] = LN_EPS * (np.arange(PER_SEQ * SUB)[None] * P + np.arange(P)[:, None] + 1)
    part["upto"][:] = np.triu(np.ones((P, P)))
    part["last"][P - 1] = 1
    return c, part


def in_steps(engine, norm, ahead, main, tail):
    def body(i, h):
        for step in range(16):
            if not isinstance(i, int) or i > 0:
                tail(i - 1, 1 - h, step)
            main(i, h, step)
            if not isinstance(i, int) or i + 1 < TILES:
                ahead(i + 1, 1 - h, step)
            if not isinstance(i, int) or i + 2 < TILES:
                norm(i + 2, h, step)

    for step in range(16):
        norm(0, 0, step)
    for step in range(16):
        ahead(0, 0, step)
        norm(1, 1, step)
    body(0, 0)
    body(1, 1)
    with engine.Fori(1, TILES // 2 - 1) as b:
        body(2 * b, 0)
        body(2 * b + 1, 1)
    body(TILES - 2, 0)
    body(TILES - 1, 1)
    for step in range(16):
        tail(TILES - 1, 1, step)


def quaternion_memory(nc, x_tok, consts, weights, load_moe, moe_hi, moe_lo):
    with ExitStack() as ctx:
        def sb(name, shape, dt=F32):
            return ctx.enter_context(nc.sbuf_tensor("c_" + name, shape, dt))

        def bank(name):
            return ctx.enter_context(nc.psum_tensor("c_" + name, [P, TILE], F32))

        def sem(name):
            return nc.alloc_semaphore("c_" + name)

        def w(name):
            return weights[:, CW_AT[name][0]:CW_AT[name][1]]

        ident = consts[:, C_AT["ident"][0]:C_AT["ident"][1]]
        half = sb("minus_half", [P, SUB])
        eps = sb("eps", [P, SUB])
        stats = sb("stats", [P, SUB, 6])
        moments = sb("moments", [P, SUB, 2])
        var_eps = sb("var_eps", [P, SUB])
        rstd = sb("rstd", [P, SUB])
        shift = sb("shift", [P, SUB])
        xn = sb("xn", [P, SUB, P])
        xt = sb("xt", [P, TILE])
        key = sb("key", [P, 2, SUB, QC, P])
        value = sb("value", [P, SUB, P])
        square = sb("square", [P, SUB, P])
        norm2 = sb("norm2", [P, P])
        length = sb("length", [P, P])
        norm_max = sb("norm_max", [P, P])
        rnorm = sb("rnorm", [P, 2, P])
        value_n = sb("value_n", [P, SUB, P])
        bound = sb("bound", [P, SUB, QC, P])
        memory = sb("memory", [P, 2, SUB, P])
        memory_n = sb("memory_n", [P, SUB, P])
        read = sb("read", [P, SUB, QC, P])
        real = sb("real", [P, SUB, P])
        got = sb("got", [P, SUB, P])
        stats2 = sb("stats2", [P, SUB, 6])
        moments2 = sb("moments2", [P, SUB, 2])
        var_eps2 = sb("var_eps2", [P, SUB])
        rstd2 = sb("rstd2", [P, SUB])
        shift2 = sb("shift2", [P, SUB])
        normed = sb("normed", [P, SUB, P])
        normed_t = sb("normed_t", [P, TILE])
        kept0 = sb("kept0", [P, SUB, P])
        kept = sb("kept", [P, 2, SUB, P])

        bank_x, bank_v, bank_r, bank_o = bank("x"), bank("v"), bank("r"), bank("o")
        bank_k = [bank(f"k{n}") for n in range(2)]
        bank_m = [bank(f"m{n}") for n in range(2)]

        half_set, signed = sem("half_set"), sem("signed")
        go = sem("go")
        stats_ready, moments_ready, var_ready = sem("stats_ready"), sem("moments_ready"), sem("var_ready")
        rstd_ready, shift_ready, xn_ready = sem("rstd_ready"), sem("shift_ready"), sem("xn_ready")
        xt_out, xt_ready = sem("xt_out"), sem("xt_ready")
        k_out, v_out, key_ready, value_ready = sem("k_out"), sem("v_out"), sem("key_ready"), sem("value_ready")
        square_ready, norm2_ready, norm_ready, max_ready = sem("square_ready"), sem("norm2_ready"), sem("norm_ready"), sem("max_ready")
        rnorm_ready, valuen_ready = sem("rnorm_ready"), sem("valuen_ready")
        bound_dve, bound_pool = sem("bound_dve"), sem("bound_pool")
        memory_out, memory_ready, memoryn_ready = sem("memory_out"), sem("memory_ready"), sem("memoryn_ready")
        read_dve, read_pool = sem("read_dve"), sem("read_pool")
        read_out, real_ready, got_ready = sem("read_out"), sem("real_ready"), sem("got_ready")
        stats2_ready, moments2_ready, var2_ready = sem("stats2_ready"), sem("moments2_ready"), sem("var2_ready")
        rstd2_ready, shift2_ready, normed_ready = sem("rstd2_ready"), sem("shift2_ready"), sem("normed_ready")
        normedt_out, normedt_ready, wo_out, x_ready = sem("normedt_out"), sem("normedt_ready"), sem("wo_out"), sem("x_ready")
        kept0_ready, kept_ready = sem("kept0_ready"), sem("kept_ready")

        def by_quat(ap):
            return ap.rearrange("p s (q c) -> p (s q) c", c=QC)

        def per_quat(ap):
            return ap.unsqueeze(2).broadcast_to([P, P, QC])

        def spread_component(ap):
            return ap.rearrange("p (q m) -> p m q", m=QC).unsqueeze(3).broadcast_to([P, QC, QUATS, QC])

        def in_quats(ap):
            return ap.rearrange("p m (q c) -> p m q c", c=QC)

        with nc.Block() as block:
            @block.sync
            def _(sp):
                load_moe(sp)

            @block.tensor
            def _(pe):
                def norm(i, h, step):
                    if step == 12:
                        pe.wait_ge(xn_ready, i + 1)
                        need(pe, normedt_ready, i - 2)
                        for s in range(SUB):
                            mm = pe.transpose(bank_x[:, s * P:(s + 1) * P], xn[:, s, :], ident)
                        mm.then_inc(xt_out, 1)

                def ahead(i, h, step):
                    if step < SUB:
                        s = step
                        if s == 0:
                            pe.wait_ge(xt_ready, i + 1)
                            need(pe, value_ready, i)
                        need(pe, key_ready, SUB * i + s - 1)
                        tokens = xt[:, s * P:(s + 1) * P]
                        pe.matmul(bank_k[s % 2][:, :], tokens, w("wk"), start=True, stop=True).then_inc(k_out, 1)
                        mm = pe.matmul(bank_v[:, s * P:(s + 1) * P], tokens, w("wv"), start=True, stop=True)
                        if s == SUB - 1:
                            mm.then_inc(v_out, 1)

                def main(i, h, step):
                    if step in (1, 3, 5, 7):
                        s = step // 2
                        if s < 2:
                            pe.wait_ge(bound_dve, 2 * i + s + 1)
                        else:
                            pe.wait_ge(bound_pool, 2 * i + s - 1)
                        need(pe, memory_ready, SUB * i + s - 1)
                        carried = h or s
                        for m in range(QC):
                            mm = pe.matmul(bank_m[s % 2][:, 0:P], w("upto"), bound[:, s, m, :],
                                           start=(m == 0), stop=(m == QC - 1 and not carried))
                        if carried:
                            pe.wait_ge(memory_ready, SUB * i + s)
                            before = memory[:, h, s - 1, :] if s else memory[:, 1 - h, SUB - 1, :]
                            mm = pe.matmul(bank_m[s % 2][:, 0:P], w("last"), before, start=False, stop=True)
                        mm.then_inc(memory_out, 1)
                    if step >= 12:
                        s = step - 12
                        if s == 0:
                            need(pe, got_ready, i)
                        if s < 2:
                            pe.wait_ge(read_dve, 2 * i + s + 1)
                        else:
                            pe.wait_ge(read_pool, 2 * i + s - 1)
                        for m in range(QC):
                            mm = pe.matmul(bank_r[:, s * P:(s + 1) * P], ident, read[:, s, m, :],
                                           start=(m == 0), stop=(m == QC - 1))
                        if s == SUB - 1:
                            mm.then_inc(read_out, 1)

                def tail(i, h, step):
                    if step == 8:
                        pe.wait_ge(normed_ready, i + 1)
                        pe.wait_ge(xt_ready, min(i + 3, TILES) if isinstance(i, int) else i + 3)
                        for s in range(SUB):
                            mm = pe.transpose(bank_x[:, s * P:(s + 1) * P], normed[:, s, :], ident)
                        mm.then_inc(normedt_out, 1)
                    if step == 11:
                        pe.wait_ge(normedt_ready, i + 1)
                        need(pe, x_ready, i)
                        for s in range(SUB):
                            mm = pe.matmul(bank_o[:, s * P:(s + 1) * P], normed_t[:, s * P:(s + 1) * P], w("wo"),
                                           start=True, stop=True)
                        mm.then_inc(wo_out, 1)

                pe.wait_ge(signed, 2 * len(MINUS))
                in_steps(pe, norm, ahead, main, tail)

            @block.vector
            def _(dve):
                def norm(i, h, step):
                    if step == 4:
                        need(dve, var_ready, i)
                        for s in range(SUB):
                            st = dve.bn_stats(stats[:, s, :], x_tok[:, SUB * i + s, :])
                        st.then_inc(stats_ready, 1)
                    if step == 5:
                        dve.wait_ge(stats_ready, i + 1)
                        need(dve, shift_ready, i)
                        dve.sem_inc(go, 1)
                        for s in range(SUB):
                            ag = dve.bn_aggr(moments[:, s, :], stats[:, s, :])
                        ag.then_inc(moments_ready, 1)
                    if step == 8:
                        dve.wait_ge(rstd_ready, i + 1)
                        need(dve, xn_ready, i)
                        dve.scalar_tensor_tensor(shift[:, :], moments[:, :, 0], -1.0, rstd[:, :],
                                                 ALU.mult, ALU.mult).then_inc(shift_ready, 1)

                def ahead(i, h, step):
                    if step in (1, 2, 3, 4):
                        s = step - 1
                        dve.wait_ge(k_out, SUB * i + s + 1)
                        need(dve, real_ready, i - 1)
                        need(dve, read_pool, 2 * (i - 1))
                        dve.tensor_tensor(key[:, h, s, :, :].rearrange("p m c -> p (m c)"), bank_k[s % 2][:, :], w("bk"),
                                          ALU.add).then_inc(key_ready, 1)
                    if step == 5:
                        dve.wait_ge(v_out, i + 1)
                        need(dve, valuen_ready, i)
                        dve.tensor_tensor(value[:, :, :], bank_v[:, :].rearrange("p (s c) -> p s c", s=SUB),
                                          w("bv").unsqueeze(1).broadcast_to([P, SUB, P]), ALU.add).then_inc(value_ready, 1)
                    if step == 6:
                        dve.wait_ge(square_ready, i + 1)
                        need(dve, norm_ready, i)
                        dve.tensor_reduce(norm2[:, :], by_quat(square[:, :, :]), AXIS.X, ALU.add).then_inc(norm2_ready, 1)
                    if step == 8:
                        dve.wait_ge(norm_ready, i + 1)
                        dve.tensor_scalar(norm_max[:, :], length[:, :], NORM_EPS, None, ALU.max).then_inc(max_ready, 1)
                    if step == 10:
                        dve.wait_ge(max_ready, i + 1)
                        dve.reciprocal(rnorm[:, h, :], norm_max[:, :]).then_inc(rnorm_ready, 1)
                    if step == 11:
                        dve.wait_ge(value_ready, i + 1)
                        dve.wait_ge(rnorm_ready, i + 1)
                        need(dve, bound_dve, 2 * i)
                        need(dve, bound_pool, 2 * i)
                        dve.tensor_tensor(by_quat(value_n[:, :, :]), by_quat(value[:, :, :]), per_quat(rnorm[:, h, :]),
                                          ALU.mult).then_inc(valuen_ready, 1)

                def main(i, h, step):
                    if step == 0:
                        dve.wait_ge(valuen_ready, i + 1)
                        need(dve, memory_out, SUB * i)
                        for s in (0, 1):
                            dve.tensor_tensor(in_quats(bound[:, s, :, :]), in_quats(key[:, h, s, :, :]),
                                              spread_component(value_n[:, s, :]), ALU.mult).then_inc(bound_dve, 1)
                    if step == 9:
                        dve.wait_ge(memory_ready, SUB * (i + 1))
                        need(dve, real_ready, i)
                        need(dve, read_pool, 2 * i)
                        dve.tensor_tensor(by_quat(memory_n[:, :, :]), by_quat(memory[:, h, :, :]), per_quat(rnorm[:, h, :]),
                                          ALU.mult).then_inc(memoryn_ready, 1)
                    if step == 10:
                        dve.wait_ge(memoryn_ready, i + 1)
                        need(dve, read_out, i)
                        for s in (0, 1):
                            dve.tensor_tensor(in_quats(read[:, s, :, :]), in_quats(key[:, h, s, :, :]),
                                              spread_component(memory_n[:, s, :]), ALU.mult).then_inc(read_dve, 1)
                    if step == 12:
                        need(dve, got_ready, i)
                        k0 = key[:, h, :, 0, 0:P:QC]
                        dve.tensor_tensor(real[:, :, :].rearrange("p s (q c) -> p s q c", c=QC),
                                          memory_n[:, :, :].rearrange("p s (q c) -> p s q c", c=QC),
                                          k0.unsqueeze(3).broadcast_to([P, SUB, QUATS, QC]), ALU.mult).then_inc(real_ready, 1)

                def tail(i, h, step):
                    if isinstance(i, int) and i == TILES - 1 and step in (0, 3, 7, 10):
                        moe_lo(dve, {0: 3, 3: 0, 7: 1, 10: 2}[step])
                    if step == 0:
                        dve.wait_ge(real_ready, i + 1)
                        dve.wait_ge(read_out, i + 1)
                        need(dve, normed_ready, i)
                        dve.scalar_tensor_tensor(got[:, :, :].rearrange("p s c -> p (s c)"), real[:, :, :].rearrange("p s c -> p (s c)"),
                                                 2.0, bank_r[:, :], ALU.mult, ALU.subtract).then_inc(got_ready, 1)
                    if step == 1:
                        dve.wait_ge(got_ready, i + 1)
                        for s in range(SUB):
                            st = dve.bn_stats(stats2[:, s, :], got[:, s, :])
                        st.then_inc(stats2_ready, 1)
                    if step == 2:
                        dve.wait_ge(stats2_ready, i + 1)
                        dve.sem_inc(go, 1)
                        for s in range(SUB):
                            ag = dve.bn_aggr(moments2[:, s, :], stats2[:, s, :])
                        ag.then_inc(moments2_ready, 1)
                    if step == 4:
                        dve.wait_ge(rstd2_ready, i + 1)
                        dve.scalar_tensor_tensor(shift2[:, :], moments2[:, :, 0], -1.0, rstd2[:, :],
                                                 ALU.mult, ALU.mult).then_inc(shift2_ready, 1)
                    if step == 13:
                        dve.wait_ge(wo_out, i + 1)
                        dve.wait_ge(kept_ready, i + 1)
                        dve.tensor_tensor(x_tok[:, bass.ds(SUB * i, SUB), :], bank_o[:, :].rearrange("p (s c) -> p s c", s=SUB),
                                          kept[:, h, :, :], ALU.add).then_inc(x_ready, 1)

                dve.memset(eps[:, :], LN_EPS)
                dve.memset(half[:, :], -0.5).then_inc(half_set, 1)
                for name in ("wk", "bk"):
                    for m, c in MINUS:
                        place = w(name)[:, m * P + c:(m + 1) * P:QC]
                        dve.tensor_scalar(place, place, -1.0, None, ALU.mult).then_inc(signed, 1)
                dve.wait_ge(signed, 2 * len(MINUS))
                in_steps(dve, norm, ahead, main, tail)

            @block.scalar
            def _(act):
                def norm(i, h, step):
                    if step == 9:
                        act.wait_ge(shift_ready, i + 1)
                        need(act, xt_out, i)
                        need(act, kept0_ready, i)
                        for s in range(SUB):
                            a = act.activation(xn[:, s, :], x_tok[:, SUB * i + s, :], ACT.Identity,
                                               bias=shift[:, s:s + 1], scale=rstd[:, s:s + 1])
                        a.then_inc(xn_ready, 1)
                    if step == 12:
                        act.wait_ge(xt_out, i + 1)
                        need(act, v_out, i)
                        act.activation(xt[:, :], bank_x[:, :], ACT.Copy).then_inc(xt_ready, 1)

                def ahead(i, h, step):
                    if step == 6:
                        act.wait_ge(key_ready, SUB * (i + 1))
                        need(act, norm2_ready, i)
                        act.activation(square[:, :, :], key[:, h, :, 0, :], ACT.Square).then_inc(square_ready, 1)
                    if step == 7:
                        act.wait_ge(norm2_ready, i + 1)
                        need(act, max_ready, i)
                        act.activation(length[:, :], norm2[:, :], ACT.Sqrt).then_inc(norm_ready, 1)

                def main(i, h, step):
                    if step in (2, 4, 6, 8):
                        s = step // 2 - 1
                        act.wait_ge(memory_out, SUB * i + s + 1)
                        need(act, memoryn_ready, i - 1)
                        act.activation(memory[:, h, s, :], bank_m[s % 2][:, 0:P], ACT.Copy).then_inc(memory_ready, 1)
                    if isinstance(i, int) and i == TILES - 1 and step in (10, 11, 12, 13):
                        moe_hi(act, (3, 0, 1, 2)[step - 10])

                def tail(i, h, step):
                    if step in (6, 7):
                        if step == 6:
                            act.wait_ge(shift2_ready, i + 1)
                            need(act, normedt_out, i)
                        for s in (0, 1) if step == 6 else (2, 3):
                            a = act.activation(normed[:, s, :], got[:, s, :], ACT.Identity,
                                               bias=shift2[:, s:s + 1], scale=rstd2[:, s:s + 1])
                        if step == 7:
                            a.then_inc(normed_ready, 1)
                    if step == 9:
                        act.wait_ge(normedt_out, i + 1)
                        need(act, wo_out, i)
                        act.activation(normed_t[:, :], bank_x[:, :], ACT.Identity, bias=w("shift"), scale=w("gain")).then_inc(normedt_ready, 1)

                in_steps(act, norm, ahead, main, tail)

            @block.gpsimd
            def _(pool):
                def norm(i, h, step):
                    if step == 6:
                        pool.wait_ge(moments_ready, i + 1)
                        pool.tensor_tensor(var_eps[:, :], moments[:, :, 1], eps[:, :], ALU.add).then_inc(var_ready, 1)
                        pool.wait_ge(var_ready, i + 1)
                        need(pool, xn_ready, i)
                        pool.tensor_tensor(rstd[:, :], var_eps[:, :], half[:, :], ALU.pow).then_inc(rstd_ready, 1)

                def ahead(i, h, step):
                    if step == 4:
                        pool.wait_ge(xn_ready, i + 1)
                        need(pool, kept_ready, i)
                        pool.tensor_tensor(kept0[:, :, :], xn[:, :, :], w("bo").unsqueeze(1).broadcast_to([P, SUB, P]),
                                           ALU.add).then_inc(kept0_ready, 1)
                    if step == 12:
                        pool.wait_ge(kept0_ready, i + 1)
                        need(pool, x_ready, i - 1)
                        pool.tensor_tensor(kept[:, h, :, :], kept0[:, :, :], x_tok[:, bass.ds(SUB * i, SUB), :],
                                           ALU.add).then_inc(kept_ready, 1)

                def main(i, h, step):
                    if step == 0:
                        pool.wait_ge(valuen_ready, i + 1)
                        need(pool, memory_out, SUB * i)
                        for s in (2, 3):
                            pool.tensor_tensor(in_quats(bound[:, s, :, :]), in_quats(key[:, h, s, :, :]),
                                               spread_component(value_n[:, s, :]), ALU.mult).then_inc(bound_pool, 1)
                    if step == 10:
                        pool.wait_ge(memoryn_ready, i + 1)
                        need(pool, read_out, i)
                        for s in (2, 3):
                            pool.tensor_tensor(in_quats(read[:, s, :, :]), in_quats(key[:, h, s, :, :]),
                                               spread_component(memory_n[:, s, :]), ALU.mult).then_inc(read_pool, 1)

                def tail(i, h, step):
                    if step == 3:
                        pool.wait_ge(moments2_ready, i + 1)
                        pool.tensor_tensor(var_eps2[:, :], moments2[:, :, 1], w("eps_pos")[:, h * SUB:(h + 1) * SUB],
                                           ALU.add).then_inc(var2_ready, 1)
                        pool.wait_ge(var2_ready, i + 1)
                        need(pool, normed_ready, i)
                        pool.tensor_tensor(rstd2[:, :], var_eps2[:, :], half[:, :], ALU.pow).then_inc(rstd2_ready, 1)

                pool.wait_ge(half_set, 1)
                in_steps(pool, norm, ahead, main, tail)

E2, H2, TOP_K = 32, 64, 4
CAPACITY = 4 * (TOKENS * TOP_K) // E2
PAIRS = E2 // 2
UNITS = PAIRS + 1
D_W = [("wg", E2), ("spread", PAIRS * P), ("segment", SUB * E2), ("strict", P), ("ones", P)]
DW_AT, DW_WIDTH = offsets(D_W)


def shape_constants_d():
    c = np.zeros((P, DW_WIDTH), np.float32)
    part = {name: c[:, a:b] for name, (a, b) in DW_AT.items()}
    for e in range(E2):
        for half in (0, E2):
            part["spread"][half + e, e * H2:(e + 1) * H2] = 1
    part["segment"][:] = np.arange(SUB * E2) % E2 != 0
    part["strict"][:] = np.triu(np.ones((P, P)), 1)
    part["ones"][:] = 1
    return c, part


def moe_operands(nc, ctx):
    def sb(name, shape, dt=F32):
        return ctx.enter_context(nc.sbuf_tensor("d_" + name, shape, dt))

    return {
        "small": sb("small", [P, DW_WIDTH]),
        "raw": [sb(f"raw{n}", [P, UNITS * P]) for n in range(3)],
        "hi": [sb(f"hi{n}", [P, UNITS * P], F32R) for n in range(3)],
        "lo": [sb(f"lo{n}", [P, UNITS * P], F32R) for n in range(3)],
        "spread": sb("spread", [P, PAIRS * P], F32R),
        "wg_hi": sb("wg_hi", [P, E2], F32R),
        "wg_lo": sb("wg_lo", [P, E2], F32R),
        "strict": sb("strict", [P, P], BF16),
        "ones": sb("ones", [P, P], BF16),
    }


def split_operands(nc, moe, w_in, w1_in, w3_in, w2_in):
    loaded = [nc.alloc_semaphore(f"d_loaded{n}") for n in range(4)]
    hi_made = [nc.alloc_semaphore(f"d_hi_made{n}") for n in range(4)]

    def w(name):
        return moe["small"][:, DW_AT[name][0]:DW_AT[name][1]]

    def load(sp):
        sp.dma_start(moe["small"][:, :], w_in).then_inc(loaded[3], 16)
        for n, w_dram in enumerate((w1_in, w3_in, w2_in)):
            sp.dma_start(moe["raw"][n][:, :], w_dram).then_inc(loaded[n], 16)

    def make_hi(act, n):
        act.wait_ge(loaded[n], 16)
        if n == 3:
            act.activation(moe["wg_hi"][:, :], w("wg"), ACT.Copy).then_inc(hi_made[n], 1)
        else:
            act.activation(moe["hi"][n][:, :], moe["raw"][n][:, :], ACT.Copy).then_inc(hi_made[n], 1)

    def make_lo(dve, n):
        dve.wait_ge(hi_made[n], 1)
        if n == 3:
            dve.wait_ge(loaded[n], 16)
            dve.tensor_tensor(moe["wg_lo"][:, :], w("wg"), moe["wg_hi"][:, :].bitcast(F32), ALU.subtract)
            dve.tensor_copy(moe["strict"][:, :], w("strict"))
            dve.tensor_copy(moe["ones"][:, :], w("ones"))
            dve.tensor_copy(moe["spread"][:, :], w("spread"))
        else:
            dve.wait_ge(loaded[n], 16)
            dve.tensor_tensor(moe["lo"][n][:, :], moe["raw"][n][:, :], moe["hi"][n][:, :].bitcast(F32), ALU.subtract)

    return load, make_hi, make_lo


def top4_experts(nc, x_tok, consts, out_dram, moe):
    with ExitStack() as ctx:
        def sb(name, shape, dt=F32):
            return ctx.enter_context(nc.sbuf_tensor("d_" + name, shape, dt))

        def bank(name):
            return ctx.enter_context(nc.psum_tensor("d_" + name, [P, TILE], F32))

        def sem(name):
            return nc.alloc_semaphore("d_" + name)

        small, hi, lo, spread = moe["small"], moe["hi"], moe["lo"], moe["spread"]
        wg_hi, wg_lo, strict, ones = moe["wg_hi"], moe["wg_lo"], moe["strict"], moe["ones"]

        def w(name):
            return small[:, DW_AT[name][0]:DW_AT[name][1]]

        ident = consts[:, C_AT["ident"][0]:C_AT["ident"][1]]
        half = sb("minus_half", [P, SUB])
        eps = sb("eps", [P, SUB])

        stats = sb("stats", [P, SUB, 6])
        moments = sb("moments", [P, SUB, 2])
        var_eps = sb("var_eps", [P, SUB])
        rstd = sb("rstd", [P, SUB])
        shift = sb("shift", [P, SUB])
        xn = sb("xn", [P, SUB, P])
        x_hi = sb("x_hi", [P, 2, TILE], F32R)
        x_lo = sb("x_lo", [P, 2, TILE], F32R)

        table_call = sb("table_call", [P, 1])
        minus_max = sb("minus_max", [P, SUB])
        exps = sb("exps", [P, SUB, E2])
        total = sb("total", [P, SUB])
        inverse = sb("inverse", [P, SUB])
        scores = sb("scores", [P, SUB, E2])
        top = sb("top", [P, SUB, 8])
        above = sb("above", [P, SUB, E2])
        n_above = sb("n_above", [P, SUB])
        room = sb("room", [P, SUB])
        equal = sb("equal", [P, SUB, E2])
        nth_equal = sb("nth_equal", [P, SUB, E2])
        fits = sb("fits", [P, SUB, E2])
        taken = sb("taken", [P, SUB, E2])
        mask = sb("mask", [P, SUB, E2])
        mask_b = sb("mask_b", [P, SUB, E2], BF16)
        used = sb("used", [P, E2])
        rank = sb("rank", [P, SUB, E2])
        masked = sb("masked", [P, SUB, E2])
        weight = sb("weight", [P, SUB, E2])
        parts = sb("parts", [P, SUB, P])
        parts_t = sb("parts_t", [P, 2, TILE], F32R)

        silu = sb("silu", [P, 2, TILE])
        double_silu = sb("double_silu", [P, 2, TILE])
        product = sb("product", [P, 2, TILE])
        hidden = sb("hidden", [P, 2, TILE])
        hid_hi = sb("hid_hi", [P, 2, TILE], F32R)
        hid_lo = sb("hid_lo", [P, 2, TILE], F32R)
        y_sb = sb("y_sb", [P, TILE])
        out_sb = [sb(f"out{n}", [P, SUB, P]) for n in range(2)]

        bank_1 = [bank(f"h1_{n}") for n in range(2)]
        bank_3 = [bank(f"h3_{n}") for n in range(2)]
        bank_w = bank("w")
        bank_y = [bank(f"y{n}") for n in range(2)]
        bank_x = bank("x")

        set_up = sem("set_up")
        go = sem("go")
        stats_ready, moments_ready, var_ready = sem("stats_ready"), sem("moments_ready"), sem("var_ready")
        rstd_ready, shift_ready, xn_ready = sem("rstd_ready"), sem("shift_ready"), sem("xn_ready")
        xt_out, xhi_ready, xlo_ready = sem("xt_out"), sem("xhi_ready"), sem("xlo_ready")
        logits_out, exps_ready, routing, mask_ready = sem("logits_out"), sem("exps_ready"), sem("routing"), sem("mask_ready")
        rank_out, parts_ready, parts_out, partst_ready = sem("rank_out"), sem("parts_ready"), sem("parts_out"), sem("partst_ready")
        h1_out, h3_out, w_out = sem("h1_out"), sem("h3_out"), sem("w_out")
        silu_ready, product_ready, hidden_ready = sem("silu_ready"), sem("product_ready"), sem("hidden_ready")
        hi_ready, lo_ready, unit_out = sem("hi_ready"), sem("lo_ready"), sem("unit_out")
        y_ready, yt_out, out_ready, stored = sem("y_ready"), sem("yt_out"), sem("out_ready"), [sem(f"stored{n}") for n in range(2)]

        ranking = sem("ranking")
        ROUTING = 14
        BY_TANH = (7, 8)
        doubled = sem("doubled")

        def schedule(engine, norm, ahead, unit, end):
            def body(i, h):
                for u in range(UNITS):
                    unit(i, h, u)
                    if not isinstance(i, int) or i > 0:
                        end(i - 1, 1 - h, u)
                    if not isinstance(i, int) or i + 1 < TILES:
                        ahead(i + 1, 1 - h, u)
                    if not isinstance(i, int) or i + 2 < TILES:
                        norm(i + 2, h, u)

            for u in range(UNITS):
                norm(0, 0, u)
            for u in range(UNITS):
                ahead(0, 0, u)
                norm(1, 1, u)
            body(0, 0)
            body(1, 1)
            with engine.Fori(1, TILES // 2 - 1) as b:
                body(2 * b, 0)
                body(2 * b + 1, 1)
            body(TILES - 2, 0)
            body(TILES - 1, 1)
            for u in range(UNITS):
                end(TILES - 1, 1, u)

        with nc.Block() as block:
            @block.sync
            def _(sp):
                def norm(i, h, u):
                    pass

                ahead = unit = norm

                def end(i, h, u):
                    if u == 6:
                        sp.wait_ge(out_ready, i + 1)
                        sp.dma_start(out_dram[:, bass.ds(SUB * i, SUB), :], out_sb[h][:, :, :]).then_inc(stored[h], 16)

                schedule(sp, norm, ahead, unit, end)
                for n in range(2):
                    sp.wait_ge(stored[n], 16 * TILES // 2)

            @block.tensor
            def _(pe):
                def three(out, weights_hi, weights_lo, moving_hi, moving_lo, start=True, stop=True):
                    pe.matmul(out, weights_hi, moving_hi, start=start, stop=False)
                    pe.matmul(out, weights_hi, moving_lo, start=False, stop=False)
                    return pe.matmul(out, weights_lo, moving_hi, start=False, stop=stop)

                def norm(i, h, u):
                    pass

                def ahead(i, h, u):
                    if u == 1:
                        pe.wait_ge(xn_ready, i + 1)
                        need(pe, partst_ready, i)
                        for s in range(SUB):
                            mm = pe.transpose(bank_x[:, s * P:(s + 1) * P], xn[:, s, :], ident)
                        mm.then_inc(xt_out, 1)
                    if u == 6:
                        pe.wait_ge(xlo_ready, i + 1)
                        pe.wait_ge(xhi_ready, i + 1)
                        need(pe, out_ready, i - 1)
                        for s in range(SUB):
                            tokens = slice(s * P, (s + 1) * P)
                            mm = three(bank_x[:, s * E2:(s + 1) * E2], x_hi[:, h, tokens], x_lo[:, h, tokens],
                                       wg_hi[:, :], wg_lo[:, :])
                        mm.then_inc(logits_out, 1)
                    if u == 13:
                        pe.wait_ge(mask_ready, i + 1)
                        for s in range(SUB):
                            for t in range(s):
                                pe.matmul(bank_x[:, s * E2:(s + 1) * E2], ones[:, :], mask_b[:, t, :], start=(t == 0), stop=False)
                            pe.matmul(bank_x[:, s * E2:(s + 1) * E2], strict[:, :], mask_b[:, s, :], start=(s == 0), stop=True)
                        for t in range(SUB):
                            mm = pe.matmul(bank_x[:, SUB * E2:(SUB + 1) * E2], ones[:, :], mask_b[:, t, :],
                                           start=(t == 0), stop=(t == SUB - 1))
                        mm.then_inc(rank_out, 1)
                    if u == 16:
                        pe.wait_ge(parts_ready, i + 1)
                        for s in range(SUB):
                            mm = pe.transpose(bank_x[:, s * P:(s + 1) * P], parts[:, s, :], ident)
                        mm.then_inc(parts_out, 1)

                def second(i, h, u):
                    n, r = UNITS * i + u, (h + u) % 2
                    pe.wait_ge(hi_ready, n + 1)
                    pe.wait_ge(lo_ready, n + 1)
                    if u == 0:
                        need(pe, y_ready, i - 1)
                    cols = slice(u * P, (u + 1) * P)
                    three(bank_y[h][:, :], hi[2][:, cols], lo[2][:, cols], hid_hi[:, r, :], hid_lo[:, r, :],
                          start=(u == 0), stop=(u == UNITS - 1)).then_inc(unit_out, 1)

                def unit(i, h, u):
                    n, r = UNITS * i + u, (h + u) % 2
                    if u == 1:
                        pe.wait_ge(xlo_ready, i + 1)
                        pe.wait_ge(xhi_ready, i + 1)
                    cols = slice(u * P, (u + 1) * P)
                    need(pe, product_ready if u - 2 in BY_TANH else silu_ready, n - 1)
                    three(bank_1[r][:, :], hi[0][:, cols], lo[0][:, cols], x_hi[:, h, :], x_lo[:, h, :]).then_inc(h1_out, 1)
                    need(pe, product_ready, n - 1)
                    three(bank_3[r][:, :], hi[1][:, cols], lo[1][:, cols], x_hi[:, h, :], x_lo[:, h, :]).then_inc(h3_out, 1)
                    if u >= 2:
                        second(i, h, u - 2)
                    elif not (isinstance(i, int) and i == 0):
                        second(i - 1, 1 - h, UNITS - 2 + u)
                    if u < PAIRS:
                        if u == 0:
                            pe.wait_ge(partst_ready, i + 1)
                        need(pe, hidden_ready, n - 1 if u == 0 else n)
                        pe.matmul(bank_w[:, :], spread[:, cols], parts_t[:, h, :], start=True, stop=True).then_inc(w_out, 1)

                def end(i, h, u):
                    if isinstance(i, int) and i == TILES - 1 and u < 2:
                        second(i, h, UNITS - 2 + u)
                    if u == 4:
                        pe.wait_ge(y_ready, i + 1)
                        if isinstance(i, int) and i >= TILES - 2:
                            if i == TILES - 2:
                                pe.wait_ge(partst_ready, TILES)
                            else:
                                pe.wait_ge(out_ready, TILES - 1)
                        else:
                            pe.wait_ge(xlo_ready, i + 3)
                        for s in range(SUB):
                            mm = pe.transpose(bank_x[:, s * P:(s + 1) * P], y_sb[:, s * P:(s + 1) * P], ident)
                        mm.then_inc(yt_out, 1)

                schedule(pe, norm, ahead, unit, end)

            @block.vector
            def _(dve):
                def norm(i, h, u):
                    if u == 2:
                        need(dve, var_ready, i)
                        for s in range(SUB):
                            st = dve.bn_stats(stats[:, s, :], x_tok[:, SUB * i + s, :])
                        st.then_inc(stats_ready, 1)
                    if u == 3:
                        dve.wait_ge(stats_ready, i + 1)
                        need(dve, shift_ready, i)
                        dve.sem_inc(go, 1)
                        for s in range(SUB):
                            ag = dve.bn_aggr(moments[:, s, :], stats[:, s, :])
                        ag.then_inc(moments_ready, 1)
                    if u == 6:
                        dve.wait_ge(rstd_ready, i + 1)
                        need(dve, xn_ready, i)
                        dve.scalar_tensor_tensor(shift[:, :], moments[:, :, 0], -1.0, rstd[:, :],
                                                 ALU.mult, ALU.mult).then_inc(shift_ready, 1)

                def ahead(i, h, u):
                    def put(instruction):
                        instruction.then_inc(routing, 1)

                    def after(n):
                        dve.wait_ge(routing, ROUTING * i + n)

                    def each(ap):
                        return ap.unsqueeze(2).broadcast_to([P, SUB, E2])

                    if u == 2:
                        dve.wait_ge(xhi_ready, i + 1)
                        need(dve, h3_out, UNITS * (i - 1))
                        dve.tensor_tensor(x_lo[:, h, :], bank_x[:, :], x_hi[:, h, :].bitcast(F32), ALU.subtract).then_inc(xlo_ready, 1)
                    if u == 6:
                        dve.wait_ge(logits_out, i + 1)
                        need(dve, exps_ready, i)
                        dve.tensor_reduce(minus_max[:, :], bank_x[:, 0:SUB * E2].rearrange("p (s e) -> p s e", s=SUB),
                                          AXIS.X, ALU.max, negate=True).then_inc(routing, 1)
                    if u == 8:
                        dve.wait_ge(exps_ready, i + 1)
                        put(dve.tensor_reduce(total[:, :], exps[:, :, :], AXIS.X, ALU.add))
                        after(2)
                        put(dve.reciprocal(inverse[:, :], total[:, :]))
                    if u == 9:
                        after(3)
                        put(dve.tensor_tensor(scores[:, :, :], exps[:, :, :], each(inverse[:, :]), ALU.mult))
                        after(4)
                        dve.sem_inc(go, 1)
                        for s in range(SUB):
                            mx = dve.max(top[:, s, :], scores[:, s, :])
                        put(mx)
                    if u == 10:
                        fourth = each(top[:, :, TOP_K - 1])
                        after(5)
                        put(dve.tensor_tensor(above[:, :, :], scores[:, :, :], fourth, ALU.is_gt))
                        put(dve.tensor_tensor(equal[:, :, :], scores[:, :, :], fourth, ALU.is_equal))
                        after(7)
                        put(dve.tensor_reduce(n_above[:, :], above[:, :, :], AXIS.X, ALU.add))
                        put(dve.tensor_tensor_scan(nth_equal[:, :, :].rearrange("p s e -> p (s e)"), w("segment"),
                                                   equal[:, :, :].rearrange("p s e -> p (s e)"), 0.0, ALU.mult, ALU.add))
                        after(9)
                        put(dve.tensor_scalar(room[:, :], n_above[:, :], -1.0, float(TOP_K), ALU.mult, ALU.add))
                    if u == 12:
                        after(10)
                        put(dve.tensor_tensor(fits[:, :, :], nth_equal[:, :, :], each(room[:, :]), ALU.is_le))
                        after(11)
                        put(dve.tensor_tensor(taken[:, :, :], fits[:, :, :], equal[:, :, :], ALU.mult))
                        after(12)
                        put(dve.tensor_tensor(mask[:, :, :], taken[:, :, :], above[:, :, :], ALU.add))
                        after(13)
                        need(dve, rank_out, i)
                        dve.tensor_copy(mask_b[:, :, :], mask[:, :, :]).then_inc(mask_ready, 1)
                        put(dve.tensor_tensor(masked[:, :, :], mask[:, :, :], scores[:, :, :], ALU.mult))
                    if u == 14:
                        dve.wait_ge(rank_out, i + 1)
                        dve.tensor_tensor(rank[:, :, :], bank_x[:, 0:SUB * E2].rearrange("p (s e) -> p s e", s=SUB),
                                          used[:, :].unsqueeze(1).broadcast_to([P, SUB, E2]), ALU.add).then_inc(ranking, 1)
                        dve.wait_ge(ranking, 4 * i + 1)
                        after(14)
                        dve.tensor_tensor(used[:, :], used[:, :], bank_x[:, SUB * E2:(SUB + 1) * E2], ALU.add).then_inc(ranking, 1)
                        dve.scalar_tensor_tensor(weight[:, :, :], rank[:, :, :], float(CAPACITY), masked[:, :, :],
                                                 ALU.is_lt, ALU.mult).then_inc(ranking, 1)
                    if u == 15:
                        dve.wait_ge(ranking, 4 * i + 3)
                        need(dve, parts_out, i)
                        dve.tensor_copy(parts[:, :, 0:E2].bitcast(F32R), weight[:, :, :]).then_inc(ranking, 1)
                        dve.wait_ge(ranking, 4 * i + 4)
                        dve.tensor_tensor(parts[:, :, E2:2 * E2], weight[:, :, :], parts[:, :, 0:E2],
                                          ALU.subtract).then_inc(parts_ready, 1)

                def unit(i, h, u):
                    n, r = UNITS * i + u, (h + u) % 2
                    dve.wait_ge(silu_ready, n + 1)
                    dve.wait_ge(h3_out, n + 1)
                    if u < PAIRS:
                        need(dve, hidden_ready, n - 1)
                        gate = silu
                        if u in BY_TANH:
                            gate = double_silu
                            dve.scalar_tensor_tensor(double_silu[:, r, :], silu[:, r, :], 1.0, bank_1[r][:, :],
                                                     ALU.add, ALU.mult).then_inc(doubled, 1)
                            dve.wait_ge(doubled, len(BY_TANH) * i + BY_TANH.index(u) + 1)
                        dve.tensor_tensor(product[:, r, :], gate[:, r, :], bank_3[r][:, :], ALU.mult).then_inc(product_ready, 1)
                        dve.wait_ge(product_ready, n + 1)
                        dve.wait_ge(w_out, PAIRS * i + u + 1)
                        need(dve, hi_ready, n - 1)
                        need(dve, lo_ready, n - 1)
                        if u in BY_TANH:
                            dve.scalar_tensor_tensor(hidden[:, r, :], product[:, r, :], 0.5, bank_w[:, :],
                                                     ALU.mult, ALU.mult).then_inc(hidden_ready, 1)
                        else:
                            dve.tensor_tensor(hidden[:, r, :], product[:, r, :], bank_w[:, :], ALU.mult).then_inc(hidden_ready, 1)
                    else:
                        need(dve, hi_ready, n - 1)
                        need(dve, lo_ready, n - 1)
                        dve.tensor_tensor(hidden[:, r, :], silu[:, r, :], bank_3[r][:, :], ALU.mult).then_inc(product_ready, 1)
                        dve.wait_ge(product_ready, n + 1)
                        dve.sem_inc(hidden_ready, 1)

                def end(i, h, u):
                    if u == 5:
                        dve.wait_ge(yt_out, i + 1)
                        if not isinstance(i, int) or i >= 2:
                            dve.wait_ge(stored[h], 16 * (i // 2) if isinstance(i, int) else 8 * i - 8 * h)
                        dve.tensor_tensor(out_sb[h][:, :, :], x_tok[:, bass.ds(SUB * i, SUB), :],
                                          bank_x[:, :].rearrange("p (s c) -> p s c", s=SUB), ALU.add).then_inc(out_ready, 1)

                dve.memset(eps[:, :], LN_EPS)
                dve.memset(half[:, :], -0.5)
                dve.memset(used[:, :], 0.0)
                dve.memset(parts[:, :, :], 0.0).then_inc(set_up, 1)
                dve.wait_ge(set_up, 1)
                schedule(dve, norm, ahead, unit, end)

            @block.scalar
            def _(act):
                def norm(i, h, u):
                    if u in (12, 13):
                        if u == 12:
                            act.wait_ge(shift_ready, i + 1)
                            need(act, xt_out, i)
                        for s in (0, 1) if u == 12 else (2, 3):
                            a = act.activation(xn[:, s, :], x_tok[:, SUB * i + s, :], ACT.Identity,
                                               bias=shift[:, s:s + 1], scale=rstd[:, s:s + 1])
                        if u == 13:
                            a.then_inc(xn_ready, 1)

                def ahead(i, h, u):
                    if u == 1:
                        act.wait_ge(xt_out, i + 1)
                        need(act, h3_out, UNITS * (i - 1))
                        act.activation(x_hi[:, h, :], bank_x[:, :], ACT.Copy).then_inc(xhi_ready, 1)
                    if u == 6:
                        act.activation(table_call[:, :], eps[:, 0:1], ACT.Exp)
                    if u == 7:
                        act.wait_ge(routing, ROUTING * i + 1)
                        need(act, routing, ROUTING * (i - 1) + 4)
                        for s in range(SUB):
                            a = act.activation(exps[:, s, :], bank_x[:, s * E2:(s + 1) * E2], ACT.Exp, bias=minus_max[:, s:s + 1])
                        a.then_inc(exps_ready, 1)
                    if u == 16:
                        act.wait_ge(parts_out, i + 1)
                        need(act, w_out, PAIRS * (i - 1))
                        act.activation(parts_t[:, h, :], bank_x[:, :], ACT.Copy).then_inc(partst_ready, 1)

                def unit(i, h, u):
                    n, r = UNITS * i + u, (h + u) % 2
                    act.wait_ge(h1_out, n + 1)
                    need(act, product_ready, n - 1)
                    if u in BY_TANH:
                        act.activation(silu[:, r, :], bank_1[r][:, :], ACT.Tanh, scale=0.5).then_inc(silu_ready, 1)
                    else:
                        act.activation(silu[:, r, :], bank_1[r][:, :], ACT.Silu).then_inc(silu_ready, 1)
                    if u >= 1:
                        split(n - 1, 1 - r)
                    elif not (isinstance(i, int) and i == 0):
                        split(n - 1, 1 - r)

                def split(n, r):
                    act.wait_ge(hidden_ready, n + 1)
                    need(act, unit_out, n - 1)
                    act.activation(hid_hi[:, r, :], hidden[:, r, :], ACT.Copy).then_inc(hi_ready, 1)

                def end(i, h, u):
                    if isinstance(i, int) and i == TILES - 1 and u == 0:
                        split(UNITS * TILES - 1, (1 + UNITS - 1) % 2)
                    if u == 3:
                        act.wait_ge(unit_out, UNITS * (i + 1))
                        need(act, yt_out, i)
                        act.activation(y_sb[:, :], bank_y[h][:, :], ACT.Copy).then_inc(y_ready, 1)

                act.wait_ge(set_up, 1)
                schedule(act, norm, ahead, unit, end)

            @block.gpsimd
            def _(pool):
                def ahead(i, h, u):
                    pass

                def norm(i, h, u):
                    if u == 4:
                        pool.wait_ge(moments_ready, i + 1)
                        pool.tensor_tensor(var_eps[:, :], moments[:, :, 1], eps[:, :], ALU.add).then_inc(var_ready, 1)
                        pool.wait_ge(var_ready, i + 1)
                        need(pool, xn_ready, i)
                        pool.tensor_tensor(rstd[:, :], var_eps[:, :], half[:, :], ALU.pow).then_inc(rstd_ready, 1)

                def unit(i, h, u):
                    n, r = UNITS * i + u, (h + u) % 2
                    pool.wait_ge(hi_ready, n + 1)
                    need(pool, unit_out, n - 1)
                    pool.tensor_tensor(hid_lo[:, r, :], hidden[:, r, :], hid_hi[:, r, :].bitcast(F32), ALU.subtract).then_inc(lo_ready, 1)

                def end(i, h, u):
                    pass

                pool.wait_ge(set_up, 1)
                schedule(pool, norm, ahead, unit, end)


def build(nc, x_in, out, a_in, c_in, b_in, w1_in, w2_in, b1_in, b2_in, q_in, d_in, d1_in, d3_in, d2_in):
    by_group = "b (g p) c -> p (b g) c"
    with ExitStack() as ctx:
        x_tok = ctx.enter_context(nc.sbuf_tensor("x_tok", [P, GROUPS, P], F32))
        consts = ctx.enter_context(nc.sbuf_tensor("shape_consts", [P, C_WIDTH], F32))
        memory_weights = ctx.enter_context(nc.sbuf_tensor("memory_weights", [P, CW_WIDTH], F32))
        with ExitStack() as for_router:
            router = for_router.enter_context(nc.sbuf_tensor("router_consts", [P, B_WIDTH], F32))
            with nc.cleanup_on_exit():
                time_mixing(nc, x_tok, consts, x_in.rearrange(by_group, p=P), a_in, c_in, [(router, b_in)])
            with nc.cleanup_on_exit():
                top1_experts(nc, x_tok, consts, router, w1_in, w2_in, b1_in, b2_in, [(memory_weights, q_in)])
        moe = moe_operands(nc, ctx)
        with nc.cleanup_on_exit():
            quaternion_memory(nc, x_tok, consts, memory_weights, *split_operands(nc, moe, d_in, d1_in, d3_in, d2_in))
        with nc.cleanup_on_exit():
            top4_experts(nc, x_tok, consts, out.rearrange(by_group, p=P), moe)



def packed_time_mixing(t):
    w = np.zeros((P, A_WIDTH), np.float32)
    part = {name: w[:, a:b] for name, (a, b) in A_AT.items()}
    part["mix1"][:, 0:MIXES * E_MIX] = t["maa_w1"]
    for f in range(MIXES):
        first = E_MIX * f % P
        part["mix2"][first:first + E_MIX, f * P:(f + 1) * P] = t["maa_w2"][f]
    part["td1"][:, 0:P // 2] = t["td_w1"]
    part["td2"][0:P // 2] = t["td_w2"]
    part["wr"][:] = t["Wr"].T
    part["wk"][:] = t["Wk"].T
    part["wv"][:] = t["Wv"][Y_ORDER].T
    part["wg"][:] = t["Wg"][Y_ORDER].T
    part["wo"][:] = t["Wo"].T[Y_ORDER]
    for n, name in enumerate("xwkvrg"):
        part["maa"][:, n] = t["time_maa_" + name].reshape(P)
    part["decay"][:, 0] = t["time_decay"].reshape(P)
    part["u"][:, 0] = t["u"].reshape(P)
    part["gain"][:, 0] = t["ln_g"][Y_ORDER]
    part["shift"][:, 0] = t["ln_b"][Y_ORDER]
    return w


def packed_router(t):
    w, part = shape_constants_b()
    part["bias_r"][:] = t["br"][None]
    part["wr"][:] = t["Wr"].T
    return w


def packed_quaternions(t):
    w, part = shape_constants_c()
    for m in range(QC):
        other = [c ^ m for c in range(P)]
        part["wk"][:, m * P:(m + 1) * P] = t["Wk"].T[:, other]
        part["bk"][:, m * P:(m + 1) * P] = t["bk"][other][None]
    part["wv"][:] = t["Wv"].T
    part["bv"][:] = t["bv"][None]
    part["wo"][:] = t["Wo"].T
    part["bo"][:] = t["bo"][None]
    part["gain"][:, 0] = t["ln_g"]
    part["shift"][:, 0] = t["ln_b"]
    return w


def packed_gate(t):
    w, part = shape_constants_d()
    part["wg"][:] = t["Wg"]
    return w


def kernel(**inputs):
    import concourse.bacc as bacc
    from concourse.bass_utils import run_bass_kernel_spmd

    given = {name: np.asarray(a) for name, a in inputs.items()}

    def under(prefix):
        return {name[len(prefix):]: a for name, a in given.items() if name.startswith(prefix)}

    mixing, ffn, memory, moe = under("L0_attn_"), under("L0_ffn_"), under("L1_attn_"), under("L1_ffn_")
    arrays = {
        "in_x": mixing["x"],
        "in_mixing": packed_time_mixing(mixing),
        "in_consts": shape_constants(),
        "in_router": packed_router(ffn),
        "in_w1": ffn["W1"].transpose(2, 0, 1).reshape(P, EXPERTS * D_FF),
        "in_w2": ffn["W2"].reshape(EXPERTS, P, FF_CHUNKS, P).transpose(3, 0, 2, 1).reshape(P, EXPERTS * D_FF),
        "in_b1": ffn["b1"].reshape(1, EXPERTS * D_FF),
        "in_b2": ffn["b2"].reshape(1, EXPERTS * P),
        "in_memory": packed_quaternions(memory),
        "in_gate": packed_gate(moe),
        "in_moe1": np.concatenate([moe["W1"].transpose(1, 0, 2).reshape(P, PAIRS * P), moe["Ws1"]], axis=1),
        "in_moe3": np.concatenate([moe["W3"].transpose(1, 0, 2).reshape(P, PAIRS * P), moe["Ws3"]], axis=1),
        "in_moe2": np.concatenate([moe["W2"].reshape(PAIRS, P, P).transpose(1, 0, 2).reshape(P, PAIRS * P), moe["Ws2"]], axis=1),
    }
    arrays = {name: np.ascontiguousarray(a) for name, a in arrays.items()}
    nc = bacc.Bacc("TRN2", target_bir_lowering=False, num_devices=1)
    aps = [nc.dram_tensor(name, a.shape, mybir.dt.from_np(a.dtype), kind="ExternalInput").ap() for name, a in arrays.items()]
    out = nc.dram_tensor("out", [BATCH, SEQ, P], F32, kind="ExternalOutput").ap()
    build(nc, aps[0], out, *aps[1:])
    r = run_bass_kernel_spmd(nc, [arrays], core_ids=[0])
    return r.results[0]["out"]
```
